# Optimizing a Trainium2 kernel written in Bass

```python
import numpy as np
import jax
import jax.numpy as jnp

def _softmax(x, axis=-1):
    return jax.nn.softmax(x, axis=axis)

def _gelu(x):
    return jax.nn.gelu(x, approximate=True)

def _silu(x):
    return jax.nn.silu(x)

def _sigmoid(x):
    return jax.nn.sigmoid(x)

def _layernorm(x, axis=-1, eps=1e-05):
    m = jnp.mean(x, axis=axis, keepdims=True)
    v = jnp.var(x, axis=axis, keepdims=True)
    return (x - m) / jnp.sqrt(v + eps)

def _scatter_add(tgt, idx, src, axis=0):
    return tgt.at[idx].add(src)

def _segment_sum(src, seg, n):
    return jax.ops.segment_sum(src, seg, n)
kernel_name = 'mk_adj_resnorm_d4_adj_r2_e4a87e'

def setup_inputs(seed: int=0):
    np.random.seed(seed)
    _w = jnp.asarray

    def _rec_inputs():
        import jax
        import jax.numpy as jnp
        _gk = jax.random.key(seed)
        x = 7.22e-05 + 1 * jax.random.normal(jax.random.fold_in(_gk, 1), (64, 128, 128), jnp.float32)
        _w = (1.0 + jnp.arange(128, dtype=jnp.float32)) ** (-0.5)
        _w = _w / _w.mean()
        _pij = jnp.clip(0.015625 * _w[:, None] * _w[None, :], 0.0, 1.0)
        _a = jax.random.uniform(jax.random.fold_in(_gk, 2), (64, 128, 128)) < _pij
        _a = jnp.logical_or(_a, jnp.swapaxes(_a, -1, -2))
        _a = jnp.logical_or(_a, jnp.eye(128, dtype=bool))
        _af = _a.astype(jnp.float32)
        adj = _af
        _nm = jnp.ones((64, 128), dtype=bool)
        nodemask = jnp.where(_nm, 1.0, 0.0).astype(jnp.float32)
        return (x, adj, nodemask)
    x, adj, nodemask = _rec_inputs()

    def _L0_gnn_setup():
        import jax, jax.numpy as jnp
        import numpy as np
        from jax import lax
        DIM = 128
        EPS = 1e-05

        def _bn(h, g, b, m, v):
            scale = g / jnp.sqrt(v + EPS)
            return h * scale[None, :, None] + (b - m * scale)[None, :, None]

        def _conv1d(h, w, pad):
            return lax.conv_general_dilated(h, w, window_strides=(1,), padding=[(pad, pad)], dimension_numbers=('NCH', 'OIH', 'NCH'))
        key = jax.random.key(seed)
        ks = jax.random.split(key, 16)
        bs, n, d = (16, 1024, DIM)
        s = 0.05
        return {'x': jax.random.normal(ks[0], (bs, n, d), jnp.float32), 'mask': jnp.ones((bs, n, n), jnp.float32), 'w_se': jax.random.normal(ks[1], (3, d), jnp.float32) * s, 'b_se': jnp.zeros((3,), jnp.float32), 'conv1_w': jax.random.normal(ks[2], (d, d, 1), jnp.float32) * s, 'bn1_g': jnp.ones((d,), jnp.float32), 'bn1_b': jnp.zeros((d,), jnp.float32), 'bn1_m': jnp.zeros((d,), jnp.float32), 'bn1_v': jnp.ones((d,), jnp.float32), 'conv2_w': jax.random.normal(ks[3], (d, d, 17), jnp.float32) * s, 'bn2_g': jnp.ones((d,), jnp.float32), 'bn2_b': jnp.zeros((d,), jnp.float32), 'bn2_m': jnp.zeros((d,), jnp.float32), 'bn2_v': jnp.ones((d,), jnp.float32), 'w_msg': jax.random.normal(ks[4], (d, d), jnp.float32) * s, 'b_msg': jnp.zeros((d,), jnp.float32), 'w_ih': jax.random.normal(ks[5], (3 * d, 2 * d), jnp.float32) * s, 'b_ih': jnp.zeros((3 * d,), jnp.float32), 'w_hh': jax.random.normal(ks[6], (3 * d, d), jnp.float32) * s, 'b_hh': jnp.zeros((3 * d,), jnp.float32)}
    _L0_gnn_all = _L0_gnn_setup()
    _L0_gnn_in = {k: v for k, v in _L0_gnn_all.items() if k in ('w_se', 'b_se', 'conv1_w', 'bn1_g', 'bn1_b', 'bn1_m', 'bn1_v', 'conv2_w', 'bn2_g', 'bn2_b', 'bn2_m', 'bn2_v', 'w_msg', 'b_msg', 'w_ih', 'b_ih', 'w_hh', 'b_hh')}
    del _L0_gnn_all

    def _L1_gnn_setup():
        import jax, jax.numpy as jnp
        import numpy as np
        B, N, IN_DIM, OUT_DIM, H = (8, 512, 128, 128, 4)
        D = OUT_DIM // H
        NEG_INF = -9000000000000000.0
        LRELU_SLOPE = 0.2
        key = jax.random.key(seed)
        k1, k2, k3, k4 = jax.random.split(key, 4)
        x = jax.random.normal(k1, (B, N, IN_DIM), dtype=jnp.float32)
        adj = jax.random.randint(k2, (B, N, N), 0, 2).astype(jnp.float32)
        W = jax.random.normal(k3, (IN_DIM, H * D), dtype=jnp.float32) * jnp.sqrt(2.0 / (IN_DIM + H * D))
        a = jax.random.normal(k4, (H, 2 * D), dtype=jnp.float32) * jnp.sqrt(2.0 / (H + 2 * D))
        return {'x': x, 'adj': adj, 'W': W, 'a': a}
    _L1_gnn_all = _L1_gnn_setup()
    _L1_gnn_in = {k: v for k, v in _L1_gnn_all.items() if k in ('W', 'a')}
    del _L1_gnn_all

    def _L2_gnn_setup():
        import jax, jax.numpy as jnp
        import numpy as np
        B, N = (1, 2048)
        D_IN, D_OUT, H = (128, 128, 8)
        HD = D_OUT // H
        NEG = -9000000000000000.0

        def _xavier(key, shape):
            lim = np.sqrt(6.0 / (shape[0] + shape[1])).astype(np.float32)
            return jax.random.uniform(key, shape, jnp.float32, -lim, lim)
        key = jax.random.key(seed)
        ks = jax.random.split(key, 8)
        x = jax.random.normal(ks[0], (B, N, D_IN), jnp.float32)
        adj = (jax.random.uniform(ks[1], (B, N, N)) < 0.05).astype(jnp.float32)
        idx = jnp.arange(N)
        adj = adj.at[:, idx, idx].set(1.0)
        Wq = _xavier(ks[2], (D_IN, D_OUT))
        bq = jnp.zeros((D_OUT,), jnp.float32)
        Wk = _xavier(ks[3], (D_IN, D_OUT))
        bk = jnp.zeros((D_OUT,), jnp.float32)
        Wv = _xavier(ks[4], (D_IN, D_OUT))
        bv = jnp.zeros((D_OUT,), jnp.float32)
        Wo = _xavier(ks[5], (D_OUT, D_OUT))
        bo = jnp.zeros((D_OUT,), jnp.float32)
        return dict(x=x, adj=adj, Wq=Wq, bq=bq, Wk=Wk, bk=bk, Wv=Wv, bv=bv, Wo=Wo, bo=bo)
    _L2_gnn_all = _L2_gnn_setup()
    _L2_gnn_in = {k: v for k, v in _L2_gnn_all.items() if k in ('Wq', 'bq', 'Wk', 'bk', 'Wv', 'bv', 'Wo', 'bo')}
    del _L2_gnn_all

    def _L3_gnn_setup():
        import jax, jax.numpy as jnp
        import numpy as np
        B, N, IN_DIM, OUT_DIM = (8, 1024, 128, 128)
        EDGE_P = 0.02
        MASK_P = 0.9
        key = jax.random.key(seed)
        ks = jax.random.split(key, 8)
        x = jax.random.normal(ks[0], (B, N, IN_DIM), dtype=jnp.float32)
        adj = (jax.random.uniform(ks[1], (B, N, N)) < EDGE_P).astype(jnp.float32)
        mask = (jax.random.uniform(ks[2], (B, N)) < MASK_P).astype(jnp.float32)
        lim1 = 1.0 / np.sqrt(IN_DIM)
        W = jax.random.uniform(ks[3], (OUT_DIM, IN_DIM), minval=-lim1, maxval=lim1, dtype=jnp.float32)
        b = jax.random.uniform(ks[4], (OUT_DIM,), minval=-lim1, maxval=lim1, dtype=jnp.float32)
        lim2 = 1.0 / np.sqrt(2 * OUT_DIM)
        a1 = jax.random.uniform(ks[5], (OUT_DIM,), minval=-lim2, maxval=lim2, dtype=jnp.float32)
        a2 = jax.random.uniform(ks[6], (OUT_DIM,), minval=-lim2, maxval=lim2, dtype=jnp.float32)
        att_b = jax.random.uniform(ks[7], (), minval=-lim2, maxval=lim2, dtype=jnp.float32)
        return {'x': x, 'adj': adj, 'mask': mask, 'W': W, 'b': b, 'a1': a1, 'a2': a2, 'att_b': att_b}
    _L3_gnn_all = _L3_gnn_setup()
    _L3_gnn_in = {k: v for k, v in _L3_gnn_all.items() if k in ('W', 'b', 'a1', 'a2', 'att_b')}
    del _L3_gnn_all
    return {'x': x, 'adj': adj, 'nodemask': nodemask, 'L0_gnn_w_se': _L0_gnn_in['w_se'], 'L0_gnn_b_se': _L0_gnn_in['b_se'], 'L0_gnn_conv1_w': _L0_gnn_in['conv1_w'], 'L0_gnn_bn1_g': _L0_gnn_in['bn1_g'], 'L0_gnn_bn1_b': _L0_gnn_in['bn1_b'], 'L0_gnn_bn1_m': _L0_gnn_in['bn1_m'], 'L0_gnn_bn1_v': _L0_gnn_in['bn1_v'], 'L0_gnn_conv2_w': _L0_gnn_in['conv2_w'], 'L0_gnn_bn2_g': _L0_gnn_in['bn2_g'], 'L0_gnn_bn2_b': _L0_gnn_in['bn2_b'], 'L0_gnn_bn2_m': _L0_gnn_in['bn2_m'], 'L0_gnn_bn2_v': _L0_gnn_in['bn2_v'], 'L0_gnn_w_msg': _L0_gnn_in['w_msg'], 'L0_gnn_b_msg': _L0_gnn_in['b_msg'], 'L0_gnn_w_ih': _L0_gnn_in['w_ih'], 'L0_gnn_b_ih': _L0_gnn_in['b_ih'], 'L0_gnn_w_hh': _L0_gnn_in['w_hh'], 'L0_gnn_b_hh': _L0_gnn_in['b_hh'], 'L1_gnn_W': _L1_gnn_in['W'], 'L1_gnn_a': _L1_gnn_in['a'], 'L2_gnn_Wq': _L2_gnn_in['Wq'], 'L2_gnn_bq': _L2_gnn_in['bq'], 'L2_gnn_Wk': _L2_gnn_in['Wk'], 'L2_gnn_bk': _L2_gnn_in['bk'], 'L2_gnn_Wv': _L2_gnn_in['Wv'], 'L2_gnn_bv': _L2_gnn_in['bv'], 'L2_gnn_Wo': _L2_gnn_in['Wo'], 'L2_gnn_bo': _L2_gnn_in['bo'], 'L3_gnn_W': _L3_gnn_in['W'], 'L3_gnn_b': _L3_gnn_in['b'], 'L3_gnn_a1': _L3_gnn_in['a1'], 'L3_gnn_a2': _L3_gnn_in['a2'], 'L3_gnn_att_b': _L3_gnn_in['att_b']}

def reference(x, adj, nodemask, L0_gnn_w_se, L0_gnn_b_se, L0_gnn_conv1_w, L0_gnn_bn1_g, L0_gnn_bn1_b, L0_gnn_bn1_m, L0_gnn_bn1_v, L0_gnn_conv2_w, L0_gnn_bn2_g, L0_gnn_bn2_b, L0_gnn_bn2_m, L0_gnn_bn2_v, L0_gnn_w_msg, L0_gnn_b_msg, L0_gnn_w_ih, L0_gnn_b_ih, L0_gnn_w_hh, L0_gnn_b_hh, L1_gnn_W, L1_gnn_a, L2_gnn_Wq, L2_gnn_bq, L2_gnn_Wk, L2_gnn_bk, L2_gnn_Wv, L2_gnn_bv, L2_gnn_Wo, L2_gnn_bo, L3_gnn_W, L3_gnn_b, L3_gnn_a1, L3_gnn_a2, L3_gnn_att_b):
    import jax
    import jax.numpy as jnp

    def _L0_gnn_ref(x, mask, w_se, b_se, conv1_w, bn1_g, bn1_b, bn1_m, bn1_v, conv2_w, bn2_g, bn2_b, bn2_m, bn2_v, w_msg, b_msg, w_ih, b_ih, w_hh, b_hh):
        import jax, jax.numpy as jnp
        import numpy as np
        from jax import lax
        DIM = 128
        EPS = 1e-05

        def _bn(h, g, b, m, v):
            scale = g / jnp.sqrt(v + EPS)
            return h * scale[None, :, None] + (b - m * scale)[None, :, None]

        def _conv1d(h, w, pad):
            return lax.conv_general_dilated(h, w, window_strides=(1,), padding=[(pad, pad)], dimension_numbers=('NCH', 'OIH', 'NCH'))
        d = x.shape[-1]
        xc = jnp.transpose(x, (0, 2, 1))
        h = _bn(_conv1d(xc, conv1_w, 0), bn1_g, bn1_b, bn1_m, bn1_v)
        h = jax.nn.relu(h)
        h = _bn(_conv1d(h, conv2_w, 8), bn2_g, bn2_b, bn2_m, bn2_v)
        x_conv = jnp.transpose(jax.nn.relu(h + xc), (0, 2, 1))
        s = x @ w_se.T + b_se
        sq = jnp.sum(s * s, axis=-1)
        dist = sq[:, :, None] + sq[:, None, :] - 2.0 * jnp.einsum('bnd,bmd->bnm', s, s)
        A = jnp.exp(-dist) * mask
        msg = jax.nn.relu(x @ w_msg.T + b_msg)
        x_nmp = jnp.einsum('bnm,bmd->bnd', A, msg)
        x_in = jnp.concatenate([x_conv, x_nmp], axis=-1)
        gi = x_in @ w_ih.T + b_ih
        gh = x @ w_hh.T + b_hh
        gi_r, gi_z, gi_n = (gi[..., :d], gi[..., d:2 * d], gi[..., 2 * d:])
        gh_r, gh_z, gh_n = (gh[..., :d], gh[..., d:2 * d], gh[..., 2 * d:])
        r = jax.nn.sigmoid(gi_r + gh_r)
        z = jax.nn.sigmoid(gi_z + gh_z)
        nn_ = jnp.tanh(gi_n + r * gh_n)
        return (1.0 - z) * nn_ + z * x

    def _L1_gnn_ref(x, adj, W, a):
        import jax, jax.numpy as jnp
        import numpy as np
        B, N, IN_DIM, OUT_DIM, H = (8, 512, 128, 128, 4)
        D = OUT_DIM // H
        NEG_INF = -9000000000000000.0
        LRELU_SLOPE = 0.2
        h = jnp.einsum('bni,io->bno', x, W).reshape(x.shape[0], x.shape[1], H, D)
        h = h.transpose(0, 2, 1, 3)
        a1, a2 = (a[:, :D], a[:, D:])
        e_i = jnp.einsum('bhnd,hd->bhn', h, a1)
        e_j = jnp.einsum('bhmd,hd->bhm', h, a2)
        e = e_i[:, :, :, None] + e_j[:, :, None, :]
        e = jnp.where(e > 0, e, LRELU_SLOPE * e)
        e = jnp.where(adj[:, None, :, :] > 0, e, NEG_INF)
        attn = jax.nn.softmax(e, axis=-1)
        out = jnp.einsum('bhnm,bhmd->bhnd', attn, h)
        out = out.transpose(0, 2, 1, 3).reshape(x.shape[0], x.shape[1], H * D)
        return out

    def _L2_gnn_ref(x, adj, Wq, bq, Wk, bk, Wv, bv, Wo, bo):
        import jax, jax.numpy as jnp
        import numpy as np
        B, N = (1, 2048)
        D_IN, D_OUT, H = (128, 128, 8)
        HD = D_OUT // H
        NEG = -9000000000000000.0

        def _xavier(key, shape):
            lim = np.sqrt(6.0 / (shape[0] + shape[1])).astype(np.float32)
            return jax.random.uniform(key, shape, jnp.float32, -lim, lim)
        b, n, _ = x.shape

        def split_heads(t):
            return t.reshape(b, n, H, HD).transpose(0, 2, 1, 3)
        q = split_heads(x @ Wq + bq)
        k = split_heads(x @ Wk + bk)
        v = split_heads(x @ Wv + bv)
        scores = jnp.einsum('bhqd,bhkd->bhqk', q, k) / np.float32(np.sqrt(HD))
        scores = jnp.where(adj[:, None, :, :] > 0, scores, jnp.float32(NEG))
        attn = jax.nn.softmax(scores, axis=-1)
        out = jnp.einsum('bhqk,bhkd->bhqd', attn, v)
        out = out.transpose(0, 2, 1, 3).reshape(b, n, D_OUT)
        return out @ Wo + bo

    def _L3_gnn_ref(x, adj, mask, W, b, a1, a2, att_b):
        import jax, jax.numpy as jnp
        import numpy as np
        B, N, IN_DIM, OUT_DIM = (8, 1024, 128, 128)
        EDGE_P = 0.02
        MASK_P = 0.9
        h = jnp.einsum('bni,di->bnd', x, W) + b
        s1 = h @ a1
        s2 = h @ a2
        logits = s1[:, :, None] + s2[:, None, :] + att_b
        att = jax.nn.sigmoid(logits) * adj
        att = att * mask[:, :, None] * mask[:, None, :]
        att = att / (jnp.sum(att, axis=-1, keepdims=True) + 1e-08)
        h_new = jnp.einsum('bij,bjd->bid', att, h)
        return h_new * mask[:, :, None]
    x = _layernorm(x + _L0_gnn_ref(x, adj, L0_gnn_w_se, L0_gnn_b_se, L0_gnn_conv1_w, L0_gnn_bn1_g, L0_gnn_bn1_b, L0_gnn_bn1_m, L0_gnn_bn1_v, L0_gnn_conv2_w, L0_gnn_bn2_g, L0_gnn_bn2_b, L0_gnn_bn2_m, L0_gnn_bn2_v, L0_gnn_w_msg, L0_gnn_b_msg, L0_gnn_w_ih, L0_gnn_b_ih, L0_gnn_w_hh, L0_gnn_b_hh), axis=-1)
    x = _layernorm(x + _L1_gnn_ref(x, adj, L1_gnn_W, L1_gnn_a), axis=-1)
    x = _layernorm(x + _L2_gnn_ref(x, adj, L2_gnn_Wq, L2_gnn_bq, L2_gnn_Wk, L2_gnn_bk, L2_gnn_Wv, L2_gnn_bv, L2_gnn_Wo, L2_gnn_bo), axis=-1)
    x = _layernorm(x + _L3_gnn_ref(x, adj, nodemask, L3_gnn_W, L3_gnn_b, L3_gnn_a1, L3_gnn_a2, L3_gnn_att_b), axis=-1)
    return x

_drawn_inputs = setup_inputs


def setup_inputs(seed=0):
    import zlib

    import numpy as np

    out = dict(_drawn_inputs(seed))
    spreads = {'L0_gnn_b_se': (0.0, 2.0),
     'L0_gnn_bn1_g': (1.0, 0.6),
     'L0_gnn_bn1_b': (0.0, 0.402),
     'L0_gnn_bn1_m': (0.0, 0.337),
     'L0_gnn_bn1_v': (1.0, 0.6),
     'L0_gnn_bn2_g': (1.0, 0.2),
     'L0_gnn_bn2_b': (0.0, 0.481),
     'L0_gnn_bn2_m': (0.0, 0.447),
     'L0_gnn_bn2_v': (1.0, 0.6),
     'L0_gnn_b_msg': (0.0, 0.1),
     'L0_gnn_b_ih': (0.0, 0.1),
     'L0_gnn_b_hh': (0.0, 0.27),
     'L2_gnn_bq': (0.0, 0.289),
     'L2_gnn_bk': (0.0, 2.0),
     'L2_gnn_bv': (0.0, 0.1),
     'L2_gnn_bo': (0.0, 0.1)}
    factors = {'L3_gnn_a1': 28.401}
    for name, (base, spread) in spreads.items():
        noise = np.random.default_rng([zlib.crc32(name.encode()), seed]).standard_normal(out[name].shape)
        drawn = base * np.exp(spread * noise) if base else spread * noise
        out[name] = jnp.asarray(drawn.astype(out[name].dtype))
    for name, factor in factors.items():
        out[name] = (out[name] * factor).astype(out[name].dtype)
    return out
```

```python
from contextlib import ExitStack

import concourse.bass as bass
from concourse import mybir

F32 = mybir.dt.float32
BF16 = mybir.dt.bfloat16
ACT = mybir.ActivationFunctionType
ALU = mybir.AluOpType
AX = mybir.AxisListType

GRAPHS, N, D = 64, 128, 128
QUAD = 4
QUADS = GRAPHS // QUAD
TAPS = 17
PAD = TAPS // 2
H1 = 4
D1 = D // H1
H2 = 8
D2 = D // H2
EPS = 1e-5
TINY = 1e-8
BIG = 3.0e38
NEG = -9.0e15
SLOPE = 0.2
LAYERS = 4

INS = ["x", "adj", "nodemask", "L0_gnn_w_se", "L0_gnn_b_se", "L0_gnn_conv1_w", "L0_gnn_bn1_g", "L0_gnn_bn1_b",
       "L0_gnn_bn1_m", "L0_gnn_bn1_v", "L0_gnn_conv2_w", "L0_gnn_bn2_g", "L0_gnn_bn2_b", "L0_gnn_bn2_m",
       "L0_gnn_bn2_v", "L0_gnn_w_msg", "L0_gnn_b_msg", "L0_gnn_w_ih", "L0_gnn_b_ih", "L0_gnn_w_hh", "L0_gnn_b_hh",
       "L1_gnn_W", "L1_gnn_a", "L2_gnn_Wq", "L2_gnn_bq", "L2_gnn_Wk", "L2_gnn_bk", "L2_gnn_Wv", "L2_gnn_bv",
       "L2_gnn_Wo", "L2_gnn_bo", "L3_gnn_W", "L3_gnn_b", "L3_gnn_a1", "L3_gnn_a2", "L3_gnn_att_b"]


def nth(q, per, k):
    return q * per + k


def later(q):
    return not isinstance(q, int) or q > 0


def build(nc, ins, out):
    with ExitStack() as ctx:
        def sb(name, shape, dt=F32):
            return ctx.enter_context(nc.sbuf_tensor(name, shape, dt))

        def sem(name):
            return ctx.enter_context(nc.semaphore(name))

        bank = [ctx.enter_context(nc.psum_tensor(f"bank{c}", [128, QUAD, 128], F32)) for c in "ABCDFGHI"]
        bA, bB, bC, bD, bF, bG, bH, bI = bank

        ident = sb("ident", [128, 128])
        ident16 = sb("ident16", [128, 128], BF16)
        w2raw = sb("w2raw", [128, D, TAPS])
        wihraw = sb("wihraw", [128, 3, 2, 128])
        whhraw = sb("whhraw", [128, 3, 128])
        raw = sb("raw", [128, 3, 128])
        wseraw = sb("wseraw", [3, 128])
        maskraw = sb("maskraw", [GRAPHS, N])
        w2T = sb("w2T", [128, 20, 128])
        gateT = sb("gateT", [128, 9, 128])
        wseT = sb("wseT", [128, 35])
        nodeT = sb("nodeT", [128, GRAPHS])
        rows = sb("rows", [20, 128])
        col = sb("col", [128, 20])
        BN1G, BN1B, BN1M, BN1V, BN2G, BN2B, BN2M, BN2V, BIH, BHH, BQ, BK, BV, B3, A1, A2 = 0, 1, 2, 3, 4, 5, 6, 7, 8, 11, 14, 15, 16, 17, 18, 19
        VECTORS = 20
        bse = sb("bse", [35, 1])
        sc = sb("sc", [128, 16])
        SC1, SH1, SC2, SH2, HBR, HBZ, TMP = 0, 1, 2, 3, 4, 5, 6
        wa = sb("wa", [128, 2 * H1])
        w1 = sb("w1", [128, 128])
        abc = sb("abc", [128, H1, 2 * D1])
        aprod = sb("aprod", [128, 2 * H1, D1])
        wq = sb("wq", [128, 128])
        wk = sb("wk", [128, 128])
        wv = sb("wv", [128, 128])
        wo = sb("wo", [128, 128])
        bcast = sb("bcast", [128, 3, 128])
        cbc = sb("cbc", [128, 128])
        spread = sb("spread", [128, 2, 128])
        a12 = col[:, A1:A2 + 1]
        w3a = sb("w3a", [128, 2])
        attb = sb("attb", [128, 1])
        nc3 = sb("nc3", [128, 1])
        sel1 = sb("sel1", [3 * H1, H1, 128], BF16)
        ones3 = sb("ones3", [3, 128], BF16)
        ones = sb("ones", [128, 128])
        head = sb("head", [128, H2])
        half = sb("half", [128, QUAD])

        x0 = sb("x0", [128, QUAD, 128])
        adj0 = sb("adj0", [128, QUAD, 128])
        x0T = sb("x0T", [128, QUAD, 128])
        adj0T = sb("adj0T", [128, QUAD, 128])
        h1 = sb("h1", [128, QUAD, 128 + 2 * PAD])
        sa = sb("sa", [67, QUAD, 128])
        sbm = sb("sbm", [67, QUAD, 128])
        msgb = sb("msgb", [128, QUAD, 128])
        msg = sb("msg", [128, QUAD, 128])
        ea = sb("ea", [128, QUAD, 128])
        aT = sb("aT", [128, QUAD, 128])
        xnT = sb("xnT", [128, QUAD, 128])
        xcb = sb("xcb", [128, QUAD, 128])
        xcT = sb("xcT", [128, QUAD, 128])
        rT = sb("rT", [128, QUAD, 128])
        zT = sb("zT", [128, QUAD, 128])
        r1T = sb("r1T", [128, QUAD, 128])
        tT = sb("tT", [128, QUAD, 128])
        uT = sb("uT", [128, QUAD, 128])
        nT = sb("nT", [128, QUAD, 128])
        dT = sb("dT", [128, QUAD, 128])
        sT = sb("sT", [128, QUAD, 128])
        eT = sb("eT", [128, QUAD, 128])
        yT = sb("yT", [128, QUAD, 128])
        stats = [sb(f"stats{i}", [128, QUAD, 6]) for i in range(LAYERS)]
        mom = [sb(f"mom{i}", [128, 3, QUAD]) for i in range(LAYERS)]
        mv = [sb(f"mv{i}", [128, 3, QUAD]) for i in range(LAYERS)]
        ve = [sb(f"ve{i}", [128, QUAD]) for i in range(LAYERS)]
        rstd = [sb(f"rstd{i}", [128, QUAD]) for i in range(LAYERS)]
        x1 = sb("x1", [128, QUAD, 128])
        adj1 = sb("adj1", [128, QUAD, 128])
        x1T = sb("x1T", [128, QUAD, 128])
        mb1 = sb("mb1", [128, QUAD, 128], BF16)
        e1 = sb("e1", [128, QUAD, 2 * H1])
        ej3 = sb("ej3", [128, QUAD, H1, 3], BF16)
        ejr = sb("ejr", [128, QUAD, H1])
        ejT = sb("ejT", [3 * H1, QUAD, 128], BF16)
        h1x = sb("h1x", [128, QUAD, H1, D1 + 1])
        zi = sb("zi", [128, H1, 128])
        zl = sb("zl", [128, H1, 128])
        nm1 = sb("nm1", [128, H1])
        p1 = sb("p1", [128, H1, 128])
        p1T = sb("p1T", [128, H1, 128])
        rc1 = sb("rc1", [128, H1])
        o1 = sb("o1", [128, H1, D1])
        y1 = sb("y1", [128, QUAD, 128])
        x2 = sb("x2", [128, QUAD, 128])
        x2c = sb("x2c", [128, QUAD, 128])
        adj2 = sb("adj2", [128, QUAD, 128])
        x2T = sb("x2T", [128, QUAD, 128])
        mb2 = sb("mb2", [128, QUAD, 128], BF16)
        qT = sb("qT", [128, QUAD, 128])
        qh = sb("qh", [128, H2, QUAD, 128])
        kT = sb("kT", [128, QUAD, 128])
        v2x = sb("v2x", [128, QUAD, H2, D2 + 1])
        nm2 = sb("nm2", [128, 2, 4])
        p2 = sb("p2", [128, 2, 4, 128])
        p2T = sb("p2T", [128, 2, 4, 128])
        rc2 = sb("rc2", [128, H2])
        o2 = sb("o2", [128, H2, D2])
        o2T = sb("o2T", [128, QUAD, 128])
        y2 = sb("y2", [128, QUAD, 128])
        x3 = sb("x3", [128, QUAD, 128])
        adj3 = sb("adj3", [128, QUAD, 128])
        x3T = sb("x3T", [128, QUAD, 128])
        adj3T = sb("adj3T", [128, QUAD, 128])
        e3 = sb("e3", [128, QUAD, 2])
        s2n = sb("s2n", [128, QUAD])
        s13 = sb("s13", [128, QUAD, 3], BF16)
        s1r = sb("s1r", [128, QUAD])
        s1T = sb("s1T", [3, QUAD, 128], BF16)
        hb3 = sb("hb3", [128, QUAD, 128])
        h3x = sb("h3x", [128, QUAD, 129])
        mk = sb("mk", [128, QUAD])
        mk2 = sb("mk2", [128, QUAD])
        t3 = sb("t3", [128, QUAD, 128])
        d3 = sb("d3", [128, QUAD, 128])
        r3 = sb("r3", [128, QUAD, 128])
        att3 = sb("att3", [128, QUAD, 128])
        den3 = sb("den3", [128, 2, 4])
        y3 = sb("y3", [128, QUAD, 128])
        res = sb("res", [128, QUAD, 128])

        names = """w_in c_in col_in pool_c prep_ps prep_a prep_d late_in late_ps late_d
            x0_in adj0_in x0T_ps adj0T_ps x0T_r adj0T_r h1_ps h1_r s_ps sa_r sb_r msg_ps msgb_r msg_r dist_ps ea_r
            aT_r xn_ps xn_r c2_ps xcb_r xc_r ghn_ps r_ps r_r r1_r t_r z_ps z_r gin_ps u_r n_r d_r sT_r e_r y0_r
            y0T_ps adj1_in mb1_r x1_r x1T_ps x1T_r e1_ps e1_r ejs_r ej3_r ejT_ps ejT_r h1n_ps h1x_r z1_ps zi_r zl_r
            nm1_r p1_r p1T_ps p1T_r u1_ps rc1_r o1_r y1_r
            adj2_in mb2_r x2_r x2c_r x2T_ps x2T_r q_ps qT_r qh_r k_ps kT_r v_ps v_r s2_ps nm2_r p2_r p2T_ps p2Ta_r
            p2Td_r u2_ps rc2_r o2_r o2T_ps o2T_r wo_ps y2_r
            adj3_in x3_r x3T_ps x3T_r adj3T_ps adj3T_r mk_r mks_r e3_ps e3_r s1s_r s13_r s1T_ps s1T_r h3_ps hb3_r h3x_r
            z3_ps t3_r d3_r att3_r u3_ps f3_r y3_r res_r out_w""".split()
        S = {n: sem(n) for n in names}
        st_r = [sem(f"stats{i}_r") for i in range(LAYERS)]
        mv_r = [sem(f"mv{i}_r") for i in range(LAYERS)]
        ve_r = [sem(f"ve{i}_r") for i in range(LAYERS)]
        rstd_r = [sem(f"rstd{i}_r") for i in range(LAYERS)]

        POOL_C = 21
        LATE_D = 5
        graphs = range(QUAD)
        mm = nc.tensor.matmul

        def quad_of(name, q):
            return ins[name][bass.ds(q * QUAD, QUAD)].rearrange("g n d -> n g d")

        def plan(t):
            offs = (0, 1, 1, 2, 2, 3, 3)
            if not isinstance(t, int):
                return [t - o for o in offs]
            return [t - o if 0 <= t - o < QUADS else None for o in offs]

        LAST = QUADS + LAYERS - 2
        FIRST, END = LAYERS, QUADS

        def run(eng, step):
            for t in range(FIRST):
                step(t)
            with eng.Fori(FIRST, END) as t:
                step(t)
            for t in range(END, LAST + 1):
                step(t)

        block = ctx.enter_context(nc.Block())

        @block.sync
        def _(sp):
            sp.dma_start(w2raw[:, :, :], ins["L0_gnn_conv2_w"]).then_inc(S["w_in"], 16)
            sp.dma_start(raw[:, 0, :], ins["L0_gnn_conv1_w"].rearrange("o i k -> o (i k)")).then_inc(S["w_in"], 16)
            sp.dma_start(raw[:, 1, :], ins["L0_gnn_w_msg"]).then_inc(S["w_in"], 16)
            sp.dma_start(raw[:, 2, :], ins["L3_gnn_W"]).then_inc(S["w_in"], 16)
            sp.dma_start(wihraw[:, :, :, :], ins["L0_gnn_w_ih"].rearrange("(c o) (b i) -> o c b i", c=3, b=2)).then_inc(S["w_in"], 16)
            sp.dma_start(whhraw[:, :, :], ins["L0_gnn_w_hh"].rearrange("(c o) i -> o c i", c=3)).then_inc(S["w_in"], 16)
            sp.dma_start(wseraw[:, :], ins["L0_gnn_w_se"]).then_inc(S["w_in"], 16)
            sp.dma_start(maskraw[:, :], ins["nodemask"]).then_inc(S["w_in"], 16)
            for dst, name in ((w1, "L1_gnn_W"), (wq, "L2_gnn_Wq"), (wk, "L2_gnn_Wk"), (wv, "L2_gnn_Wv"), (wo, "L2_gnn_Wo")):
                sp.dma_start(dst[:, :], ins[name]).then_inc(S["late_in"], 16)
            sp.dma_start(abc[:, :, :], ins["L1_gnn_a"].partition_broadcast(128)).then_inc(S["late_in"], 16)
            for i, name in enumerate(("L0_gnn_b_msg", "L2_gnn_bo", "L3_gnn_b")):
                sp.dma_start(bcast[:, i, :], ins[name].partition_broadcast(128)).then_inc(S["late_in"], 16)

            def step(t):
                q0, _, q1, _, q2, _, q3 = plan(t)
                if q0 is not None:
                    if later(q0):
                        sp.wait_ge(S["x0T_ps"], nth(q0, 1, 0))
                        sp.wait_ge(S["adj0T_ps"], nth(q0, 1, 0))
                    sp.dma_start(x0[:, :, :], quad_of("x", q0)).then_inc(S["x0_in"], 16)
                    sp.dma_start(adj0[:, :, :], quad_of("adj", q0)).then_inc(S["adj0_in"], 16)
                if q1 is not None:
                    if later(q1):
                        sp.wait_ge(S["mb1_r"], nth(q1, 1, 0))
                    sp.dma_start(adj1[:, :, :], quad_of("adj", q1)).then_inc(S["adj1_in"], 16)
                if q2 is not None:
                    if later(q2):
                        sp.wait_ge(S["mb2_r"], nth(q2, 1, 0))
                    sp.dma_start(adj2[:, :, :], quad_of("adj", q2)).then_inc(S["adj2_in"], 16)
                if q3 is not None:
                    if later(q3):
                        sp.wait_ge(S["adj3T_ps"], nth(q3, 1, 0))
                    sp.dma_start(adj3[:, :, :], quad_of("adj", q3)).then_inc(S["adj3_in"], 16)
                if q3 is not None and later(q3):
                    store(q3 - 1)

            def store(q):
                sp.wait_ge(S["res_r"], nth(q, 1, 1))
                sp.dma_start(out[bass.ds(q * QUAD, QUAD)].rearrange("g n d -> n g d"), res[:, :, :]).then_inc(S["out_w"], 16)

            run(sp, step)
            store(QUADS - 1)
            sp.wait_ge(S["out_w"], 16 * QUADS)

        @block.gpsimd
        def _(gp):
            g_ = nc.gpsimd
            n_c = [0]

            def const(ins_):
                n_c[0] += 1
                ins_.then_inc(S["pool_c"], 1)

            const(g_.memset(ident[:, :], 0.0))
            const(g_.memset(sel1[:, :, :], 1.0))
            const(g_.memset(head[:, :], float(D2) ** -0.5))
            const(g_.memset(ones[:, :], 1.0))
            const(g_.memset(ones3[:, :], 1.0))
            const(g_.memset(half[:, :], -0.5))
            const(g_.memset(h1[:, :, :], 0.0))
            const(g_.memset(sa[:, :, :], 0.0))
            const(g_.memset(sbm[:, :, :], 0.0))
            const(g_.memset(h1x[:, :, :, D1:D1 + 1], 1.0))
            const(g_.memset(v2x[:, :, :, D2:D2 + 1], 1.0))
            const(g_.memset(wseT[:, :], 0.0))
            const(g_.memset(bse[:, :], 0.0))
            gp.wait_ge(S["pool_c"], n_c[0])
            const(g_.affine_select(out=ident[:, :], in_=ident[:, :], compare_op=ALU.not_equal, fill=1.0, base=0,
                                   pattern=[[-1, 128]], channel_multiplier=1))
            const(g_.affine_select(out=sel1[:, :, :], in_=sel1[:, :, :], compare_op=ALU.is_ge, fill=0.0, base=0,
                                   pattern=[[-3, H1], [0, 128]], channel_multiplier=1))
            const(g_.affine_select(out=head[:, :], in_=head[:, :], compare_op=ALU.is_ge, fill=0.0, base=0,
                                   pattern=[[-D2, H2]], channel_multiplier=1))
            for tile, value in ((sa[64:67, :, :], 1.0), (sbm[32:35, :, :], -1.0)):
                gp.wait_ge(S["pool_c"], n_c[0])
                const(g_.memset(tile, value))
            gp.wait_ge(S["pool_c"], n_c[0])
            const(g_.affine_select(out=sel1[:, :, :], in_=sel1[:, :, :], compare_op=ALU.is_ge, fill=0.0, base=2,
                                   pattern=[[3, H1], [0, 128]], channel_multiplier=-1))
            const(g_.affine_select(out=head[:, :], in_=head[:, :], compare_op=ALU.is_ge, fill=0.0, base=D2 - 1,
                                   pattern=[[D2, H2]], channel_multiplier=-1))
            const(g_.tensor_copy(ident16[:, :], ident[:, :]))
            assert n_c[0] == POOL_C
            for at, name, parts in ((BN1G, "L0_gnn_bn1_g", 1), (BN1B, "L0_gnn_bn1_b", 1), (BN1M, "L0_gnn_bn1_m", 1),
                                    (BN1V, "L0_gnn_bn1_v", 1), (BN2G, "L0_gnn_bn2_g", 1), (BN2B, "L0_gnn_bn2_b", 1),
                                    (BN2M, "L0_gnn_bn2_m", 1), (BN2V, "L0_gnn_bn2_v", 1), (BIH, "L0_gnn_b_ih", 3),
                                    (BHH, "L0_gnn_b_hh", 3), (BQ, "L2_gnn_bq", 1), (BK, "L2_gnn_bk", 1), (BV, "L2_gnn_bv", 1),
                                    (B3, "L3_gnn_b", 1), (A1, "L3_gnn_a1", 1), (A2, "L3_gnn_a2", 1)):
                gp.dma_start(rows[at:at + parts, :], ins[name].rearrange("(c p) -> c p", c=parts)).then_inc(S["col_in"], 16)
            gp.wait_ge(S["pool_c"], POOL_C)
            gp.dma_start(attb[:, :], ins["L3_gnn_att_b"].partition_broadcast(128)).then_inc(S["col_in"], 16)
            for at in (0, 32):
                gp.dma_start(bse[at:at + 3, :], ins["L0_gnn_b_se"].rearrange("(p c) -> p c", c=1)).then_inc(S["col_in"], 16)
            gp.wait_ge(S["late_d"], LATE_D)

            def root(i, q):
                gp.wait_ge(ve_r[i], nth(q, 1, 1))
                g_.tensor_tensor(rstd[i][:, :], ve[i][:, :], half[:, :], ALU.pow).then_inc(rstd_r[i], 1)

            def step(t):
                q0, c0, q1, c1, q2, c2, q3 = plan(t)
                if c1 is not None:
                    root(1, c1)
                if c2 is not None:
                    root(2, c2)
                if c0 is not None:
                    root(0, c0)
                if q2 is not None:
                    gp.wait_ge(S["x2_r"], nth(q2, 1, 1))
                    g_.tensor_tensor(x2c[:, :, :], x2[:, :, :], cbc[:, :].unsqueeze(1).to_broadcast([128, QUAD, 128]),
                                     ALU.add).then_inc(S["x2c_r"], 1)
                    gp.wait_ge(S["qT_r"], nth(q2, 1, 1))
                    for h in range(H2):
                        g_.tensor_tensor(qh[:, h, :, :], qT[:, :, :], head[:, h:h + 1].unsqueeze(2).to_broadcast([128, QUAD, 128]),
                                         ALU.mult).then_inc(S["qh_r"], 1)
                if q0 is not None:
                    gp.wait_ge(S["adj0T_r"], nth(q0, 1, 1))
                    gp.wait_ge(S["ea_r"], nth(q0, 1, 1))
                    g_.tensor_tensor(aT[:, :, :], ea[:, :, :], adj0T[:, :, :], ALU.mult).then_inc(S["aT_r"], 1)
                if q3 is not None:
                    gp.wait_ge(S["hb3_r"], nth(q3, 1, 1))
                    gp.wait_ge(S["mk_r"], nth(q3, 1, 1))
                    g_.tensor_tensor(h3x[:, :, 0:128], hb3[:, :, :], mk[:, :].unsqueeze(2).to_broadcast([128, QUAD, 128]),
                                     ALU.mult).then_inc(S["h3x_r"], 1)
                    g_.tensor_copy(h3x[:, :, 128:129], mk[:, :].unsqueeze(2)).then_inc(S["h3x_r"], 1)
                    root(3, q3)

            run(gp, step)

        @block.tensor
        def _(pe):
            def transpose(o, i, size=128):
                return nc.tensor.transpose(o, i, ident[0:size, 0:size])

            pe.wait_ge(S["pool_c"], POOL_C)
            pe.wait_ge(S["w_in"], 16 * 8)
            for b in range(4):
                for k in range(4):
                    last = transpose(bank[b][:, k, :], w2raw[:, :, 4 * b + k])
                last.then_inc(S["prep_ps"], 1)
            transpose(bF[:, 0, :], w2raw[:, :, 16])
            for k in range(3):
                last = transpose(bF[:, k + 1, :], raw[:, k, :])
            last.then_inc(S["prep_ps"], 1)
            gates = [wihraw[:, c, b, :] for c in range(3) for b in range(2)] + [whhraw[:, c, :] for c in range(3)]
            for b in range(2):
                for k in range(4):
                    last = transpose(bank[5 + b][:, k, :], gates[4 * b + k])
                last.then_inc(S["prep_ps"], 1)
            transpose(bI[:, 0, :], gates[8])
            nc.tensor.transpose(bI[:, 1, 0:GRAPHS], maskraw[:, :], ident[0:GRAPHS, 0:GRAPHS])
            pe.wait_ge(S["col_in"], 16 * 19)
            nc.tensor.transpose(bI[:, 3, 0:VECTORS], rows[:, :], ident[0:VECTORS, 0:VECTORS])
            nc.tensor.transpose(bI[:, 2, 0:3], wseraw[:, :], ident[0:3, 0:3]).then_inc(S["prep_ps"], 1)
            pe.wait_ge(S["late_in"], 16 * 9)
            pe.wait_ge(S["prep_a"], 4)
            pe.wait_ge(S["late_d"], 2)
            mm(bA[:, 0, 0:2], raw[:, 2, :], a12, start=True, stop=True)
            mm(bA[:, 1, 0:2], spread[:, 1, :], a12, start=True, stop=True)
            mm(bA[:, 2, :], spread[:, 0, :], wo[:, :], start=True, stop=True).then_inc(S["late_ps"], 1)
            pe.wait_ge(S["prep_d"], 7)
            pe.wait_ge(S["late_d"], LATE_D)

            def transposes(dst, src):
                for g in graphs:
                    last = transpose(dst[:, g, :], src[:, g, :])
                return last

            def weights_first(dst, lhsT, rhs, start=True, stop=True):
                return mm(dst, lhsT, rhs, start=start, stop=stop)

            def l0_transposes(q):
                pe.wait_ge(S["x0_in"], nth(q, 16, 16))
                if later(q):
                    pe.wait_ge(S["u_r"], nth(q, 1, 0))
                transposes(bA, x0).then_inc(S["x0T_ps"], 1)
                pe.wait_ge(S["adj0_in"], nth(q, 16, 16))
                if later(q):
                    pe.wait_ge(S["t_r"], nth(q, 1, 0))
                transposes(bB, adj0).then_inc(S["adj0T_ps"], 1)

            def l0_project(q):
                pe.wait_ge(S["x0T_r"], nth(q, 1, 1))
                mm(bA[:, :, :], w2T[:, 17, :], x0T[:, :, :], start=True, stop=True).then_inc(S["h1_ps"], 1)
                pe.wait_ge(S["adj0T_r"], nth(q, 1, 1))
                mm(bB[0:35, :, :], wseT[:, :], x0T[:, :, :], start=True, stop=True).then_inc(S["s_ps"], 1)

            def l0_messages(q):
                pe.wait_ge(S["h1_r"], nth(q, 1, 1))
                for g in graphs:
                    last = mm(bA[:, g, :], x0T[:, g, :], w2T[:, 18, :], start=True, stop=True)
                last.then_inc(S["msg_ps"], 1)
                pe.wait_ge(S["sa_r"], nth(q, 2, 2))
                pe.wait_ge(S["sb_r"], nth(q, 2, 2))
                for g in graphs:
                    last = mm(bB[:, g, :], sa[:, g, :], sbm[:, g, :], start=True, stop=True)
                last.then_inc(S["dist_ps"], 1)

            def l0_nmp(q):
                pe.wait_ge(S["msg_r"], nth(q, 1, 1))
                pe.wait_ge(S["aT_r"], nth(q, 1, 1))
                for g in graphs:
                    last = mm(bA[:, g, :], msg[:, g, :], aT[:, g, :], start=True, stop=True)
                last.then_inc(S["xn_ps"], 1)

            def l0_conv(q, first, end):
                if first == 0:
                    pe.wait_ge(S["x1_r"], nth(q, QUAD, 0)) if later(q) else None
                for k in range(first, end):
                    last = mm(bC[:, :, :], w2T[:, k, :], h1[:, :, k:k + 128], start=k == 0, stop=k == TAPS - 1)
                if end == TAPS:
                    last.then_inc(S["c2_ps"], 1)

            def l0_gate_hn(q):
                pe.wait_ge(S["ea_r"], nth(q, 1, 1))
                mm(bB[:, :, :], gateT[:, 8, :], x0T[:, :, :], start=True, stop=True).then_inc(S["ghn_ps"], 1)

            def l0_gate(q, dst, c):
                mm(dst, gateT[:, 6 + c, :], x0T[:, :, :], start=True, stop=False)
                mm(dst, gateT[:, 2 * c + 1, :], xnT[:, :, :], start=False, stop=False)
                return mm(dst, gateT[:, 2 * c, :], xcT[:, :, :], start=False, stop=True)

            def l0_gate_r(q):
                pe.wait_ge(S["xn_r"], nth(q, 1, 1))
                pe.wait_ge(S["xc_r"], nth(q, 1, 1))
                l0_gate(q, bA[:, :, :], 0).then_inc(S["r_ps"], 1)

            def l0_gate_z(q):
                l0_gate(q, bC[:, :, :], 1).then_inc(S["z_ps"], 1)

            def l0_gate_n(q):
                pe.wait_ge(S["r_r"], nth(q, 1, 1))
                mm(bA[:, :, :], gateT[:, 5, :], xnT[:, :, :], start=True, stop=False)
                mm(bA[:, :, :], gateT[:, 4, :], xcT[:, :, :], start=False, stop=True).then_inc(S["gin_ps"], 1)

            def l0_close(q):
                pe.wait_ge(S["y0_r"], nth(q, 1, 1))
                transposes(bC, yT).then_inc(S["y0T_ps"], 1)

            def l1_transposes(q):
                pe.wait_ge(S["x1_r"], nth(q, QUAD, QUAD))
                if later(q):
                    pe.wait_ge(S["o1_r"], nth(q, QUAD, 0))
                transposes(bD, x1).then_inc(S["x1T_ps"], 1)

            def l1_scores(q):
                pe.wait_ge(S["x1T_r"], nth(q, 1, 1))
                for g in graphs:
                    last = mm(bD[:, 0, 8 * g:8 * g + 8], x1T[:, g, :], wa[:, :], start=True, stop=True)
                last.then_inc(S["e1_ps"], 1)

            def l1_values(q):
                pe.wait_ge(S["e1_r"], nth(q, 1, 1))
                for g in graphs:
                    last = mm(bD[:, g, :], x1T[:, g, :], w1[:, :], start=True, stop=True)
                last.then_inc(S["h1n_ps"], 1)

            ejT_ps = bD[:, :, :].rearrange("p g n -> p (g n)").bitcast(BF16)

            def l1_rows(q):
                pe.wait_ge(S["h1x_r"], nth(q, 1, 1))
                pe.wait_ge(S["ej3_r"], nth(q, 1, 1))
                for g in graphs:
                    last = nc.tensor.transpose(ejT_ps[0:3 * H1, 128 * g:128 * g + 128],
                                               ej3[:, g, :, :].rearrange("p h c -> p (h c)"), ident16[:, :])
                last.then_inc(S["ejT_ps"], 1)

            def l1_logits(q, g):
                pe.wait_ge(S["mb1_r"], nth(q, 1, 1))
                if g == 0:
                    pe.wait_ge(S["ejT_r"], nth(q, 1, 1))
                else:
                    pe.wait_ge(S["o1_r"], nth(q, QUAD, g))
                mm(bD[:, :, :], ident16[:, :], mb1[:, g:g + 1, :].to_broadcast([128, H1, 128]), start=True, stop=False)
                for h in range(H1):
                    last = mm(bD[:, h, :], sel1[:, h, :], ejT[:, g, :], start=False, stop=h == H1 - 1)
                last.then_inc(S["z1_ps"], 1)

            def l1_turn(q, g):
                pe.wait_ge(S["p1_r"], nth(q, QUAD, g + 1))
                for h in range(H1):
                    last = transpose(bD[:, h, :], p1[:, h, :])
                last.then_inc(S["p1T_ps"], 1)

            def l1_output(q, g):
                pe.wait_ge(S["p1T_r"], nth(q, QUAD, g + 1))
                for h in range(H1):
                    last = mm(bD[:, h, 0:D1 + 1], p1T[:, h, :], h1x[:, g, h, :], start=True, stop=True)
                last.then_inc(S["u1_ps"], 1)

            def l2_transposes(q):
                pe.wait_ge(S["x2_r"], nth(q, QUAD, QUAD))
                if later(q):
                    pe.wait_ge(S["y2_r"], nth(q, 1, 0))
                transposes(bH, x2).then_inc(S["x2T_ps"], 1)

            def l2_project(q):
                pe.wait_ge(S["x2T_r"], nth(q, 1, 1))
                if later(q):
                    pe.wait_ge(S["p2Ta_r"], nth(q, QUAD, 0))
                    pe.wait_ge(S["p2Td_r"], nth(q, QUAD, 0))
                mm(bF[:, :, :], wq[:, :], x2T[:, :, :], start=True, stop=True).then_inc(S["q_ps"], 1)
                mm(bG[:, :, :], wk[:, :], x2T[:, :, :], start=True, stop=True).then_inc(S["k_ps"], 1)
                for g in graphs:
                    last = mm(bH[:, g, :], x2T[:, g, :], wv[:, :], start=True, stop=True)
                last.then_inc(S["v_ps"], 1)

            halves = ((bF, "p2Ta_r", "qT_r"), (bG, "p2Td_r", "kT_r"))

            def l2_logits(q, g):
                pe.wait_ge(S["mb2_r"], nth(q, 1, 1))
                if g == 0:
                    pe.wait_ge(S["qh_r"], nth(q, H2, H2))
                    pe.wait_ge(S["kT_r"], nth(q, 1, 1))
                for i, (dst, turned, _) in enumerate(halves):
                    if g:
                        pe.wait_ge(S[turned], nth(q, QUAD, g))
                    mm(dst[:, :, :], ident16[:, :], mb2[:, g:g + 1, :].to_broadcast([128, 4, 128]), start=True, stop=False)
                    for h in range(4):
                        last = mm(dst[:, h, :], qh[:, 4 * i + h, g, :], kT[:, g, :], start=False, stop=h == 3)
                    last.then_inc(S["s2_ps"], 1)

            def l2_turn(q, g):
                for i, (dst, _, _) in enumerate(halves):
                    pe.wait_ge(S["p2_r"], nth(q, 2 * QUAD, 2 * g + i + 1))
                    for h in range(4):
                        last = transpose(dst[:, h, :], p2[:, i, h, :])
                    last.then_inc(S["p2T_ps"], 1)

            uv = bH[:, :, :].rearrange("p g n -> p (g n)")[:, 0:H2 * (D2 + 1)].rearrange("p (h e) -> p h e", h=H2)

            def l2_output(q, g):
                if g == 0:
                    pe.wait_ge(S["v_r"], nth(q, 1, 1))
                else:
                    pe.wait_ge(S["o2T_r"], nth(q, QUAD, g))
                for i, name in enumerate(("p2Ta_r", "p2Td_r")):
                    pe.wait_ge(S[name], nth(q, QUAD, g + 1))
                    for h in range(4):
                        last = mm(uv[:, 4 * i + h, :], p2T[:, i, h, :], v2x[:, g, 4 * i + h, :], start=True, stop=True)
                last.then_inc(S["u2_ps"], 1)

            def l2_output_turn(q, g):
                pe.wait_ge(S["o2_r"], nth(q, QUAD, g + 1))
                transpose(bH[:, g, :], o2[:, :, :].rearrange("p h e -> p (h e)")).then_inc(S["o2T_ps"], 1)

            def l2_close(q):
                pe.wait_ge(S["o2T_r"], nth(q, QUAD, QUAD))
                for g in graphs:
                    last = mm(bH[:, g, :], o2T[:, g, :], wo[:, :], start=True, stop=True)
                last.then_inc(S["wo_ps"], 1)

            def l3_adj(q):
                pe.wait_ge(S["adj3_in"], nth(q, 16, 16))
                if later(q):
                    pe.wait_ge(S["y3_r"], nth(q, QUAD, 0))
                transposes(bI, adj3).then_inc(S["adj3T_ps"], 1)

            def l3_transposes(q):
                pe.wait_ge(S["x3_r"], nth(q, QUAD, QUAD))
                pe.wait_ge(S["adj3T_r"], nth(q, 1, 1))
                transposes(bI, x3).then_inc(S["x3T_ps"], 1)

            def l3_scores(q):
                pe.wait_ge(S["x3T_r"], nth(q, 1, 1))
                for g in graphs:
                    last = mm(bI[:, 0, 2 * g:2 * g + 2], x3T[:, g, :], w3a[:, :], start=True, stop=True)
                last.then_inc(S["e3_ps"], 1)

            def l3_values(q):
                pe.wait_ge(S["e3_r"], nth(q, 1, 1))
                for g in graphs:
                    last = mm(bI[:, g, :], x3T[:, g, :], w2T[:, 19, :], start=True, stop=True)
                last.then_inc(S["h3_ps"], 1)

            s1T_ps = bI[:, :, :].rearrange("p g n -> p (g n)").bitcast(BF16)

            def l3_rows(q):
                pe.wait_ge(S["hb3_r"], nth(q, 1, 1))
                pe.wait_ge(S["s13_r"], nth(q, 1, 1))
                for g in graphs:
                    last = nc.tensor.transpose(s1T_ps[0:3, 128 * g:128 * g + 128], s13[:, g, :], ident16[:, :])
                last.then_inc(S["s1T_ps"], 1)

            def l3_logits(q):
                pe.wait_ge(S["s1T_r"], nth(q, 1, 1))
                mm(bI[:, :, :], ones3[:, :], s1T[:, :, :], start=True, stop=True).then_inc(S["z3_ps"], 1)

            u3 = bI[:, :, :].rearrange("p g n -> p (g n)")[:, 0:2 * 129].rearrange("p (g e) -> p g e", g=2)

            def l3_output(q, pair):
                if pair == 0:
                    pe.wait_ge(S["att3_r"], nth(q, 1, 1))
                    pe.wait_ge(S["h3x_r"], nth(q, 2, 2))
                else:
                    pe.wait_ge(S["y3_r"], nth(q, QUAD, 2))
                for g in range(2):
                    last = mm(u3[:, g, :], att3[:, 2 * pair + g, :], h3x[:, 2 * pair + g, :], start=True, stop=True)
                last.then_inc(S["u3_ps"], 1)

            def step(t):
                q0, c0, q1, c1, q2, c2, q3 = plan(t)
                if q3 is not None:
                    l3_adj(q3)
                if c2 is not None:
                    l2_output_turn(c2, QUAD - 1)
                if q0 is not None:
                    l0_transposes(q0)
                if c2 is not None:
                    l2_close(c2)
                if c0 is not None:
                    l0_close(c0)
                if q2 is not None:
                    l2_transposes(q2)
                if q0 is not None:
                    l0_project(q0)
                if q3 is not None:
                    l3_transposes(q3)
                if q0 is not None:
                    l0_messages(q0)
                if q2 is not None:
                    l2_project(q2)
                if q3 is not None:
                    l3_scores(q3)
                if q1 is not None:
                    l1_transposes(q1)
                if q0 is not None:
                    l0_conv(q0, 0, 1)
                if q3 is not None:
                    l3_values(q3)
                if q1 is not None:
                    l1_scores(q1)
                if q0 is not None:
                    l0_nmp(q0)
                    l0_conv(q0, 1, 2)
                if q1 is not None:
                    l1_values(q1)
                if q3 is not None:
                    l3_rows(q3)
                if q0 is not None:
                    l0_conv(q0, 2, 3)
                if q1 is not None:
                    l1_rows(q1)
                if q3 is not None:
                    l3_logits(q3)
                taps = iter([(3, 4), (4, 5), (5, 7), (7, 8), (8, 9), (9, 11), (11, 12), (12, 13), (13, 15), (15, 17)])
                for g in graphs:
                    if q2 is not None:
                        if g:
                            l2_output_turn(q2, g - 1)
                        l2_logits(q2, g)
                    if q1 is not None:
                        l1_logits(q1, g)
                    if q0 is not None and g < 3:
                        l0_conv(q0, *next(taps))
                    if q3 is not None and g in (1, 2):
                        l3_output(q3, g - 1)
                    if q0 is not None and g == 3:
                        l0_gate_hn(q0)
                    if q2 is not None:
                        l2_turn(q2, g)
                    if q0 is not None:
                        l0_conv(q0, *next(taps)) if g < 3 else l0_gate_r(q0)
                    if q1 is not None:
                        l1_turn(q1, g)
                    if q0 is not None:
                        l0_conv(q0, *next(taps)) if g < 3 else l0_gate_z(q0)
                    if q2 is not None:
                        l2_output(q2, g)
                    if q0 is not None and g == 2:
                        l0_conv(q0, *next(taps))
                    if q0 is not None and g == 3:
                        l0_gate_n(q0)
                    if q1 is not None:
                        l1_output(q1, g)

            run(pe, step)

        @block.scalar
        def _(act):
            a_ = nc.scalar.activation
            for b, dst in ((0, w2T[:, 0:4, :]), (2, w2T[:, 8:12, :]), (4, w2T[:, 16:20, :]), (6, gateT[:, 4:8, :])):
                act.wait_ge(S["prep_ps"], b + 1)
                a_(dst, bank[b][:, :, :], ACT.Copy).then_inc(S["prep_a"], 1)
            act.wait_ge(S["late_d"], 1)
            for at in (SC1, SC2):
                a_(sc[:, at:at + 1], sc[:, at + 1:at + 2], ACT.Sqrt).then_inc(S["prep_a"], 1)
            act.wait_ge(S["late_d"], LATE_D)

            def l0_x(q):
                act.wait_ge(S["x0T_ps"], nth(q, 1, 1))
                if later(q):
                    act.wait_ge(S["d_r"], nth(q, 1, 0))
                    act.wait_ge(S["sT_r"], nth(q, 1, 0))
                a_(x0T[:, :, :], bA[:, :, :], ACT.Copy).then_inc(S["x0T_r"], 1)

            def l0_h1(q):
                act.wait_ge(S["h1_ps"], nth(q, 1, 1))
                a_(h1[:, :, PAD:PAD + 128], bA[:, :, :], ACT.Relu, bias=sc[:, SH1:SH1 + 1], scale=sc[:, SC1:SC1 + 1]).then_inc(S["h1_r"], 1)
                act.wait_ge(S["s_ps"], nth(q, 1, 1))
                if later(q):
                    act.wait_ge(S["sb_r"], nth(q, 2, 0))
                a_(sa[0:3, :, :], bB[0:3, :, :], ACT.Identity, bias=bse[0:3, :]).then_inc(S["sa_r"], 1)
                a_(sa[32:35, :, :], bB[32:35, :, :], ACT.Square, bias=bse[32:35, :]).then_inc(S["sa_r"], 1)

            def l0_exp(q):
                act.wait_ge(S["dist_ps"], nth(q, 1, 1))
                if later(q):
                    act.wait_ge(S["aT_r"], nth(q, 1, 0))
                a_(ea[:, :, :], bB[:, :, :], ACT.Exp).then_inc(S["ea_r"], 1)

            def l0_xn(q):
                act.wait_ge(S["xn_ps"], nth(q, 1, 1))
                a_(xnT[:, :, :], bA[:, :, :], ACT.Copy).then_inc(S["xn_r"], 1)

            def l0_xc(q):
                act.wait_ge(S["xcb_r"], nth(q, 1, 1))
                a_(xcT[:, :, :], xcb[:, :, :], ACT.Relu, bias=sc[:, SH2:SH2 + 1]).then_inc(S["xc_r"], 1)

            def l0_r(q):
                act.wait_ge(S["r_ps"], nth(q, 1, 1))
                if later(q):
                    act.wait_ge(S["r1_r"], nth(q, 1, 0))
                a_(rT[:, :, :], bA[:, :, :], ACT.Tanh, bias=sc[:, HBR:HBR + 1], scale=0.5).then_inc(S["r_r"], 1)

            def l0_z(q):
                act.wait_ge(S["z_ps"], nth(q, 1, 1))
                if later(q):
                    act.wait_ge(S["e_r"], nth(q, 1, 0))
                a_(zT[:, :, :], bC[:, :, :], ACT.Tanh, bias=sc[:, HBZ:HBZ + 1], scale=0.5).then_inc(S["z_r"], 1)

            def l0_n(q):
                act.wait_ge(S["u_r"], nth(q, 1, 1))
                a_(nT[:, :, :], uT[:, :, :], ACT.Tanh, bias=col[:, BIH + 2:BIH + 3]).then_inc(S["n_r"], 1)

            def l1_x(q):
                act.wait_ge(S["x1T_ps"], nth(q, 1, 1))
                a_(x1T[:, :, :], bD[:, :, :], ACT.Copy).then_inc(S["x1T_r"], 1)

            def l1_h(q):
                act.wait_ge(S["h1n_ps"], nth(q, 1, 1))
                a_(h1x[:, :, :, 0:D1], bD[:, :, :].rearrange("p g (h e) -> p g h e", h=H1), ACT.Copy).then_inc(S["h1x_r"], 1)

            def l1_rows(q):
                act.wait_ge(S["ejT_ps"], nth(q, 1, 1))
                a_(ejT[:, :, :], bD[:, :, :].rearrange("p g n -> p (g n)").bitcast(BF16)[0:3 * H1, 0:512].rearrange("p (g n) -> p g n", g=QUAD),
                   ACT.Copy).then_inc(S["ejT_r"], 1)

            def l1_exp(q, g):
                act.wait_ge(S["nm1_r"], nth(q, QUAD, g + 1))
                if g or later(q):
                    act.wait_ge(S["p1T_ps"], nth(q, QUAD, g))
                for h in range(H1):
                    last = a_(p1[:, h, :], zl[:, h, :], ACT.Exp, bias=nm1[:, h:h + 1])
                last.then_inc(S["p1_r"], 1)

            def l1_turned(q, g):
                act.wait_ge(S["p1T_ps"], nth(q, QUAD, g + 1))
                if g or later(q):
                    act.wait_ge(S["u1_ps"], nth(q, QUAD, g))
                a_(p1T[:, :, :], bD[:, :, :], ACT.Copy).then_inc(S["p1T_r"], 1)

            def l2_x(q):
                act.wait_ge(S["x2T_ps"], nth(q, 1, 1))
                a_(x2T[:, :, :], bH[:, :, :], ACT.Copy).then_inc(S["x2T_r"], 1)

            def l2_kv(q):
                act.wait_ge(S["k_ps"], nth(q, 1, 1))
                a_(kT[:, :, :], bG[:, :, :], ACT.Identity, bias=col[:, BK:BK + 1]).then_inc(S["kT_r"], 1)
                act.wait_ge(S["v_ps"], nth(q, 1, 1))
                a_(v2x[:, :, :, 0:D2], bH[:, :, :].rearrange("p g (h e) -> p g h e", h=H2), ACT.Copy).then_inc(S["v_r"], 1)

            def l2_exp(q, g):
                if g or later(q):
                    act.wait_ge(S["p2T_ps"], nth(q, 2 * QUAD, 2 * g))
                for i, src in enumerate((bF, bG)):
                    act.wait_ge(S["nm2_r"], nth(q, 2 * QUAD, 2 * g + i + 1))
                    for h in range(4):
                        last = a_(p2[:, i, h, :], src[:, h, :], ACT.Exp, bias=nm2[:, i, h:h + 1])
                    last.then_inc(S["p2_r"], 1)

            def l2_turned(q, g):
                act.wait_ge(S["p2T_ps"], nth(q, 2 * QUAD, 2 * g + 1))
                if g or later(q):
                    act.wait_ge(S["u2_ps"], nth(q, QUAD, g))
                a_(p2T[:, 0, :, :], bF[:, :, :], ACT.Copy).then_inc(S["p2Ta_r"], 1)

            def l2_output_turned(q, g):
                act.wait_ge(S["o2T_ps"], nth(q, QUAD, g + 1))
                a_(o2T[:, g, :], bH[:, g, :], ACT.Copy).then_inc(S["o2T_r"], 1)

            def l3_x(q):
                act.wait_ge(S["x3T_ps"], nth(q, 1, 1))
                a_(x3T[:, :, :], bI[:, :, :], ACT.Copy).then_inc(S["x3T_r"], 1)

            def l3_rows(q):
                act.wait_ge(S["s1T_ps"], nth(q, 1, 1))
                a_(s1T[:, :, :], bI[:, :, :].rearrange("p g n -> p (g n)").bitcast(BF16)[0:3, 0:512].rearrange("p (g n) -> p g n", g=QUAD),
                   ACT.Copy).then_inc(S["s1T_r"], 1)

            def l3_exp(q):
                act.wait_ge(S["z3_ps"], nth(q, 1, 1))
                act.wait_ge(S["e3_r"], nth(q, 1, 1))
                if later(q):
                    act.wait_ge(S["att3_r"], nth(q, 1, 0))
                for g in graphs:
                    last = a_(t3[:, g, :], bI[:, g, :], ACT.Exp, bias=s2n[:, g:g + 1], scale=-1.0)
                last.then_inc(S["t3_r"], 1)

            def step(t):
                q0, c0, q1, c1, q2, c2, q3 = plan(t)
                if c2 is not None:
                    l2_output_turned(c2, QUAD - 1)
                if q0 is not None:
                    l0_x(q0)
                if q2 is not None:
                    l2_x(q2)
                if q0 is not None:
                    l0_h1(q0)
                if q3 is not None:
                    l3_x(q3)
                if q0 is not None:
                    l0_exp(q0)
                if q2 is not None:
                    l2_kv(q2)
                if q1 is not None:
                    l1_x(q1)
                if q0 is not None:
                    l0_xn(q0)
                if q1 is not None:
                    l1_h(q1)
                if q3 is not None:
                    l3_rows(q3)
                if q1 is not None:
                    l1_rows(q1)
                if q3 is not None:
                    l3_exp(q3)
                for g in graphs:
                    if q2 is not None:
                        if g:
                            l2_output_turned(q2, g - 1)
                        l2_exp(q2, g)
                    if q1 is not None:
                        l1_exp(q1, g)
                    if q0 is not None and g == 3:
                        l0_xc(q0)
                    if q2 is not None:
                        l2_turned(q2, g)
                    if q0 is not None and g == 3:
                        l0_r(q0)
                    if q1 is not None:
                        l1_turned(q1, g)
                    if q0 is not None and g == 3:
                        l0_z(q0)
                        l0_n(q0)

            run(act, step)

        @block.vector
        def _(dve):
            v = nc.vector
            for b, dst in ((1, w2T[:, 4:8, :]), (3, w2T[:, 12:16, :]), (5, gateT[:, 0:4, :])):
                dve.wait_ge(S["prep_ps"], b + 1)
                v.tensor_copy(dst, bank[b][:, :, :]).then_inc(S["prep_d"], 1)
            dve.wait_ge(S["prep_ps"], 8)
            v.tensor_copy(gateT[:, 8, :], bI[:, 0, :]).then_inc(S["prep_d"], 1)
            v.tensor_copy(nodeT[:, :], bI[:, 1, 0:GRAPHS]).then_inc(S["prep_d"], 1)
            dve.wait_ge(S["pool_c"], POOL_C)
            for at in (0, 32):
                last = v.tensor_copy(wseT[:, at:at + 3], bI[:, 2, 0:3])
            last.then_inc(S["prep_d"], 1)
            v.tensor_copy(col[:, :], bI[:, 3, 0:VECTORS]).then_inc(S["prep_d"], 1)
            dve.wait_ge(S["prep_d"], 7)
            for at, src in ((SH1, BN1V), (SH2, BN2V)):
                last = v.tensor_scalar(sc[:, at:at + 1], col[:, src:src + 1], EPS, None, ALU.add)
            last.then_inc(S["late_d"], 1)
            v.tensor_copy(spread[:, 0, :], col[:, BV:BV + 1].to_broadcast([128, 128]))
            v.tensor_copy(spread[:, 1, :], col[:, B3:B3 + 1].to_broadcast([128, 128])).then_inc(S["late_d"], 1)
            dve.wait_ge(S["prep_a"], 6)
            n = [7]

            def chain(ins_):
                n[0] += 1
                ins_.then_inc(S["prep_d"], 1)
                dve.wait_ge(S["prep_d"], n[0])

            for g_at, b_at, m_at, scale, shift in ((BN1G, BN1B, BN1M, SC1, SH1), (BN2G, BN2B, BN2M, SC2, SH2)):
                c = lambda tile, at: tile[:, at:at + 1]
                chain(v.reciprocal(c(sc, TMP), c(sc, scale)))
                chain(v.tensor_tensor(c(sc, scale), c(sc, TMP), c(col, g_at), ALU.mult))
                chain(v.tensor_tensor(c(sc, TMP), c(sc, scale), c(col, m_at), ALU.mult))
                chain(v.tensor_tensor(c(sc, shift), c(col, b_at), c(sc, TMP), ALU.subtract))
            chain(v.tensor_tensor(sc[:, TMP:TMP + 2], col[:, BIH:BIH + 2], col[:, BHH:BHH + 2], ALU.add))
            chain(v.tensor_scalar(sc[:, HBR:HBR + 2], sc[:, TMP:TMP + 2], 0.5, None, ALU.mult))
            dve.wait_ge(S["late_in"], 16 * 9)
            w1h = w1[:, :].rearrange("p (h e) -> p h e", h=H1)
            for i in range(2):
                chain(v.tensor_tensor(aprod[:, H1 * i:H1 * i + H1, :], w1h, abc[:, :, D1 * i:D1 * i + D1], ALU.mult))
            chain(v.tensor_reduce(wa[:, :], aprod[:, :, :], AX.X, ALU.add))
            dve.wait_ge(S["late_ps"], 1)
            v.tensor_copy(w3a[:, :], bA[:, 0, 0:2]).then_inc(S["late_d"], 1)
            chain(v.tensor_copy(sc[:, 8:10], bA[:, 1, 0:2]))
            chain(v.tensor_tensor(sc[:, 10:11], sc[:, 8:9], sc[:, 9:10], ALU.add))
            chain(v.tensor_tensor(sc[:, 11:12], sc[:, 10:11], attb[:, :], ALU.add))
            v.tensor_scalar(nc3[:, :], sc[:, 11:12], -1.0, None, ALU.mult).then_inc(S["late_d"], 1)
            v.tensor_tensor(cbc[:, :], bA[:, 2, :], bcast[:, 1, :], ALU.add).then_inc(S["late_d"], 1)
            dve.wait_ge(S["late_d"], LATE_D)

            def norm_stats(i, q, src):
                if later(q):
                    dve.wait_ge(rstd_r[i], nth(q, 1, 0))
                for g in graphs:
                    last = v.bn_stats(stats[i][:, g, :], src[:, g, :])
                last.then_inc(st_r[i], 1)
                dve.wait_ge(st_r[i], nth(q, 1, 1))
                mean_e, m2_e, mean_o, m2_o = (stats[i][:, :, c] for c in (1, 2, 4, 5))
                v.tensor_tensor(mom[i][:, 0, :], mean_e, mean_o, ALU.add)
                v.tensor_tensor(mom[i][:, 1, :], mean_e, mean_o, ALU.subtract)
                v.tensor_tensor(mom[i][:, 2, :], m2_e, m2_o, ALU.add).then_inc(mv_r[i], 1)
                dve.wait_ge(mv_r[i], nth(q, 2, 1))
                v.tensor_scalar(mv[i][:, 0, :], mom[i][:, 0, :], 0.5, None, ALU.mult)
                v.tensor_tensor(mv[i][:, 1, :], mom[i][:, 1, :], mom[i][:, 1, :], ALU.mult)
                v.tensor_scalar(mv[i][:, 2, :], mom[i][:, 2, :], 1.0 / D, EPS, ALU.mult, ALU.add).then_inc(mv_r[i], 1)
                dve.wait_ge(mv_r[i], nth(q, 2, 2))
                v.scalar_tensor_tensor(ve[i][:, :], mv[i][:, 1, :], 0.25, mv[i][:, 2, :], ALU.mult, ALU.add).then_inc(ve_r[i], 1)

            def norm_apply(i, q, dst, src, done):
                dve.wait_ge(rstd_r[i], nth(q, 1, 1))
                for g in graphs:
                    last = v.tensor_scalar(dst[:, g, :], src[:, g, :], mv[i][:, 0, g:g + 1], rstd[i][:, g:g + 1], ALU.subtract, ALU.mult)
                    if done != S["res_r"]:
                        last.then_inc(done, 1)
                if done == S["res_r"]:
                    last.then_inc(done, 1)

            def split3(dst, src, rest, first, last_sem, q):
                v.tensor_copy(dst[0], src).then_inc(first, 1)
                dve.wait_ge(first, nth(q, 3, 1))
                v.tensor_tensor(rest, src, dst[0], ALU.subtract).then_inc(first, 1)
                dve.wait_ge(first, nth(q, 3, 2))
                v.tensor_copy(dst[1], rest).then_inc(first, 1)
                dve.wait_ge(first, nth(q, 3, 3))
                v.tensor_tensor(dst[2], rest, dst[1], ALU.subtract).then_inc(last_sem, 1)

            def l0_adj(q):
                dve.wait_ge(S["adj0T_ps"], nth(q, 1, 1))
                if later(q):
                    dve.wait_ge(S["aT_r"], nth(q, 1, 0))
                v.tensor_copy(adj0T[:, :, :], bB[:, :, :]).then_inc(S["adj0T_r"], 1)

            def l0_s(q):
                dve.wait_ge(S["sa_r"], nth(q, 2, 2))
                v.tensor_scalar(sbm[0:3, :, :], sa[0:3, :, :], 2.0, None, ALU.mult).then_inc(S["sb_r"], 1)
                v.tensor_scalar(sbm[64:67, :, :], sa[32:35, :, :], -1.0, None, ALU.mult).then_inc(S["sb_r"], 1)

            def l0_msg(q):
                dve.wait_ge(S["msg_ps"], nth(q, 1, 1))
                v.tensor_tensor(msgb[:, :, :], bA[:, :, :], bcast[:, 0:1, :].to_broadcast([128, QUAD, 128]), ALU.add).then_inc(S["msgb_r"], 1)
                dve.wait_ge(S["msgb_r"], nth(q, 1, 1))
                v.tensor_scalar(msg[:, :, :], msgb[:, :, :], 0.0, None, ALU.max).then_inc(S["msg_r"], 1)

            def l0_xc(q):
                dve.wait_ge(S["c2_ps"], nth(q, 1, 1))
                v.scalar_tensor_tensor(xcb[:, :, :], bC[:, :, :], sc[:, SC2:SC2 + 1], x0T[:, :, :], ALU.mult, ALU.add).then_inc(S["xcb_r"], 1)

            def l0_r1(q):
                dve.wait_ge(S["r_r"], nth(q, 1, 1))
                v.tensor_scalar(r1T[:, :, :], rT[:, :, :], 1.0, None, ALU.add).then_inc(S["r1_r"], 1)
                dve.wait_ge(S["r1_r"], nth(q, 1, 1))
                dve.wait_ge(S["ghn_ps"], nth(q, 1, 1))
                v.scalar_tensor_tensor(tT[:, :, :], bB[:, :, :], col[:, BHH + 2:BHH + 3], r1T[:, :, :], ALU.add, ALU.mult).then_inc(S["t_r"], 1)

            def l0_u(q):
                dve.wait_ge(S["t_r"], nth(q, 1, 1))
                dve.wait_ge(S["gin_ps"], nth(q, 1, 1))
                v.scalar_tensor_tensor(uT[:, :, :], tT[:, :, :], 0.5, bA[:, :, :], ALU.mult, ALU.add).then_inc(S["u_r"], 1)

            def l0_y(q):
                dve.wait_ge(S["n_r"], nth(q, 1, 1))
                v.tensor_tensor(dT[:, :, :], x0T[:, :, :], nT[:, :, :], ALU.subtract).then_inc(S["d_r"], 1)
                v.tensor_tensor(sT[:, :, :], x0T[:, :, :], nT[:, :, :], ALU.add).then_inc(S["sT_r"], 1)
                dve.wait_ge(S["d_r"], nth(q, 1, 1))
                dve.wait_ge(S["z_r"], nth(q, 1, 1))
                v.scalar_tensor_tensor(eT[:, :, :], zT[:, :, :], 1.0, dT[:, :, :], ALU.add, ALU.mult).then_inc(S["e_r"], 1)
                dve.wait_ge(S["e_r"], nth(q, 1, 1))
                v.scalar_tensor_tensor(yT[:, :, :], eT[:, :, :], 0.5, sT[:, :, :], ALU.mult, ALU.add).then_inc(S["y0_r"], 1)

            def bias_of(dst, src, loaded, used, done, q):
                dve.wait_ge(S[loaded], nth(q, 16, 16))
                if later(q):
                    dve.wait_ge(S[used[0]], nth(q, used[1], 0))
                v.tensor_scalar(dst[:, :, :], src[:, :, :], 0.0, NEG, ALU.is_le, ALU.mult).then_inc(S[done], 1)

            def l1_scores(q):
                dve.wait_ge(S["e1_ps"], nth(q, 1, 1))
                v.tensor_copy(e1[:, :, :], bD[:, 0, 0:8 * QUAD].rearrange("p (g c) -> p g c", g=QUAD)).then_inc(S["e1_r"], 1)
                dve.wait_ge(S["e1_r"], nth(q, 1, 1))
                split3([ej3[:, :, :, i] for i in range(3)], e1[:, :, H1:2 * H1], ejr[:, :, :], S["ejs_r"], S["ej3_r"], q)

            def l1_logits(q, g):
                dve.wait_ge(S["z1_ps"], nth(q, QUAD, g + 1))
                v.tensor_tensor(zi[:, :, :], bD[:, :, :], e1[:, g, 0:H1].unsqueeze(2).to_broadcast([128, H1, 128]), ALU.add).then_inc(S["zi_r"], 1)
                dve.wait_ge(S["zi_r"], nth(q, QUAD, g + 1))
                if g or later(q):
                    dve.wait_ge(S["p1_r"], nth(q, QUAD, g))
                v.scalar_tensor_tensor(zl[:, :, :], zi[:, :, :], SLOPE, zi[:, :, :], ALU.mult, ALU.max).then_inc(S["zl_r"], 1)
                dve.wait_ge(S["zl_r"], nth(q, QUAD, g + 1))
                v.tensor_reduce(nm1[:, :], zl[:, :, :], AX.X, ALU.max, negate=True).then_inc(S["nm1_r"], 1)

            def l1_output(q, g):
                dve.wait_ge(S["u1_ps"], nth(q, QUAD, g + 1))
                v.reciprocal(rc1[:, :], bD[:, :, D1]).then_inc(S["rc1_r"], 1)
                dve.wait_ge(S["rc1_r"], nth(q, QUAD, g + 1))
                v.tensor_tensor(o1[:, :, :], bD[:, :, 0:D1], rc1[:, :].unsqueeze(2).to_broadcast([128, H1, D1]), ALU.mult).then_inc(S["o1_r"], 1)
                dve.wait_ge(S["o1_r"], nth(q, QUAD, g + 1))
                v.tensor_tensor(y1[:, g, :], o1[:, :, :].rearrange("p h e -> p (h e)"), x1[:, g, :], ALU.add).then_inc(S["y1_r"], 1)

            def l2_q(q):
                dve.wait_ge(S["q_ps"], nth(q, 1, 1))
                if later(q):
                    dve.wait_ge(S["qh_r"], nth(q, H2, 0))
                v.tensor_scalar(qT[:, :, :], bF[:, :, :], col[:, BQ:BQ + 1], None, ALU.add).then_inc(S["qT_r"], 1)

            def l2_max(q, g):
                if g or later(q):
                    dve.wait_ge(S["p2_r"], nth(q, 2 * QUAD, 2 * g))
                for i, src in enumerate((bF, bG)):
                    dve.wait_ge(S["s2_ps"], nth(q, 2 * QUAD, 2 * g + i + 1))
                    v.tensor_reduce(nm2[:, i, :], src[:, :, :], AX.X, ALU.max, negate=True).then_inc(S["nm2_r"], 1)

            def l2_turned(q, g):
                dve.wait_ge(S["p2T_ps"], nth(q, 2 * QUAD, 2 * g + 2))
                if g or later(q):
                    dve.wait_ge(S["u2_ps"], nth(q, QUAD, g))
                v.tensor_copy(p2T[:, 1, :, :], bG[:, :, :]).then_inc(S["p2Td_r"], 1)

            uv = bH[:, :, :].rearrange("p g n -> p (g n)")[:, 0:H2 * (D2 + 1)].rearrange("p (h e) -> p h e", h=H2)

            def l2_output(q, g):
                dve.wait_ge(S["u2_ps"], nth(q, QUAD, g + 1))
                v.reciprocal(rc2[:, :], uv[:, :, D2]).then_inc(S["rc2_r"], 1)
                dve.wait_ge(S["rc2_r"], nth(q, QUAD, g + 1))
                v.tensor_tensor(o2[:, :, :], uv[:, :, 0:D2], rc2[:, :].unsqueeze(2).to_broadcast([128, H2, D2]), ALU.mult).then_inc(S["o2_r"], 1)

            def l2_close(q):
                dve.wait_ge(S["wo_ps"], nth(q, 1, 1))
                dve.wait_ge(S["x2c_r"], nth(q, 1, 1))
                v.tensor_tensor(y2[:, :, :], bH[:, :, :], x2c[:, :, :], ALU.add).then_inc(S["y2_r"], 1)
                dve.wait_ge(S["y2_r"], nth(q, 1, 1))

            def l3_masks(q):
                dve.wait_ge(S["adj3T_ps"], nth(q, 1, 1))
                v.tensor_copy(adj3T[:, :, :], bI[:, :, :]).then_inc(S["adj3T_r"], 1)
                v.tensor_copy(mk[:, :], nodeT[:, bass.ds(q * QUAD, QUAD)]).then_inc(S["mk_r"], 1)
                dve.wait_ge(S["mk_r"], nth(q, 1, 1))
                v.tensor_tensor(mk2[:, :], mk[:, :], mk[:, :], ALU.mult).then_inc(S["mks_r"], 1)

            def l3_scores(q):
                dve.wait_ge(S["e3_ps"], nth(q, 1, 1))
                if later(q):
                    dve.wait_ge(S["t3_r"], nth(q, 1, 0))
                e = bI[:, 0, 0:2 * QUAD].rearrange("p (g c) -> p g c", g=QUAD)
                v.tensor_scalar(s2n[:, :], e[:, :, 1], -1.0, nc3[:, :], ALU.mult, ALU.add)
                v.tensor_copy(e3[:, :, :], e).then_inc(S["e3_r"], 1)
                dve.wait_ge(S["e3_r"], nth(q, 1, 1))
                split3([s13[:, :, i] for i in range(3)], e3[:, :, 0], s1r[:, :], S["s1s_r"], S["s13_r"], q)

            def l3_values(q):
                dve.wait_ge(S["h3_ps"], nth(q, 1, 1))
                if later(q):
                    dve.wait_ge(S["h3x_r"], nth(q, 2, 0))
                v.tensor_tensor(hb3[:, :, :], bI[:, :, :], bcast[:, 2:3, :].to_broadcast([128, QUAD, 128]), ALU.add).then_inc(S["hb3_r"], 1)

            def l3_att(q):
                dve.wait_ge(S["t3_r"], nth(q, 1, 1))
                v.tensor_scalar(d3[:, :, :], t3[:, :, :], 1.0, BIG, ALU.add, ALU.min).then_inc(S["d3_r"], 1)
                dve.wait_ge(S["d3_r"], nth(q, 2, 1))
                v.reciprocal(r3[:, :, :], d3[:, :, :]).then_inc(S["d3_r"], 1)
                dve.wait_ge(S["d3_r"], nth(q, 2, 2))
                v.tensor_tensor(att3[:, :, :], r3[:, :, :], adj3T[:, :, :], ALU.mult).then_inc(S["att3_r"], 1)

            u3 = bI[:, :, :].rearrange("p g n -> p (g n)")[:, 0:2 * 129].rearrange("p (g e) -> p g e", g=2)

            def l3_output(q, pair):
                at = slice(2 * pair, 2 * pair + 2)
                k = 4 * pair
                dve.wait_ge(S["u3_ps"], nth(q, 2, pair + 1))
                v.tensor_tensor(den3[:, :, 0], u3[:, :, 128], mk[:, at], ALU.mult).then_inc(S["f3_r"], 1)
                dve.wait_ge(S["f3_r"], nth(q, 8, k + 1))
                v.tensor_scalar(den3[:, :, 1], den3[:, :, 0], TINY, None, ALU.add).then_inc(S["f3_r"], 1)
                dve.wait_ge(S["f3_r"], nth(q, 8, k + 2))
                v.reciprocal(den3[:, :, 2], den3[:, :, 1]).then_inc(S["f3_r"], 1)
                dve.wait_ge(S["f3_r"], nth(q, 8, k + 3))
                v.tensor_tensor(den3[:, :, 3], den3[:, :, 2], mk2[:, at], ALU.mult).then_inc(S["f3_r"], 1)
                dve.wait_ge(S["f3_r"], nth(q, 8, k + 4))
                for g in range(2):
                    v.scalar_tensor_tensor(y3[:, 2 * pair + g, :], u3[:, g, 0:128], den3[:, g, 3:4], x3[:, 2 * pair + g, :],
                                           ALU.mult, ALU.add).then_inc(S["y3_r"], 1)

            def l3_close(q):
                dve.wait_ge(S["y3_r"], nth(q, QUAD, QUAD))
                norm_stats(3, q, y3)
                if later(q):
                    dve.wait_ge(S["out_w"], nth(q, 16, 0))
                norm_apply(3, q, res, y3, S["res_r"])

            def step(t):
                q0, c0, q1, c1, q2, c2, q3 = plan(t)
                if c1 is not None:
                    dve.wait_ge(S["y1_r"], nth(c1, QUAD, QUAD))
                    norm_stats(1, c1, y1)
                if q3 is not None:
                    l3_masks(q3)
                if q0 is not None:
                    l0_adj(q0)
                if c1 is not None:
                    norm_apply(1, c1, x2, y1, S["x2_r"])
                if c2 is not None:
                    l2_close(c2)
                    norm_stats(2, c2, y2)
                if q2 is not None:
                    bias_of(mb2, adj2, "adj2_in", ("s2_ps", 2 * QUAD), "mb2_r", q2)
                if c0 is not None:
                    dve.wait_ge(S["y0T_ps"], nth(c0, 1, 1))
                    norm_stats(0, c0, bC)
                if c2 is not None:
                    norm_apply(2, c2, x3, y2, S["x3_r"])
                if q1 is not None:
                    bias_of(mb1, adj1, "adj1_in", ("z1_ps", QUAD), "mb1_r", q1)
                if c0 is not None:
                    norm_apply(0, c0, x1, bC, S["x1_r"])
                if q0 is not None:
                    l0_s(q0)
                    l0_msg(q0)
                if q2 is not None:
                    l2_q(q2)
                if q3 is not None:
                    l3_scores(q3)
                if q1 is not None:
                    l1_scores(q1)
                if q3 is not None:
                    l3_values(q3)
                for g in graphs:
                    if q2 is not None:
                        l2_max(q2, g)
                    if g == 0 and q3 is not None:
                        l3_att(q3)
                    if q1 is not None:
                        l1_logits(q1, g)
                    if q0 is not None and g == 3:
                        l0_xc(q0)
                    if q3 is not None and g in (1, 2):
                        l3_output(q3, g - 1)
                    if q2 is not None:
                        l2_turned(q2, g)
                    if q0 is not None and g == 3:
                        l0_r1(q0)
                    if q2 is not None:
                        l2_output(q2, g)
                    if q0 is not None and g == 3:
                        l0_u(q0)
                    if q1 is not None:
                        l1_output(q1, g)
                    if q3 is not None and g == 3:
                        l3_close(q3)
                if q0 is not None:
                    l0_y(q0)

            run(dve, step)


def kernel(**inputs):
    import numpy as np
    import concourse.bacc as bacc
    from concourse.bass_utils import run_bass_kernel_spmd

    nc = bacc.Bacc("TRN2", target_bir_lowering=False, num_devices=1)
    arrays, ins = {}, {}
    for name in INS:
        a = np.ascontiguousarray(inputs[name])
        if a.ndim == 0:
            a = a.reshape(1)
        arrays["in_" + name] = a
        ins[name] = nc.dram_tensor("in_" + name, a.shape, mybir.dt.from_np(a.dtype), kind="ExternalInput").ap()
    out = nc.dram_tensor("out_0", (GRAPHS, N, D), F32, kind="ExternalOutput").ap()
    build(nc, ins, out)
    r = run_bass_kernel_spmd(nc, [arrays], core_ids=[0])
    return r.results[0]["out_0"]
```

```python
from contextlib import ExitStack

import concourse.bass as bass
from concourse import mybir

F32 = mybir.dt.float32
BF16 = mybir.dt.bfloat16
ACT = mybir.ActivationFunctionType
ALU = mybir.AluOpType
AX = mybir.AxisListType

GRAPHS, N, D = 64, 128, 128
QUAD = 4
QUADS = GRAPHS // QUAD
TAPS = 17
PAD = TAPS // 2
H1 = 4
D1 = D // H1
H2 = 8
D2 = D // H2
EPS = 1e-5
TINY = 1e-8
BIG = 3.0e38
NEG = -9.0e15
SLOPE = 0.2
LAYERS = 4
Q_PARTS = (0, 0, 1, 1, 0, 2, 1)
K_PARTS = (0, 1, 0, 1, 2, 0, 2)
SLOTS = len(Q_PARTS)
STACK = SLOTS * D2

PIECES = [
    ("l1_logits", 2, 2), ("l2_output", 4, 1), ("l0_conv", 1, 14), ("l0_conv", 1, 15), ("l0_conv", 1, 16),
    ("l1_turn", 2, 2), ("l0_gate_hn", 1), ("l0_gate_r", 1), ("l1_output", 2, 2), ("l2_output_turn", 4, 1),
    ("l2_weights", 4, 2, 0), ("l2_weights", 4, 2, 1), ("l1_logits", 2, 3), ("l0_gate_z", 1), ("l2_output", 4, 2),
    ("l0_gate_n", 1), ("l1_turn", 2, 3), ("l0_update", 1), ("l2_output_turn", 4, 2), ("l2_weights", 4, 3, 0),
    ("l2_weights", 4, 3, 1), ("l1_output", 2, 3), ("l0_transposes", 0), ("l2_output", 4, 3), ("l1_norm", 2),
    ("l0_project", 0), ("l0_messages", 0), ("l2_output_turn", 4, 3), ("l2_close", 4), ("l2_fetch", 3),
    ("l2_transposes", 2), ("l3_transposes", 4), ("l0_close", 1), ("l2_project", 2), ("l0_distances", 0),
    ("l0_apply", 1), ("l3_scores", 4), ("l1_transposes", 1), ("l2_parts", 2), ("l2_maximum", 3, 0),
    ("l2_maximum", 3, 1), ("l0_conv", 0, 0), ("l3_values", 4), ("l1_scores", 1), ("l2_maximum", 3, 2),
    ("l2_maximum", 3, 3), ("l1_values", 1), ("l2_maximum", 3, 4), ("l3_rows", 4), ("l0_conv", 0, 1),
    ("l2_maximum", 3, 5), ("l2_maximum", 3, 6), ("l1_rows", 1), ("l0_nmp", 0), ("l2_maximum", 3, 7),
    ("l1_logits", 1, 0), ("l3_logits", 4), ("l0_conv", 0, 2), ("l0_conv", 0, 3), ("l0_conv", 0, 4), ("l0_conv", 0, 5),
    ("l2_rows", 3), ("l0_conv", 0, 6), ("l3_weights", 4), ("l0_conv", 0, 7), ("l1_turn", 1, 0), ("l0_conv", 0, 8),
    ("l1_output", 1, 0), ("l3_output", 4, 0), ("l0_conv", 0, 9), ("l1_logits", 1, 1), ("l2_weights", 3, 0, 0),
    ("l2_weights", 3, 0, 1), ("l0_conv", 0, 10), ("l3_output", 4, 1), ("l2_output", 3, 0), ("l0_conv", 0, 11),
    ("l0_conv", 0, 12), ("l1_turn", 1, 1), ("l2_output_turn", 3, 0), ("l3_close", 4), ("l2_weights", 3, 1, 0),
    ("l1_output", 1, 1), ("l2_weights", 3, 1, 1), ("l0_conv", 0, 13),
]
DEPTH = 1 + max(piece[1] for piece in PIECES)


def order():
    return PIECES


INS = ["x", "adj", "nodemask", "L0_gnn_w_se", "L0_gnn_b_se", "L0_gnn_conv1_w", "L0_gnn_bn1_g", "L0_gnn_bn1_b",
       "L0_gnn_bn1_m", "L0_gnn_bn1_v", "L0_gnn_conv2_w", "L0_gnn_bn2_g", "L0_gnn_bn2_b", "L0_gnn_bn2_m",
       "L0_gnn_bn2_v", "L0_gnn_w_msg", "L0_gnn_b_msg", "L0_gnn_w_ih", "L0_gnn_b_ih", "L0_gnn_w_hh", "L0_gnn_b_hh",
       "L1_gnn_W", "L1_gnn_a", "L2_gnn_Wq", "L2_gnn_bq", "L2_gnn_Wk", "L2_gnn_bk", "L2_gnn_Wv", "L2_gnn_bv",
       "L2_gnn_Wo", "L2_gnn_bo", "L3_gnn_W", "L3_gnn_b", "L3_gnn_a1", "L3_gnn_a2", "L3_gnn_att_b"]


def nth(q, per, k):
    return q * per + k


def later(q):
    return not isinstance(q, int) or q > 0


def build(nc, ins, out):
    with ExitStack() as ctx:
        def sb(name, shape, dt=F32):
            return ctx.enter_context(nc.sbuf_tensor(name, shape, dt))

        def sem(name):
            return ctx.enter_context(nc.semaphore(name))

        bank = [ctx.enter_context(nc.psum_tensor(f"bank{c}", [128, QUAD, 128], F32)) for c in "ABCDFGHI"]
        bA, bB, bC, bD, bF, bG, bH, bI = bank

        ident = sb("ident", [128, 128])
        ident16 = sb("ident16", [128, 128], BF16)
        w2raw = sb("w2raw", [128, D, TAPS])
        wihraw = sb("wihraw", [128, 3, 2, 128])
        whhraw = sb("whhraw", [128, 3, 128])
        raw = sb("raw", [128, 3, 128])
        wseraw = sb("wseraw", [3, 128])
        maskraw = sb("maskraw", [GRAPHS, N])
        w2T = sb("w2T", [128, 20, 128])
        gateT = sb("gateT", [128, 9, 128])
        wseT = sb("wseT", [128, 35])
        nodeT = sb("nodeT", [128, GRAPHS])
        rows = sb("rows", [20, 128])
        col = sb("col", [128, 20])
        BN1G, BN1B, BN1M, BN1V, BN2G, BN2B, BN2M, BN2V, BIH, BHH, BQ, BK, BV, B3, A1, A2 = 0, 1, 2, 3, 4, 5, 6, 7, 8, 11, 14, 15, 16, 17, 18, 19
        VECTORS = 20
        bse = sb("bse", [35, 1])
        sc = sb("sc", [128, 16])
        SC1, SH1, SC2, SH2, HBR, HBZ, TMP = 0, 1, 2, 3, 4, 5, 6
        wa = sb("wa", [128, 2 * H1])
        w1 = sb("w1", [128, 128])
        abc = sb("abc", [128, H1, 2 * D1])
        aprod = sb("aprod", [128, 2 * H1, D1])
        wq = sb("wq", [128, 128])
        wk = sb("wk", [128, 128])
        wv = sb("wv", [128, 128])
        wo = sb("wo", [128, 128])
        bcast = sb("bcast", [128, 3, 128])
        cbc = sb("cbc", [128, 128])
        spread = sb("spread", [128, 2, 128])
        a12 = col[:, A1:A2 + 1]
        w3a = sb("w3a", [128, 2])
        attb = sb("attb", [128, 1])
        nc3 = sb("nc3", [128, 1])
        sel1 = sb("sel1", [3 * H1, H1, 128], BF16)
        ones3 = sb("ones3", [3, 128], BF16)
        ones = sb("ones", [128, 128])
        half = sb("half", [128, QUAD])

        x0 = sb("x0", [128, QUAD, 128])
        adj0 = sb("adj0", [128, QUAD, 128])
        x0T = sb("x0T", [128, QUAD, 128])
        adjT = sb("adjT", [128, GRAPHS, 128])
        h1 = sb("h1", [128, QUAD, 128 + 2 * PAD])
        sa = sb("sa", [67, QUAD, 128])
        sbm = sb("sbm", [67, QUAD, 128])
        msgb = sb("msgb", [128, QUAD, 128])
        msg = sb("msg", [128, QUAD, 128])
        ea = sb("ea", [128, QUAD, 128])
        aT = sb("aT", [128, QUAD, 128])
        xnT = sb("xnT", [128, QUAD, 128])
        xcb = sb("xcb", [128, QUAD, 128])
        xcT = sb("xcT", [128, QUAD, 128])
        rT = sb("rT", [128, QUAD, 128])
        zT = sb("zT", [128, QUAD, 128])
        r1T = sb("r1T", [128, QUAD, 128])
        tT = sb("tT", [128, QUAD, 128])
        uT = sb("uT", [128, QUAD, 128])
        nT = sb("nT", [128, QUAD, 128])
        dT, sT, eT = uT, r1T, tT
        yT = sb("yT", [128, QUAD, 128])
        stats = [sb(f"stats{i}", [128, QUAD, 6]) for i in range(LAYERS)]
        mom = [sb(f"mom{i}", [128, 3, QUAD]) for i in range(LAYERS)]
        mv = [sb(f"mv{i}", [128, 3, QUAD]) for i in range(LAYERS)]
        ve = [sb(f"ve{i}", [128, QUAD]) for i in range(LAYERS)]
        rstd = [sb(f"rstd{i}", [128, QUAD]) for i in range(LAYERS)]
        x1 = sb("x1", [128, QUAD, 128])
        adj1 = sb("adj1", [128, QUAD, 128])
        x1T = sb("x1T", [128, QUAD, 128])
        mb1 = sb("mb1", [128, QUAD, 128], BF16)
        e1 = sb("e1", [128, QUAD, 2 * H1])
        ej3 = sb("ej3", [128, QUAD, H1, 3], BF16)
        ejr = sb("ejr", [128, QUAD, H1])
        ejT = sb("ejT", [3 * H1, QUAD, 128], BF16)
        h1x = sb("h1x", [128, QUAD, H1, D1 + 1])
        zi = sb("zi", [128, H1, 128])
        zl = sb("zl", [128, H1, 128])
        nm1 = sb("nm1", [128, H1])
        p1 = sb("p1", [128, H1, 128])
        p1T = sb("p1T", [128, H1, 128])
        rc1 = sb("rc1", [128, H1])
        o1 = sb("o1", [128, H1, D1])
        y1 = sb("y1", [128, QUAD, 128])
        x2 = sb("x2", [128, QUAD, 128])
        x2c = sb("x2c", [128, QUAD, 128])
        adj2 = sb("adj2", [128, QUAD, 128])
        x2T = sb("x2T", [128, QUAD, 128])
        mb2 = sb("mb2", [128, QUAD, 128], BF16)
        qf = sb("qf", [128, 2, QUAD, 128])
        pieces3 = sb("pieces3", [128, 2, 3, QUAD, 128], BF16)
        rest = sb("rest", [128, 2, QUAD, 128])
        qst = sb("qst", [STACK + 3, H2, QUAD, 128], BF16)
        kst = sb("kst", [STACK + 3, H2, QUAD, 128], BF16)
        v2n = sb("v2n", [128, QUAD, 128])
        v2x = sb("v2x", [128, QUAD, H2, D2 + 1])
        x2d = sb("x2d", [128, QUAD, 128])
        nm2 = sb("nm2", [128, H2, QUAD])
        nm2r = sb("nm2r", [128, H2, QUAD])
        nm23 = sb("nm23", [128, 3, H2, QUAD], BF16)
        nm2T = sb("nm2T", [3 * H2 * QUAD, 128], BF16)
        p2T = sb("p2T", [128, 2, 4, 128])
        rc2 = sb("rc2", [128, H2])
        o2 = sb("o2", [128, H2, D2])
        o2T = sb("o2T", [128, QUAD, 128])
        y2 = sb("y2", [128, QUAD, 128])
        x3 = sb("x3", [128, QUAD, 128])
        x3T = sb("x3T", [128, QUAD, 128])
        e3 = sb("e3", [128, QUAD, 2])
        s2n = sb("s2n", [128, QUAD])
        s13 = sb("s13", [128, QUAD, 3], BF16)
        s1r = sb("s1r", [128, QUAD])
        s1T = sb("s1T", [3, QUAD, 128], BF16)
        hb3 = sb("hb3", [128, QUAD, 128])
        h3x = sb("h3x", [128, QUAD, 129])
        mk = sb("mk", [128, QUAD])
        mk2 = sb("mk2", [128, QUAD])
        loan = w2raw[:, :, :].rearrange("p i k -> p (i k)")[:, 0:4 * QUAD * 128].rearrange("p (c g n) -> p c g n", c=4, g=QUAD)
        t3, d3, r3, att3 = (loan[:, i, :, :] for i in range(4))
        den3 = sb("den3", [128, 2, 4])
        y3 = sb("y3", [128, QUAD, 128])
        res = sb("res", [128, QUAD, 128])

        names = """w_in c_in col_in pool_c prep_ps prep_a prep_d late_in late_ps late_d
            x0_in adj0_in x0T_ps adj0T_ps x0T_r adj0T_r h1_ps h1_r s_ps sa_r sb_r msg_ps msgb_r msg_r dist_ps ea_r
            aT_r xn_ps xn_r c2_ps xcb_r xc_r ghn_ps r_ps r_r r1_r t_r z_ps z_r gin_ps u_r n_r d_r sT_r e_r y0_r
            y0T_ps adj1_in mb1_r x1_r x1T_ps x1T_r e1_ps e1_r ejs_r ej3_r ejT_ps ejT_r h1n_ps h1x_r z1_ps zi_r zl_r
            nm1_r p1_r p1T_ps p1T_r u1_ps rc1_r o1_r y1_r
            adj2_in mb2_r x2_r x2c_r x2d_r x2T_ps x2T_r q_ps qf_r k_ps kf_r v_ps v_r v2_r part0_r rest_r part1_r part2_r
            turn_w stack_in s2_ps nm2_r nms_r nm23_r nm2T_ps nm2T_r nmturn_w nm_in w2_ps p2_r u2_ps rc2_r o2_r
            o2T_ps o2T_r wo_ps y2_r
            x3_r x3T_ps x3T_r mk_r mks_r e3_ps e3_r s1s_r s13_r s1T_ps s1T_r h3_ps hb3_r h3x_r
            z3_ps t3_r d3_r att3_r u3_ps f3_r y3_r res_r out_w""".split()
        S = {n: sem(n) for n in names}
        st_r = [sem(f"stats{i}_r") for i in range(LAYERS)]
        mv_r = [sem(f"mv{i}_r") for i in range(LAYERS)]
        ve_r = [sem(f"ve{i}_r") for i in range(LAYERS)]
        rstd_r = [sem(f"rstd{i}_r") for i in range(LAYERS)]

        POOL_C = 19
        LATE_D = 5
        graphs = range(QUAD)
        mm = nc.tensor.matmul

        def quad_of(name, first):
            return ins[name][bass.ds(first, QUAD)].rearrange("g n d -> n g d")

        LAST = QUADS + DEPTH - 1
        FIRST, END = DEPTH, QUADS

        def run(eng, pieces, before=None):
            def step(t):
                for name, behind, *more in PIECES:
                    q = t - behind
                    if name in pieces and (not isinstance(t, int) or 0 <= q < QUADS):
                        pieces[name](q, *more)

            for t in range(FIRST):
                step(t)
            with eng.Fori(FIRST, END) as t:
                step(t)
            for t in range(END, LAST):
                step(t)

        turn_qk = nc.dram_tensor("turn_qk", (2, 3, H2 * D2, QUAD * 128), BF16, kind="Internal").ap()
        turn_nm = nc.dram_tensor("turn_nm", (3, H2 * QUAD * 128), BF16, kind="Internal").ap()

        block = ctx.enter_context(nc.Block())

        @block.sync
        def _(sp):
            sp.dma_start(w2raw[:, :, :], ins["L0_gnn_conv2_w"]).then_inc(S["w_in"], 16)
            sp.dma_start(raw[:, 0, :], ins["L0_gnn_conv1_w"].rearrange("o i k -> o (i k)")).then_inc(S["w_in"], 16)
            sp.dma_start(raw[:, 1, :], ins["L0_gnn_w_msg"]).then_inc(S["w_in"], 16)
            sp.dma_start(raw[:, 2, :], ins["L3_gnn_W"]).then_inc(S["w_in"], 16)
            sp.dma_start(wihraw[:, :, :, :], ins["L0_gnn_w_ih"].rearrange("(c o) (b i) -> o c b i", c=3, b=2)).then_inc(S["w_in"], 16)
            sp.dma_start(whhraw[:, :, :], ins["L0_gnn_w_hh"].rearrange("(c o) i -> o c i", c=3)).then_inc(S["w_in"], 16)
            sp.dma_start(wseraw[:, :], ins["L0_gnn_w_se"]).then_inc(S["w_in"], 16)
            sp.dma_start(maskraw[:, :], ins["nodemask"]).then_inc(S["w_in"], 16)
            for dst, name in ((w1, "L1_gnn_W"), (wq, "L2_gnn_Wq"), (wk, "L2_gnn_Wk"), (wv, "L2_gnn_Wv"), (wo, "L2_gnn_Wo")):
                sp.dma_start(dst[:, :], ins[name]).then_inc(S["late_in"], 16)
            sp.dma_start(abc[:, :, :], ins["L1_gnn_a"].partition_broadcast(128)).then_inc(S["late_in"], 16)
            for i, name in enumerate(("L0_gnn_b_msg", "L2_gnn_bo", "L3_gnn_b")):
                sp.dma_start(bcast[:, i, :], ins[name].partition_broadcast(128)).then_inc(S["late_in"], 16)

            def l0_transposes(q):
                if later(q):
                    sp.wait_ge(S["x0T_ps"], nth(q, 1, 0))
                    sp.wait_ge(S["adj0T_ps"], nth(q, 1, 0))
                sp.dma_start(x0[:, :, :], quad_of("x", q * QUAD)).then_inc(S["x0_in"], 16)
                sp.dma_start(adj0[:, :, :], quad_of("adj", q * QUAD)).then_inc(S["adj0_in"], 16)

            def l1_transposes(q):
                if later(q):
                    sp.wait_ge(S["mb1_r"], nth(q, 1, 0))
                sp.dma_start(adj1[:, :, :], quad_of("adj", q * QUAD)).then_inc(S["adj1_in"], 16)

            def l2_fetch(q):
                if later(q):
                    sp.wait_ge(S["w2_ps"], nth(q, 2 * QUAD, 0))
                sp.wait_ge(S["turn_w"], nth(q, 32, 32))
                for i in range(SLOTS):
                    for tile, side, part in ((qst, 0, Q_PARTS[i]), (kst, 1, K_PARTS[i])):
                        sp.dma_start(tile[D2 * i:D2 * i + D2, :, :, :].rearrange("d h g n -> d h (g n)"),
                                     turn_qk[side, part].rearrange("(h d) x -> d h x", h=H2)).then_inc(S["stack_in"], 16)
                if later(q):
                    sp.wait_ge(S["mb2_r"], nth(q, 1, 0))
                sp.dma_start(adj2[:, :, :], quad_of("adj", q * QUAD)).then_inc(S["adj2_in"], 16)

            def l2_parts(q):
                if later(q):
                    sp.wait_ge(S["stack_in"], nth(q, 32 * SLOTS, 0))
                for side in range(2):
                    sp.wait_ge(S["part2_r"], nth(q, 2, side + 1))
                    sp.dma_start(turn_qk[side].rearrange("c p x -> p c x"),
                                 pieces3[:, side, :, :, :].rearrange("p c g n -> p c (g n)")).then_inc(S["turn_w"], 16)

            def l2_rows(q):
                if later(q):
                    sp.wait_ge(S["nm_in"], nth(q, 16, 0))
                sp.wait_ge(S["nm2T_r"], nth(q, 1, 1))
                sp.dma_start(turn_nm.rearrange("c (x n) -> (c x) n", n=128), nm2T[:, :]).then_inc(S["nmturn_w"], 16)
                sp.wait_ge(S["nmturn_w"], nth(q, 16, 16))
                if later(q):
                    sp.wait_ge(S["w2_ps"], nth(q, 2 * QUAD, 0))
                sp.dma_start(qst[STACK:STACK + 3, :, :, :].rearrange("c h g n -> c (h g n)"), turn_nm).then_inc(S["nm_in"], 16)

            def l3_close(q):
                sp.wait_ge(S["res_r"], nth(q, 1, 1))
                sp.dma_start(out[bass.ds(q * QUAD, QUAD)].rearrange("g n d -> n g d"), res[:, :, :]).then_inc(S["out_w"], 16)

            run(sp, dict(l0_transposes=l0_transposes, l1_transposes=l1_transposes, l2_fetch=l2_fetch, l2_parts=l2_parts,
                         l2_rows=l2_rows, l3_close=l3_close))
            sp.wait_ge(S["out_w"], 16 * QUADS)

        @block.gpsimd
        def _(gp):
            g_ = nc.gpsimd
            n_c = [0]

            def const(ins_):
                n_c[0] += 1
                ins_.then_inc(S["pool_c"], 1)

            const(g_.memset(ident[:, :], 0.0))
            const(g_.memset(sel1[:, :, :], 1.0))
            const(g_.memset(kst[:, :, :, :], 1.0))
            const(g_.memset(ones[:, :], 1.0))
            const(g_.memset(ones3[:, :], 1.0))
            const(g_.memset(half[:, :], -0.5))
            const(g_.memset(h1[:, :, :], 0.0))
            const(g_.memset(sa[:, :, :], 0.0))
            const(g_.memset(sbm[:, :, :], 0.0))
            const(g_.memset(h1x[:, :, :, D1:D1 + 1], 1.0))
            const(g_.memset(v2x[:, :, :, D2:D2 + 1], 1.0))
            const(g_.memset(wseT[:, :], 0.0))
            const(g_.memset(bse[:, :], 0.0))
            gp.wait_ge(S["pool_c"], n_c[0])
            const(g_.affine_select(out=ident[:, :], in_=ident[:, :], compare_op=ALU.not_equal, fill=1.0, base=0,
                                   pattern=[[-1, 128]], channel_multiplier=1))
            const(g_.affine_select(out=sel1[:, :, :], in_=sel1[:, :, :], compare_op=ALU.is_ge, fill=0.0, base=0,
                                   pattern=[[-3, H1], [0, 128]], channel_multiplier=1))
            for tile, value in ((sa[64:67, :, :], 1.0), (sbm[32:35, :, :], -1.0)):
                gp.wait_ge(S["pool_c"], n_c[0])
                const(g_.memset(tile, value))
            gp.wait_ge(S["pool_c"], n_c[0])
            const(g_.affine_select(out=sel1[:, :, :], in_=sel1[:, :, :], compare_op=ALU.is_ge, fill=0.0, base=2,
                                   pattern=[[3, H1], [0, 128]], channel_multiplier=-1))
            const(g_.tensor_copy(ident16[:, :], ident[:, :]))
            assert n_c[0] == POOL_C
            for at, name, parts in ((BN1G, "L0_gnn_bn1_g", 1), (BN1B, "L0_gnn_bn1_b", 1), (BN1M, "L0_gnn_bn1_m", 1),
                                    (BN1V, "L0_gnn_bn1_v", 1), (BN2G, "L0_gnn_bn2_g", 1), (BN2B, "L0_gnn_bn2_b", 1),
                                    (BN2M, "L0_gnn_bn2_m", 1), (BN2V, "L0_gnn_bn2_v", 1), (BIH, "L0_gnn_b_ih", 3),
                                    (BHH, "L0_gnn_b_hh", 3), (BQ, "L2_gnn_bq", 1), (BK, "L2_gnn_bk", 1), (BV, "L2_gnn_bv", 1),
                                    (B3, "L3_gnn_b", 1), (A1, "L3_gnn_a1", 1), (A2, "L3_gnn_a2", 1)):
                gp.dma_start(rows[at:at + parts, :], ins[name].rearrange("(c p) -> c p", c=parts)).then_inc(S["col_in"], 16)
            gp.wait_ge(S["pool_c"], POOL_C)
            gp.dma_start(attb[:, :], ins["L3_gnn_att_b"].partition_broadcast(128)).then_inc(S["col_in"], 16)
            for at in (0, 32):
                gp.dma_start(bse[at:at + 3, :], ins["L0_gnn_b_se"].rearrange("(p c) -> p c", c=1)).then_inc(S["col_in"], 16)
            gp.wait_ge(S["late_d"], LATE_D)

            def root(i, q):
                gp.wait_ge(ve_r[i], nth(q, 1, 1))
                g_.tensor_tensor(rstd[i][:, :], ve[i][:, :], half[:, :], ALU.pow).then_inc(rstd_r[i], 1)

            def l2_transposes(q):
                gp.wait_ge(S["x2_r"], nth(q, QUAD, QUAD))
                if later(q):
                    gp.wait_ge(S["x2d_r"], nth(q, 1, 0))
                g_.tensor_tensor(x2c[:, :, :], x2[:, :, :], cbc[:, :].unsqueeze(1).to_broadcast([128, QUAD, 128]),
                                 ALU.add).then_inc(S["x2c_r"], 1)

            def l2_parts(q):
                for side, ready in ((0, "qf_r"), (1, "kf_r")):
                    gp.wait_ge(S["part0_r"], nth(q, 2, side + 1))
                    g_.tensor_tensor(rest[:, side, :, :], qf[:, side, :, :], pieces3[:, side, 0, :, :], ALU.subtract).then_inc(S["rest_r"], 1)
                for side in range(2):
                    gp.wait_ge(S["part1_r"], nth(q, 2, side + 1))
                    g_.tensor_tensor(pieces3[:, side, 2, :, :], rest[:, side, :, :], pieces3[:, side, 1, :, :], ALU.subtract).then_inc(S["part2_r"], 1)

            def l0_distances(q):
                gp.wait_ge(S["adj0T_r"], nth(q, 1, 1))
                gp.wait_ge(S["ea_r"], nth(q, 1, 1))
                g_.tensor_tensor(aT[:, :, :], ea[:, :, :], adjT[:, bass.ds(q * QUAD, QUAD), :], ALU.mult).then_inc(S["aT_r"], 1)

            def l3_values(q):
                gp.wait_ge(S["hb3_r"], nth(q, 1, 1))
                gp.wait_ge(S["mk_r"], nth(q, 1, 1))
                g_.tensor_tensor(h3x[:, :, 0:128], hb3[:, :, :], mk[:, :].unsqueeze(2).to_broadcast([128, QUAD, 128]),
                                 ALU.mult).then_inc(S["h3x_r"], 1)
                g_.tensor_copy(h3x[:, :, 128:129], mk[:, :].unsqueeze(2)).then_inc(S["h3x_r"], 1)

            run(gp, dict(l1_norm=lambda q: root(1, q), l2_close=lambda q: root(2, q),
                         l0_close=lambda q: root(0, q), l2_transposes=l2_transposes, l2_parts=l2_parts,
                         l0_distances=l0_distances, l3_values=l3_values, l3_close=lambda q: root(3, q)))

        @block.tensor
        def _(pe):
            def transpose(o, i, size=128):
                return nc.tensor.transpose(o, i, ident[0:size, 0:size])

            pe.wait_ge(S["pool_c"], POOL_C)
            pe.wait_ge(S["w_in"], 16 * 8)
            for b in range(4):
                for k in range(4):
                    last = transpose(bank[b][:, k, :], w2raw[:, :, 4 * b + k])
                last.then_inc(S["prep_ps"], 1)
            transpose(bF[:, 0, :], w2raw[:, :, 16])
            for k in range(3):
                last = transpose(bF[:, k + 1, :], raw[:, k, :])
            last.then_inc(S["prep_ps"], 1)
            gates = [wihraw[:, c, b, :] for c in range(3) for b in range(2)] + [whhraw[:, c, :] for c in range(3)]
            for b in range(2):
                for k in range(4):
                    last = transpose(bank[5 + b][:, k, :], gates[4 * b + k])
                last.then_inc(S["prep_ps"], 1)
            transpose(bI[:, 0, :], gates[8])
            nc.tensor.transpose(bI[:, 1, 0:GRAPHS], maskraw[:, :], ident[0:GRAPHS, 0:GRAPHS])
            pe.wait_ge(S["col_in"], 16 * 19)
            nc.tensor.transpose(bI[:, 3, 0:VECTORS], rows[:, :], ident[0:VECTORS, 0:VECTORS])
            nc.tensor.transpose(bI[:, 2, 0:3], wseraw[:, :], ident[0:3, 0:3]).then_inc(S["prep_ps"], 1)
            pe.wait_ge(S["late_in"], 16 * 9)
            pe.wait_ge(S["prep_a"], 4)
            pe.wait_ge(S["late_d"], 2)
            mm(bA[:, 0, 0:2], raw[:, 2, :], a12, start=True, stop=True)
            mm(bA[:, 1, 0:2], spread[:, 1, :], a12, start=True, stop=True)
            mm(bA[:, 2, :], spread[:, 0, :], wo[:, :], start=True, stop=True).then_inc(S["late_ps"], 1)
            pe.wait_ge(S["prep_d"], 7)
            pe.wait_ge(S["late_d"], LATE_D)

            def transposes(dst, src):
                for g in graphs:
                    last = transpose(dst[:, g, :], src[:, g, :])
                return last

            def weights_first(dst, lhsT, rhs, start=True, stop=True):
                return mm(dst, lhsT, rhs, start=start, stop=stop)

            def l0_transposes(q):
                pe.wait_ge(S["x0_in"], nth(q, 16, 16))
                if later(q):
                    pe.wait_ge(S["u_r"], nth(q, 1, 0))
                transposes(bA, x0).then_inc(S["x0T_ps"], 1)
                pe.wait_ge(S["adj0_in"], nth(q, 16, 16))
                if later(q):
                    pe.wait_ge(S["t_r"], nth(q, 1, 0))
                transposes(bB, adj0).then_inc(S["adj0T_ps"], 1)

            def l0_project(q):
                pe.wait_ge(S["x0T_r"], nth(q, 1, 1))
                mm(bA[:, :, :], w2T[:, 17, :], x0T[:, :, :], start=True, stop=True).then_inc(S["h1_ps"], 1)
                pe.wait_ge(S["adj0T_r"], nth(q, 1, 1))
                mm(bB[0:35, :, :], wseT[:, :], x0T[:, :, :], start=True, stop=True).then_inc(S["s_ps"], 1)

            def l0_messages(q):
                pe.wait_ge(S["h1_r"], nth(q, 1, 1))
                for g in graphs:
                    last = mm(bA[:, g, :], x0T[:, g, :], w2T[:, 18, :], start=True, stop=True)
                last.then_inc(S["msg_ps"], 1)

            def l0_distances(q):
                pe.wait_ge(S["sa_r"], nth(q, 2, 2))
                pe.wait_ge(S["sb_r"], nth(q, 2, 2))
                for g in graphs:
                    last = mm(bB[:, g, :], sa[:, g, :], sbm[:, g, :], start=True, stop=True)
                last.then_inc(S["dist_ps"], 1)

            def l0_nmp(q):
                pe.wait_ge(S["msg_r"], nth(q, 1, 1))
                pe.wait_ge(S["aT_r"], nth(q, 1, 1))
                for g in graphs:
                    last = mm(bA[:, g, :], msg[:, g, :], aT[:, g, :], start=True, stop=True)
                last.then_inc(S["xn_ps"], 1)

            def l0_conv(q, k):
                if k == 0 and later(q):
                    pe.wait_ge(S["x1_r"], nth(q, QUAD, 0))
                last = mm(bC[:, :, :], w2T[:, k, :], h1[:, :, k:k + 128], start=k == 0, stop=k == TAPS - 1)
                if k == TAPS - 1:
                    last.then_inc(S["c2_ps"], 1)

            def l0_gate_hn(q):
                pe.wait_ge(S["ea_r"], nth(q, 1, 1))
                mm(bB[:, :, :], gateT[:, 8, :], x0T[:, :, :], start=True, stop=True).then_inc(S["ghn_ps"], 1)

            def l0_gate(q, dst, c):
                mm(dst, gateT[:, 6 + c, :], x0T[:, :, :], start=True, stop=False)
                mm(dst, gateT[:, 2 * c + 1, :], xnT[:, :, :], start=False, stop=False)
                return mm(dst, gateT[:, 2 * c, :], xcT[:, :, :], start=False, stop=True)

            def l0_gate_r(q):
                pe.wait_ge(S["xn_r"], nth(q, 1, 1))
                pe.wait_ge(S["xc_r"], nth(q, 1, 1))
                l0_gate(q, bA[:, :, :], 0).then_inc(S["r_ps"], 1)

            def l0_gate_z(q):
                l0_gate(q, bC[:, :, :], 1).then_inc(S["z_ps"], 1)

            def l0_gate_n(q):
                pe.wait_ge(S["r_r"], nth(q, 1, 1))
                mm(bA[:, :, :], gateT[:, 5, :], xnT[:, :, :], start=True, stop=False)
                mm(bA[:, :, :], gateT[:, 4, :], xcT[:, :, :], start=False, stop=True).then_inc(S["gin_ps"], 1)

            def l0_close(q):
                pe.wait_ge(S["y0_r"], nth(q, 1, 1))
                transposes(bC, yT).then_inc(S["y0T_ps"], 1)

            def l1_transposes(q):
                pe.wait_ge(S["x1_r"], nth(q, QUAD, QUAD))
                if later(q):
                    pe.wait_ge(S["o1_r"], nth(q, QUAD, 0))
                transposes(bD, x1).then_inc(S["x1T_ps"], 1)

            def l1_scores(q):
                pe.wait_ge(S["x1T_r"], nth(q, 1, 1))
                for g in graphs:
                    last = mm(bD[:, 0, 8 * g:8 * g + 8], x1T[:, g, :], wa[:, :], start=True, stop=True)
                last.then_inc(S["e1_ps"], 1)

            def l1_values(q):
                pe.wait_ge(S["e1_r"], nth(q, 1, 1))
                for g in graphs:
                    last = mm(bD[:, g, :], x1T[:, g, :], w1[:, :], start=True, stop=True)
                last.then_inc(S["h1n_ps"], 1)

            ejT_ps = bD[:, :, :].rearrange("p g n -> p (g n)").bitcast(BF16)

            def l1_rows(q):
                pe.wait_ge(S["h1x_r"], nth(q, 1, 1))
                pe.wait_ge(S["ej3_r"], nth(q, 1, 1))
                for g in graphs:
                    last = nc.tensor.transpose(ejT_ps[0:3 * H1, 128 * g:128 * g + 128],
                                               ej3[:, g, :, :].rearrange("p h c -> p (h c)"), ident16[:, :])
                last.then_inc(S["ejT_ps"], 1)

            def l1_logits(q, g):
                pe.wait_ge(S["mb1_r"], nth(q, 1, 1))
                if g == 0:
                    pe.wait_ge(S["ejT_r"], nth(q, 1, 1))
                else:
                    pe.wait_ge(S["o1_r"], nth(q, QUAD, g))
                mm(bD[:, :, :], ident16[:, :], mb1[:, g:g + 1, :].to_broadcast([128, H1, 128]), start=True, stop=False)
                for h in range(H1):
                    last = mm(bD[:, h, :], sel1[:, h, :], ejT[:, g, :], start=False, stop=h == H1 - 1)
                last.then_inc(S["z1_ps"], 1)

            def l1_turn(q, g):
                pe.wait_ge(S["p1_r"], nth(q, QUAD, g + 1))
                for h in range(H1):
                    last = transpose(bD[:, h, :], p1[:, h, :])
                last.then_inc(S["p1T_ps"], 1)

            def l1_output(q, g):
                pe.wait_ge(S["p1T_r"], nth(q, QUAD, g + 1))
                for h in range(H1):
                    last = mm(bD[:, h, 0:D1 + 1], p1T[:, h, :], h1x[:, g, h, :], start=True, stop=True)
                last.then_inc(S["u1_ps"], 1)

            def l2_transposes(q):
                pe.wait_ge(S["x2_r"], nth(q, QUAD, QUAD))
                if not isinstance(q, int) or q >= 2:
                    pe.wait_ge(S["y2_r"], nth(q - 1, 1, 0))
                transposes(bH, x2).then_inc(S["x2T_ps"], 1)

            def l2_project(q):
                pe.wait_ge(S["x2T_r"], nth(q, 1, 1))
                if not isinstance(q, int) or q >= 2:
                    pe.wait_ge(S["p2_r"], nth(q - 1, 2 * QUAD, 0))
                mm(bF[:, :, :], wq[:, :], x2T[:, :, :], start=True, stop=True).then_inc(S["q_ps"], 1)
                mm(bG[:, :, :], wk[:, :], x2T[:, :, :], start=True, stop=True).then_inc(S["k_ps"], 1)
                for g in graphs:
                    last = mm(bH[:, g, :], x2T[:, g, :], wv[:, :], start=True, stop=True)
                last.then_inc(S["v_ps"], 1)

            pair = (bF, bG)

            def l2_maximum(q, job):
                g, i = divmod(job, 2)
                if job == 0:
                    pe.wait_ge(S["stack_in"], nth(q, 32 * SLOTS, 32 * SLOTS))
                    pe.wait_ge(S["mb2_r"], nth(q, 1, 1))
                if job < 2:
                    if not isinstance(q, int) or q + 1 < QUADS:
                        pe.wait_ge(S["qf_r" if job == 0 else "kf_r"], nth(q, 1, 2))
                    elif later(q):
                        pe.wait_ge(S["p2_r"], nth(q, 2 * QUAD, 0))
                else:
                    pe.wait_ge(S["nm2_r"], nth(q, 2 * QUAD, job - 1))
                dst = pair[i]
                mm(dst[:, :, :], ident16[:, :], mb2[:, g:g + 1, :].to_broadcast([128, 4, 128]), start=True, stop=False)
                for h in range(4):
                    last = mm(dst[:, h, :], qst[0:STACK, 4 * i + h, g, :], kst[0:STACK, 4 * i + h, g, :], start=False, stop=h == 3)
                last.then_inc(S["s2_ps"], 1)

            def l2_rows(q):
                pe.wait_ge(S["nm23_r"], nth(q, 1, 1))
                if not isinstance(q, int) or q + 1 < QUADS:
                    pe.wait_ge(S["v_r"], nth(q, 1, 2))
                elif later(q):
                    pe.wait_ge(S["y2_r"], nth(q, 1, 0))
                nc.tensor.transpose(bH[:, :, :].rearrange("p g n -> p (g n)").bitcast(BF16)[0:3 * H2 * QUAD, 0:128],
                                    nm23[:, :, :, :].rearrange("p c h g -> p (c h g)"), ident16[:, :]).then_inc(S["nm2T_ps"], 1)

            def l2_weights(q, g, i):
                if g == 0 and i == 0:
                    pe.wait_ge(S["nm_in"], nth(q, 16, 16))
                    pe.wait_ge(S["nm2_r"], nth(q, 2 * QUAD, 2 * QUAD))
                if g:
                    pe.wait_ge(S["p2_r"], nth(q, 2 * QUAD, 2 * g + i - 1))
                dst = pair[i]
                mm(dst[:, :, :], mb2[:, g, :], ident16[:, :].unsqueeze(1).to_broadcast([128, 4, 128]), start=True, stop=False)
                for h in range(4):
                    last = mm(dst[:, h, :], kst[:, 4 * i + h, g, :], qst[:, 4 * i + h, g, :], start=False, stop=h == 3)
                last.then_inc(S["w2_ps"], 1)

            uv = bH[:, :, :].rearrange("p g n -> p (g n)")[:, 0:H2 * (D2 + 1)].rearrange("p (h e) -> p h e", h=H2)

            def l2_output(q, g):
                pe.wait_ge(S["v2_r"], nth(q, 1, 1))
                if g == 0:
                    pe.wait_ge(S["nm2T_r"], nth(q, 1, 1))
                else:
                    pe.wait_ge(S["o2T_r"], nth(q, QUAD, g))
                pe.wait_ge(S["p2_r"], nth(q, 2 * QUAD, 2 * g + 2))
                for h in range(H2):
                    last = mm(uv[:, h, :], p2T[:, h // 4, h % 4, :], v2x[:, g, h, :], start=True, stop=True)
                last.then_inc(S["u2_ps"], 1)

            def l2_output_turn(q, g):
                pe.wait_ge(S["o2_r"], nth(q, QUAD, g + 1))
                transpose(bH[:, g, :], o2[:, :, :].rearrange("p h e -> p (h e)")).then_inc(S["o2T_ps"], 1)

            def l2_close(q):
                pe.wait_ge(S["o2T_r"], nth(q, QUAD, QUAD))
                for g in graphs:
                    last = mm(bH[:, g, :], o2T[:, g, :], wo[:, :], start=True, stop=True)
                last.then_inc(S["wo_ps"], 1)

            def l3_transposes(q):
                pe.wait_ge(S["x3_r"], nth(q, QUAD, QUAD))
                if later(q):
                    pe.wait_ge(S["y3_r"], nth(q, QUAD, 0))
                transposes(bI, x3).then_inc(S["x3T_ps"], 1)

            def l3_scores(q):
                pe.wait_ge(S["x3T_r"], nth(q, 1, 1))
                for g in graphs:
                    last = mm(bI[:, 0, 2 * g:2 * g + 2], x3T[:, g, :], w3a[:, :], start=True, stop=True)
                last.then_inc(S["e3_ps"], 1)

            def l3_values(q):
                pe.wait_ge(S["e3_r"], nth(q, 1, 1))
                for g in graphs:
                    last = mm(bI[:, g, :], x3T[:, g, :], w2T[:, 19, :], start=True, stop=True)
                last.then_inc(S["h3_ps"], 1)

            s1T_ps = bI[:, :, :].rearrange("p g n -> p (g n)").bitcast(BF16)

            def l3_rows(q):
                pe.wait_ge(S["hb3_r"], nth(q, 1, 1))
                pe.wait_ge(S["s13_r"], nth(q, 1, 1))
                for g in graphs:
                    last = nc.tensor.transpose(s1T_ps[0:3, 128 * g:128 * g + 128], s13[:, g, :], ident16[:, :])
                last.then_inc(S["s1T_ps"], 1)

            def l3_logits(q):
                pe.wait_ge(S["s1T_r"], nth(q, 1, 1))
                mm(bI[:, :, :], ones3[:, :], s1T[:, :, :], start=True, stop=True).then_inc(S["z3_ps"], 1)

            u3 = bI[:, :, :].rearrange("p g n -> p (g n)")[:, 0:2 * 129].rearrange("p (g e) -> p g e", g=2)

            def l3_output(q, pair):
                if pair == 0:
                    pe.wait_ge(S["att3_r"], nth(q, 1, 1))
                    pe.wait_ge(S["h3x_r"], nth(q, 2, 2))
                else:
                    pe.wait_ge(S["y3_r"], nth(q, QUAD, 2))
                for g in range(2):
                    last = mm(u3[:, g, :], att3[:, 2 * pair + g, :], h3x[:, 2 * pair + g, :], start=True, stop=True)
                last.then_inc(S["u3_ps"], 1)

            run(pe, dict(l0_transposes=l0_transposes, l0_project=l0_project, l0_messages=l0_messages,
                         l0_distances=l0_distances, l0_nmp=l0_nmp, l0_conv=l0_conv, l0_gate_hn=l0_gate_hn, l0_gate_r=l0_gate_r,
                         l0_gate_z=l0_gate_z, l0_gate_n=l0_gate_n, l0_close=l0_close, l1_transposes=l1_transposes,
                         l1_scores=l1_scores, l1_values=l1_values, l1_rows=l1_rows, l1_logits=l1_logits, l1_turn=l1_turn,
                         l1_output=l1_output, l2_transposes=l2_transposes, l2_project=l2_project, l2_maximum=l2_maximum,
                         l2_rows=l2_rows, l2_weights=l2_weights, l2_output=l2_output, l2_output_turn=l2_output_turn,
                         l2_close=l2_close, l3_transposes=l3_transposes, l3_scores=l3_scores, l3_values=l3_values,
                         l3_rows=l3_rows, l3_logits=l3_logits, l3_output=l3_output))

        @block.scalar
        def _(act):
            a_ = nc.scalar.activation
            for b, dst in ((0, w2T[:, 0:4, :]), (2, w2T[:, 8:12, :]), (4, w2T[:, 16:20, :]), (6, gateT[:, 4:8, :])):
                act.wait_ge(S["prep_ps"], b + 1)
                a_(dst, bank[b][:, :, :], ACT.Copy).then_inc(S["prep_a"], 1)
            act.wait_ge(S["late_d"], 1)
            for at in (SC1, SC2):
                a_(sc[:, at:at + 1], sc[:, at + 1:at + 2], ACT.Sqrt).then_inc(S["prep_a"], 1)
            act.wait_ge(S["late_d"], LATE_D)

            def l0_x(q):
                act.wait_ge(S["x0T_ps"], nth(q, 1, 1))
                if later(q):
                    act.wait_ge(S["d_r"], nth(q, 1, 0))
                    act.wait_ge(S["sT_r"], nth(q, 1, 0))
                a_(x0T[:, :, :], bA[:, :, :], ACT.Copy).then_inc(S["x0T_r"], 1)

            def l0_h1(q):
                act.wait_ge(S["h1_ps"], nth(q, 1, 1))
                a_(h1[:, :, PAD:PAD + 128], bA[:, :, :], ACT.Relu, bias=sc[:, SH1:SH1 + 1], scale=sc[:, SC1:SC1 + 1]).then_inc(S["h1_r"], 1)
                act.wait_ge(S["s_ps"], nth(q, 1, 1))
                if later(q):
                    act.wait_ge(S["sb_r"], nth(q, 2, 0))
                a_(sa[0:3, :, :], bB[0:3, :, :], ACT.Identity, bias=bse[0:3, :]).then_inc(S["sa_r"], 1)
                a_(sa[32:35, :, :], bB[32:35, :, :], ACT.Square, bias=bse[32:35, :]).then_inc(S["sa_r"], 1)

            def l0_exp(q):
                act.wait_ge(S["dist_ps"], nth(q, 1, 1))
                if later(q):
                    act.wait_ge(S["aT_r"], nth(q, 1, 0))
                a_(ea[:, :, :], bB[:, :, :], ACT.Exp).then_inc(S["ea_r"], 1)

            def l0_xn(q):
                act.wait_ge(S["xn_ps"], nth(q, 1, 1))
                a_(xnT[:, :, :], bA[:, :, :], ACT.Copy).then_inc(S["xn_r"], 1)

            def l0_xc(q):
                act.wait_ge(S["xcb_r"], nth(q, 1, 1))
                a_(xcT[:, :, :], xcb[:, :, :], ACT.Relu, bias=sc[:, SH2:SH2 + 1]).then_inc(S["xc_r"], 1)

            def l0_r(q):
                act.wait_ge(S["r_ps"], nth(q, 1, 1))
                if later(q):
                    act.wait_ge(S["r1_r"], nth(q, 1, 0))
                a_(rT[:, :, :], bA[:, :, :], ACT.Tanh, bias=sc[:, HBR:HBR + 1], scale=0.5).then_inc(S["r_r"], 1)

            def l0_z(q):
                act.wait_ge(S["z_ps"], nth(q, 1, 1))
                if later(q):
                    act.wait_ge(S["e_r"], nth(q, 1, 0))
                a_(zT[:, :, :], bC[:, :, :], ACT.Tanh, bias=sc[:, HBZ:HBZ + 1], scale=0.5).then_inc(S["z_r"], 1)

            def l0_n(q):
                act.wait_ge(S["u_r"], nth(q, 1, 1))
                a_(nT[:, :, :], uT[:, :, :], ACT.Tanh, bias=col[:, BIH + 2:BIH + 3]).then_inc(S["n_r"], 1)

            def l1_x(q):
                act.wait_ge(S["x1T_ps"], nth(q, 1, 1))
                a_(x1T[:, :, :], bD[:, :, :], ACT.Copy).then_inc(S["x1T_r"], 1)

            def l1_h(q):
                act.wait_ge(S["h1n_ps"], nth(q, 1, 1))
                a_(h1x[:, :, :, 0:D1], bD[:, :, :].rearrange("p g (h e) -> p g h e", h=H1), ACT.Copy).then_inc(S["h1x_r"], 1)

            def l1_rows(q):
                act.wait_ge(S["ejT_ps"], nth(q, 1, 1))
                a_(ejT[:, :, :], bD[:, :, :].rearrange("p g n -> p (g n)").bitcast(BF16)[0:3 * H1, 0:512].rearrange("p (g n) -> p g n", g=QUAD),
                   ACT.Copy).then_inc(S["ejT_r"], 1)

            def l1_exp(q, g):
                act.wait_ge(S["nm1_r"], nth(q, QUAD, g + 1))
                if g or later(q):
                    act.wait_ge(S["p1T_ps"], nth(q, QUAD, g))
                for h in range(H1):
                    last = a_(p1[:, h, :], zl[:, h, :], ACT.Exp, bias=nm1[:, h:h + 1])
                last.then_inc(S["p1_r"], 1)

            def l1_turned(q, g):
                act.wait_ge(S["p1T_ps"], nth(q, QUAD, g + 1))
                if g or later(q):
                    act.wait_ge(S["u1_ps"], nth(q, QUAD, g))
                a_(p1T[:, :, :], bD[:, :, :], ACT.Copy).then_inc(S["p1T_r"], 1)

            def l2_x(q):
                act.wait_ge(S["x2T_ps"], nth(q, 1, 1))
                a_(x2T[:, :, :], bH[:, :, :], ACT.Copy).then_inc(S["x2T_r"], 1)

            def l2_kv(q):
                act.wait_ge(S["k_ps"], nth(q, 1, 1))
                if later(q):
                    act.wait_ge(S["part2_r"], nth(q, 2, 0))
                    act.wait_ge(S["turn_w"], nth(q, 32, 0))
                a_(qf[:, 1, :, :], bG[:, :, :], ACT.Identity, bias=col[:, BK:BK + 1]).then_inc(S["kf_r"], 1)
                act.wait_ge(S["v_ps"], nth(q, 1, 1))
                if later(q):
                    act.wait_ge(S["v2_r"], nth(q, 1, 0))
                a_(v2n[:, :, :], bH[:, :, :], ACT.Copy).then_inc(S["v_r"], 1)

            def l2_fetch(q):
                act.wait_ge(S["x2c_r"], nth(q, 1, 1))
                if later(q):
                    act.wait_ge(S["y2_r"], nth(q, 1, 0))
                a_(x2d[:, :, :], x2c[:, :, :], ACT.Copy).then_inc(S["x2d_r"], 1)
                act.wait_ge(S["v_r"], nth(q, 1, 1))
                if later(q):
                    act.wait_ge(S["u2_ps"], nth(q, QUAD, 0))
                a_(v2x[:, :, :, 0:D2], v2n[:, :, :].rearrange("p g (h e) -> p g h e", h=H2), ACT.Copy).then_inc(S["v2_r"], 1)

            def l2_parts(q):
                for side, ready in ((0, "qf_r"), (1, "kf_r")):
                    act.wait_ge(S[ready], nth(q, 1, 1))
                    a_(pieces3[:, side, 0, :, :], qf[:, side, :, :], ACT.Copy).then_inc(S["part0_r"], 1)
                for side in range(2):
                    act.wait_ge(S["rest_r"], nth(q, 2, side + 1))
                    a_(pieces3[:, side, 1, :, :], rest[:, side, :, :], ACT.Copy).then_inc(S["part1_r"], 1)

            def l2_rows(q):
                act.wait_ge(S["nm2T_ps"], nth(q, 1, 1))
                if later(q):
                    act.wait_ge(S["nmturn_w"], nth(q, 16, 0))
                a_(nm2T[:, :], bH[:, :, :].rearrange("p g n -> p (g n)").bitcast(BF16)[0:3 * H2 * QUAD, 0:128], ACT.Copy).then_inc(S["nm2T_r"], 1)

            def l2_weights(q, g, i):
                act.wait_ge(S["w2_ps"], nth(q, 2 * QUAD, 2 * g + i + 1))
                if g or later(q):
                    act.wait_ge(S["u2_ps"], nth(q, QUAD, g))
                a_(p2T[:, i, :, :], (bF, bG)[i][:, :, :], ACT.Exp).then_inc(S["p2_r"], 1)

            def l2_output_turned(q, g):
                act.wait_ge(S["o2T_ps"], nth(q, QUAD, g + 1))
                a_(o2T[:, g, :], bH[:, g, :], ACT.Copy).then_inc(S["o2T_r"], 1)

            def l3_x(q):
                act.wait_ge(S["x3T_ps"], nth(q, 1, 1))
                a_(x3T[:, :, :], bI[:, :, :], ACT.Copy).then_inc(S["x3T_r"], 1)

            def l3_rows(q):
                act.wait_ge(S["s1T_ps"], nth(q, 1, 1))
                a_(s1T[:, :, :], bI[:, :, :].rearrange("p g n -> p (g n)").bitcast(BF16)[0:3, 0:512].rearrange("p (g n) -> p g n", g=QUAD),
                   ACT.Copy).then_inc(S["s1T_r"], 1)

            def l3_exp(q):
                act.wait_ge(S["z3_ps"], nth(q, 1, 1))
                act.wait_ge(S["e3_r"], nth(q, 1, 1))
                if later(q):
                    act.wait_ge(S["att3_r"], nth(q, 1, 0))
                for g in graphs:
                    last = a_(t3[:, g, :], bI[:, g, :], ACT.Exp, bias=s2n[:, g:g + 1], scale=-1.0)
                last.then_inc(S["t3_r"], 1)

            run(act, dict(l0_transposes=l0_x, l0_project=l0_h1, l0_distances=l0_exp, l0_nmp=l0_xn, l0_gate_r=lambda q: (l0_xc(q), l0_r(q)),
                          l0_gate_z=l0_z, l0_update=l0_n, l1_transposes=l1_x, l1_values=l1_h, l1_rows=l1_rows,
                          l1_turn=lambda q, g: (l1_exp(q, g), l1_turned(q, g)), l2_transposes=l2_x, l2_project=l2_kv, l2_fetch=l2_fetch,
                          l2_parts=l2_parts, l2_rows=l2_rows, l2_weights=l2_weights, l2_output_turn=l2_output_turned,
                          l3_transposes=l3_x, l3_rows=l3_rows, l3_logits=l3_exp))

        @block.vector
        def _(dve):
            v = nc.vector
            for b, dst in ((1, w2T[:, 4:8, :]), (3, w2T[:, 12:16, :]), (5, gateT[:, 0:4, :])):
                dve.wait_ge(S["prep_ps"], b + 1)
                v.tensor_copy(dst, bank[b][:, :, :]).then_inc(S["prep_d"], 1)
            dve.wait_ge(S["prep_ps"], 8)
            v.tensor_copy(gateT[:, 8, :], bI[:, 0, :]).then_inc(S["prep_d"], 1)
            v.tensor_copy(nodeT[:, :], bI[:, 1, 0:GRAPHS]).then_inc(S["prep_d"], 1)
            dve.wait_ge(S["pool_c"], POOL_C)
            for at in (0, 32):
                last = v.tensor_copy(wseT[:, at:at + 3], bI[:, 2, 0:3])
            last.then_inc(S["prep_d"], 1)
            v.tensor_copy(col[:, :], bI[:, 3, 0:VECTORS]).then_inc(S["prep_d"], 1)
            dve.wait_ge(S["prep_d"], 7)
            for at, src in ((SH1, BN1V), (SH2, BN2V)):
                last = v.tensor_scalar(sc[:, at:at + 1], col[:, src:src + 1], EPS, None, ALU.add)
            last.then_inc(S["late_d"], 1)
            v.tensor_copy(spread[:, 0, :], col[:, BV:BV + 1].to_broadcast([128, 128]))
            v.tensor_copy(spread[:, 1, :], col[:, B3:B3 + 1].to_broadcast([128, 128])).then_inc(S["late_d"], 1)
            dve.wait_ge(S["prep_a"], 6)
            n = [7]

            def chain(ins_):
                n[0] += 1
                ins_.then_inc(S["prep_d"], 1)
                dve.wait_ge(S["prep_d"], n[0])

            for g_at, b_at, m_at, scale, shift in ((BN1G, BN1B, BN1M, SC1, SH1), (BN2G, BN2B, BN2M, SC2, SH2)):
                c = lambda tile, at: tile[:, at:at + 1]
                chain(v.reciprocal(c(sc, TMP), c(sc, scale)))
                chain(v.tensor_tensor(c(sc, scale), c(sc, TMP), c(col, g_at), ALU.mult))
                chain(v.tensor_tensor(c(sc, TMP), c(sc, scale), c(col, m_at), ALU.mult))
                chain(v.tensor_tensor(c(sc, shift), c(col, b_at), c(sc, TMP), ALU.subtract))
            chain(v.tensor_tensor(sc[:, TMP:TMP + 2], col[:, BIH:BIH + 2], col[:, BHH:BHH + 2], ALU.add))
            chain(v.tensor_scalar(sc[:, HBR:HBR + 2], sc[:, TMP:TMP + 2], 0.5, None, ALU.mult))
            dve.wait_ge(S["late_in"], 16 * 9)
            w1h = w1[:, :].rearrange("p (h e) -> p h e", h=H1)
            for i in range(2):
                chain(v.tensor_tensor(aprod[:, H1 * i:H1 * i + H1, :], w1h, abc[:, :, D1 * i:D1 * i + D1], ALU.mult))
            chain(v.tensor_reduce(wa[:, :], aprod[:, :, :], AX.X, ALU.add))
            dve.wait_ge(S["late_ps"], 1)
            v.tensor_copy(w3a[:, :], bA[:, 0, 0:2]).then_inc(S["late_d"], 1)
            chain(v.tensor_copy(sc[:, 8:10], bA[:, 1, 0:2]))
            chain(v.tensor_tensor(sc[:, 10:11], sc[:, 8:9], sc[:, 9:10], ALU.add))
            chain(v.tensor_tensor(sc[:, 11:12], sc[:, 10:11], attb[:, :], ALU.add))
            v.tensor_scalar(nc3[:, :], sc[:, 11:12], -1.0, None, ALU.mult).then_inc(S["late_d"], 1)
            v.tensor_tensor(cbc[:, :], bA[:, 2, :], bcast[:, 1, :], ALU.add).then_inc(S["late_d"], 1)
            dve.wait_ge(S["late_d"], LATE_D)

            def norm_stats(i, q, src):
                if later(q):
                    dve.wait_ge(rstd_r[i], nth(q, 1, 0))
                for g in graphs:
                    last = v.bn_stats(stats[i][:, g, :], src[:, g, :])
                last.then_inc(st_r[i], 1)
                dve.wait_ge(st_r[i], nth(q, 1, 1))
                mean_e, m2_e, mean_o, m2_o = (stats[i][:, :, c] for c in (1, 2, 4, 5))
                v.tensor_tensor(mom[i][:, 0, :], mean_e, mean_o, ALU.add)
                v.tensor_tensor(mom[i][:, 1, :], mean_e, mean_o, ALU.subtract)
                v.tensor_tensor(mom[i][:, 2, :], m2_e, m2_o, ALU.add).then_inc(mv_r[i], 1)
                dve.wait_ge(mv_r[i], nth(q, 2, 1))
                v.tensor_scalar(mv[i][:, 0, :], mom[i][:, 0, :], 0.5, None, ALU.mult)
                v.tensor_tensor(mv[i][:, 1, :], mom[i][:, 1, :], mom[i][:, 1, :], ALU.mult)
                v.tensor_scalar(mv[i][:, 2, :], mom[i][:, 2, :], 1.0 / D, EPS, ALU.mult, ALU.add).then_inc(mv_r[i], 1)
                dve.wait_ge(mv_r[i], nth(q, 2, 2))
                v.scalar_tensor_tensor(ve[i][:, :], mv[i][:, 1, :], 0.25, mv[i][:, 2, :], ALU.mult, ALU.add).then_inc(ve_r[i], 1)

            def norm_apply(i, q, dst, src, done):
                dve.wait_ge(rstd_r[i], nth(q, 1, 1))
                for g in graphs:
                    last = v.tensor_scalar(dst[:, g, :], src[:, g, :], mv[i][:, 0, g:g + 1], rstd[i][:, g:g + 1], ALU.subtract, ALU.mult)
                    if done != S["res_r"]:
                        last.then_inc(done, 1)
                if done == S["res_r"]:
                    last.then_inc(done, 1)

            def split3(dst, src, rest, first, last_sem, q):
                v.tensor_copy(dst[0], src).then_inc(first, 1)
                dve.wait_ge(first, nth(q, 3, 1))
                v.tensor_tensor(rest, src, dst[0], ALU.subtract).then_inc(first, 1)
                dve.wait_ge(first, nth(q, 3, 2))
                v.tensor_copy(dst[1], rest).then_inc(first, 1)
                dve.wait_ge(first, nth(q, 3, 3))
                v.tensor_tensor(dst[2], rest, dst[1], ALU.subtract).then_inc(last_sem, 1)

            def l0_adj(q):
                dve.wait_ge(S["adj0T_ps"], nth(q, 1, 1))
                v.tensor_copy(adjT[:, bass.ds(q * QUAD, QUAD), :], bB[:, :, :]).then_inc(S["adj0T_r"], 1)

            def l0_s(q):
                dve.wait_ge(S["sa_r"], nth(q, 2, 2))
                v.tensor_scalar(sbm[0:3, :, :], sa[0:3, :, :], 2.0, None, ALU.mult).then_inc(S["sb_r"], 1)
                v.tensor_scalar(sbm[64:67, :, :], sa[32:35, :, :], -1.0, None, ALU.mult).then_inc(S["sb_r"], 1)

            def l0_msg(q):
                dve.wait_ge(S["msg_ps"], nth(q, 1, 1))
                v.tensor_tensor(msgb[:, :, :], bA[:, :, :], bcast[:, 0:1, :].to_broadcast([128, QUAD, 128]), ALU.add).then_inc(S["msgb_r"], 1)
                dve.wait_ge(S["msgb_r"], nth(q, 1, 1))
                v.tensor_scalar(msg[:, :, :], msgb[:, :, :], 0.0, None, ALU.max).then_inc(S["msg_r"], 1)

            def l0_xc(q):
                dve.wait_ge(S["c2_ps"], nth(q, 1, 1))
                v.scalar_tensor_tensor(xcb[:, :, :], bC[:, :, :], sc[:, SC2:SC2 + 1], x0T[:, :, :], ALU.mult, ALU.add).then_inc(S["xcb_r"], 1)

            def l0_r1(q):
                dve.wait_ge(S["r_r"], nth(q, 1, 1))
                v.tensor_scalar(r1T[:, :, :], rT[:, :, :], 1.0, None, ALU.add).then_inc(S["r1_r"], 1)
                dve.wait_ge(S["r1_r"], nth(q, 1, 1))
                dve.wait_ge(S["ghn_ps"], nth(q, 1, 1))
                v.scalar_tensor_tensor(tT[:, :, :], bB[:, :, :], col[:, BHH + 2:BHH + 3], r1T[:, :, :], ALU.add, ALU.mult).then_inc(S["t_r"], 1)

            def l0_u(q):
                dve.wait_ge(S["t_r"], nth(q, 1, 1))
                dve.wait_ge(S["gin_ps"], nth(q, 1, 1))
                v.scalar_tensor_tensor(uT[:, :, :], tT[:, :, :], 0.5, bA[:, :, :], ALU.mult, ALU.add).then_inc(S["u_r"], 1)

            def l0_y(q):
                dve.wait_ge(S["n_r"], nth(q, 1, 1))
                v.tensor_tensor(dT[:, :, :], x0T[:, :, :], nT[:, :, :], ALU.subtract).then_inc(S["d_r"], 1)
                v.tensor_tensor(sT[:, :, :], x0T[:, :, :], nT[:, :, :], ALU.add).then_inc(S["sT_r"], 1)
                dve.wait_ge(S["d_r"], nth(q, 1, 1))
                dve.wait_ge(S["z_r"], nth(q, 1, 1))
                v.scalar_tensor_tensor(eT[:, :, :], zT[:, :, :], 1.0, dT[:, :, :], ALU.add, ALU.mult).then_inc(S["e_r"], 1)
                dve.wait_ge(S["e_r"], nth(q, 1, 1))
                v.scalar_tensor_tensor(yT[:, :, :], eT[:, :, :], 0.5, sT[:, :, :], ALU.mult, ALU.add).then_inc(S["y0_r"], 1)

            def bias_of(dst, src, loaded, used, done, q):
                dve.wait_ge(S[loaded], nth(q, 16, 16))
                if later(q):
                    dve.wait_ge(S[used[0]], nth(q, used[1], 0))
                v.tensor_scalar(dst[:, :, :], src[:, :, :], 0.0, NEG, ALU.is_le, ALU.mult).then_inc(S[done], 1)

            def l1_scores(q):
                dve.wait_ge(S["e1_ps"], nth(q, 1, 1))
                v.tensor_copy(e1[:, :, :], bD[:, 0, 0:8 * QUAD].rearrange("p (g c) -> p g c", g=QUAD)).then_inc(S["e1_r"], 1)
                dve.wait_ge(S["e1_r"], nth(q, 1, 1))
                split3([ej3[:, :, :, i] for i in range(3)], e1[:, :, H1:2 * H1], ejr[:, :, :], S["ejs_r"], S["ej3_r"], q)

            def l1_logits(q, g):
                dve.wait_ge(S["z1_ps"], nth(q, QUAD, g + 1))
                v.tensor_tensor(zi[:, :, :], bD[:, :, :], e1[:, g, 0:H1].unsqueeze(2).to_broadcast([128, H1, 128]), ALU.add).then_inc(S["zi_r"], 1)
                dve.wait_ge(S["zi_r"], nth(q, QUAD, g + 1))
                if g or later(q):
                    dve.wait_ge(S["p1_r"], nth(q, QUAD, g))
                v.scalar_tensor_tensor(zl[:, :, :], zi[:, :, :], SLOPE, zi[:, :, :], ALU.mult, ALU.max).then_inc(S["zl_r"], 1)
                dve.wait_ge(S["zl_r"], nth(q, QUAD, g + 1))
                v.tensor_reduce(nm1[:, :], zl[:, :, :], AX.X, ALU.max, negate=True).then_inc(S["nm1_r"], 1)

            def l1_output(q, g):
                dve.wait_ge(S["u1_ps"], nth(q, QUAD, g + 1))
                v.reciprocal(rc1[:, :], bD[:, :, D1]).then_inc(S["rc1_r"], 1)
                dve.wait_ge(S["rc1_r"], nth(q, QUAD, g + 1))
                v.tensor_tensor(o1[:, :, :], bD[:, :, 0:D1], rc1[:, :].unsqueeze(2).to_broadcast([128, H1, D1]), ALU.mult).then_inc(S["o1_r"], 1)
                dve.wait_ge(S["o1_r"], nth(q, QUAD, g + 1))
                v.tensor_tensor(y1[:, g, :], o1[:, :, :].rearrange("p h e -> p (h e)"), x1[:, g, :], ALU.add).then_inc(S["y1_r"], 1)

            def l2_q(q):
                dve.wait_ge(S["q_ps"], nth(q, 1, 1))
                if later(q):
                    dve.wait_ge(S["part2_r"], nth(q, 2, 0))
                v.tensor_scalar(qf[:, 0, :, :], bF[:, :, :], col[:, BQ:BQ + 1], float(D2) ** -0.5, ALU.add, ALU.mult).then_inc(S["qf_r"], 1)

            def l2_maximum(q, job):
                g, i = divmod(job, 2)
                dve.wait_ge(S["s2_ps"], nth(q, 2 * QUAD, job + 1))
                v.tensor_reduce(nm2[:, 4 * i:4 * i + 4, g], (bF, bG)[i][:, :, :], AX.X, ALU.max, negate=True).then_inc(S["nm2_r"], 1)

            def l2_rows(q):
                dve.wait_ge(S["nm2_r"], nth(q, 2 * QUAD, 2 * QUAD))
                split3([nm23[:, i, :, :] for i in range(3)], nm2[:, :, :], nm2r[:, :, :], S["nms_r"], S["nm23_r"], q)

            uv = bH[:, :, :].rearrange("p g n -> p (g n)")[:, 0:H2 * (D2 + 1)].rearrange("p (h e) -> p h e", h=H2)

            def l2_output(q, g):
                dve.wait_ge(S["u2_ps"], nth(q, QUAD, g + 1))
                v.reciprocal(rc2[:, :], uv[:, :, D2]).then_inc(S["rc2_r"], 1)
                dve.wait_ge(S["rc2_r"], nth(q, QUAD, g + 1))
                v.tensor_tensor(o2[:, :, :], uv[:, :, 0:D2], rc2[:, :].unsqueeze(2).to_broadcast([128, H2, D2]), ALU.mult).then_inc(S["o2_r"], 1)

            def l2_close(q):
                dve.wait_ge(S["wo_ps"], nth(q, 1, 1))
                dve.wait_ge(S["x2d_r"], nth(q, 1, 1))
                v.tensor_tensor(y2[:, :, :], bH[:, :, :], x2d[:, :, :], ALU.add).then_inc(S["y2_r"], 1)
                dve.wait_ge(S["y2_r"], nth(q, 1, 1))

            def l3_masks(q):
                if later(q):
                    dve.wait_ge(S["h3x_r"], nth(q, 2, 0))
                v.tensor_copy(mk[:, :], nodeT[:, bass.ds(q * QUAD, QUAD)]).then_inc(S["mk_r"], 1)
                dve.wait_ge(S["mk_r"], nth(q, 1, 1))
                v.tensor_tensor(mk2[:, :], mk[:, :], mk[:, :], ALU.mult).then_inc(S["mks_r"], 1)

            def l3_scores(q):
                dve.wait_ge(S["e3_ps"], nth(q, 1, 1))
                if later(q):
                    dve.wait_ge(S["t3_r"], nth(q, 1, 0))
                e = bI[:, 0, 0:2 * QUAD].rearrange("p (g c) -> p g c", g=QUAD)
                v.tensor_scalar(s2n[:, :], e[:, :, 1], -1.0, nc3[:, :], ALU.mult, ALU.add)
                v.tensor_copy(e3[:, :, :], e).then_inc(S["e3_r"], 1)
                dve.wait_ge(S["e3_r"], nth(q, 1, 1))
                split3([s13[:, :, i] for i in range(3)], e3[:, :, 0], s1r[:, :], S["s1s_r"], S["s13_r"], q)

            def l3_values(q):
                dve.wait_ge(S["h3_ps"], nth(q, 1, 1))
                if later(q):
                    dve.wait_ge(S["h3x_r"], nth(q, 2, 0))
                v.tensor_tensor(hb3[:, :, :], bI[:, :, :], bcast[:, 2:3, :].to_broadcast([128, QUAD, 128]), ALU.add).then_inc(S["hb3_r"], 1)

            def l3_att(q):
                dve.wait_ge(S["t3_r"], nth(q, 1, 1))
                v.tensor_scalar(d3[:, :, :], t3[:, :, :], 1.0, BIG, ALU.add, ALU.min).then_inc(S["d3_r"], 1)
                dve.wait_ge(S["d3_r"], nth(q, 2, 1))
                v.reciprocal(r3[:, :, :], d3[:, :, :]).then_inc(S["d3_r"], 1)
                dve.wait_ge(S["d3_r"], nth(q, 2, 2))
                v.tensor_tensor(att3[:, :, :], r3[:, :, :], adjT[:, bass.ds(q * QUAD, QUAD), :], ALU.mult).then_inc(S["att3_r"], 1)

            u3 = bI[:, :, :].rearrange("p g n -> p (g n)")[:, 0:2 * 129].rearrange("p (g e) -> p g e", g=2)

            def l3_output(q, pair):
                at = slice(2 * pair, 2 * pair + 2)
                k = 4 * pair
                dve.wait_ge(S["u3_ps"], nth(q, 2, pair + 1))
                v.tensor_tensor(den3[:, :, 0], u3[:, :, 128], mk[:, at], ALU.mult).then_inc(S["f3_r"], 1)
                dve.wait_ge(S["f3_r"], nth(q, 8, k + 1))
                v.tensor_scalar(den3[:, :, 1], den3[:, :, 0], TINY, None, ALU.add).then_inc(S["f3_r"], 1)
                dve.wait_ge(S["f3_r"], nth(q, 8, k + 2))
                v.reciprocal(den3[:, :, 2], den3[:, :, 1]).then_inc(S["f3_r"], 1)
                dve.wait_ge(S["f3_r"], nth(q, 8, k + 3))
                v.tensor_tensor(den3[:, :, 3], den3[:, :, 2], mk2[:, at], ALU.mult).then_inc(S["f3_r"], 1)
                dve.wait_ge(S["f3_r"], nth(q, 8, k + 4))
                for g in range(2):
                    v.scalar_tensor_tensor(y3[:, 2 * pair + g, :], u3[:, g, 0:128], den3[:, g, 3:4], x3[:, 2 * pair + g, :],
                                           ALU.mult, ALU.add).then_inc(S["y3_r"], 1)

            def l3_close(q):
                dve.wait_ge(S["y3_r"], nth(q, QUAD, QUAD))
                norm_stats(3, q, y3)
                if later(q):
                    dve.wait_ge(S["out_w"], nth(q, 16, 0))
                norm_apply(3, q, res, y3, S["res_r"])

            def l1_norm(q):
                dve.wait_ge(S["y1_r"], nth(q, QUAD, QUAD))
                norm_stats(1, q, y1)

            def l0_close(q):
                dve.wait_ge(S["y0T_ps"], nth(q, 1, 1))
                norm_stats(0, q, bC)

            def l2_close_(q):
                l2_close(q)
                norm_stats(2, q, y2)

            run(dve, dict(
                l0_transposes=l0_adj, l1_norm=l1_norm, l2_output=l2_output, l0_project=l0_s, l2_close=l2_close_,
                l2_fetch=lambda q: bias_of(mb2, adj2, "adj2_in", ("w2_ps", 2 * QUAD), "mb2_r", q),
                l0_messages=l0_msg, l0_close=l0_close,
                l2_transposes=lambda q: norm_apply(1, q, x2, y1, S["x2_r"]),
                l2_project=l2_q, l3_transposes=lambda q: (norm_apply(2, q, x3, y2, S["x3_r"]), l3_masks(q)),
                l0_apply=lambda q: norm_apply(0, q, x1, bC, S["x1_r"]),
                l1_transposes=lambda q: bias_of(mb1, adj1, "adj1_in", ("z1_ps", QUAD), "mb1_r", q),
                l3_scores=l3_scores, l2_maximum=l2_maximum, l1_scores=l1_scores, l3_values=l3_values,
                l1_logits=l1_logits, l1_output=l1_output, l2_rows=l2_rows, l3_weights=l3_att, l3_output=l3_output,
                l3_close=l3_close, l0_gate_r=l0_xc, l0_gate_z=l0_r1, l0_update=lambda q: (l0_u(q), l0_y(q))))


def kernel(**inputs):
    import numpy as np
    import concourse.bacc as bacc
    from concourse.bass_utils import run_bass_kernel_spmd

    nc = bacc.Bacc("TRN2", target_bir_lowering=False, num_devices=1)
    arrays, ins = {}, {}
    for name in INS:
        a = np.ascontiguousarray(inputs[name])
        if a.ndim == 0:
            a = a.reshape(1)
        arrays["in_" + name] = a
        ins[name] = nc.dram_tensor("in_" + name, a.shape, mybir.dt.from_np(a.dtype), kind="ExternalInput").ap()
    out = nc.dram_tensor("out_0", (GRAPHS, N, D), F32, kind="ExternalOutput").ap()
    build(nc, ins, out)
    r = run_bass_kernel_spmd(nc, [arrays], core_ids=[0])
    return r.results[0]["out_0"]
```

```python
from contextlib import ExitStack

import concourse.bass as bass
from concourse import mybir

F32 = mybir.dt.float32
BF16 = mybir.dt.bfloat16
ACT = mybir.ActivationFunctionType
ALU = mybir.AluOpType
AX = mybir.AxisListType

GRAPHS, N, D = 64, 128, 128
QUAD = 4
QUADS = GRAPHS // QUAD
TAPS = 17
PAD = TAPS // 2
PAIRS = TAPS // 2
HALF = N // 2
H1 = 4
D1 = D // H1
H2 = 8
D2 = D // H2
EPS = 1e-5
TINY = 1e-8
BIG = 3.0e38
NEG = -9.0e15
SLOPE = 0.2
LAYERS = 4
Q_PARTS = (0, 0, 1, 1, 0, 2, 1)
K_PARTS = (0, 1, 0, 1, 2, 0, 2)
SLOTS = len(Q_PARTS)
STACK = SLOTS * D2

ORDERS = {
    "PE": [
        ("l0_conv", 2, 13), ("l2_output", 5, 1), ("l1_logits", 3, 2), ("l2_weights", 5, 3, 1), ("l0_conv", 2, 14),
        ("l2_output_turn", 5, 1), ("l0_conv", 2, 15), ("l0_conv", 2, 16), ("l2_output", 5, 2), ("l1_turn", 3, 2),
        ("l0_gate_hn", 2), ("l2_output_turn", 5, 2), ("l1_output", 3, 2), ("l0_gate_r", 2), ("l1_logits", 3, 3),
        ("l0_gate_z", 2), ("l0_gate_n", 2), ("l2_output", 5, 3), ("l0_transposes", 1), ("l2_output_turn", 5, 3),
        ("l1_turn", 3, 3), ("l1_output", 3, 3), ("l0_project", 1), ("l2_close", 5), ("l0_close", 2),
        ("l0_messages", 1), ("l0_distances", 1), ("l2_transposes", 3), ("l0_sum", 1, 0), ("l0_sum", 1, 1),
        ("l0_sum", 1, 2), ("l0_sum", 1, 3), ("l2_project", 3), ("l2_maximum", 4, 0), ("l2_maximum", 4, 1),
        ("l1_transposes", 2), ("l0_sum", 1, 4), ("l0_sum", 1, 5), ("l3_transposes", 5), ("l2_maximum", 4, 2),
        ("l2_maximum", 4, 3), ("l3_scores", 5), ("l1_scores", 2), ("l2_maximum", 4, 4), ("l2_maximum", 4, 5),
        ("l3_values", 5), ("l1_values", 2), ("l0_sum", 1, 6), ("l0_conv", 1, 0), ("l2_maximum", 4, 6),
        ("l2_maximum", 4, 7), ("l1_rows", 2), ("l3_rows", 5), ("l0_nmp", 1), ("l1_logits", 2, 0), ("l0_conv", 1, 1),
        ("l0_sum", 1, 7), ("l2_rows", 4), ("l3_logits", 5), ("l0_conv", 1, 2), ("l0_conv", 1, 3), ("l0_conv", 1, 4),
        ("l0_conv", 1, 5), ("l0_conv", 1, 6), ("l0_conv", 1, 7), ("l0_conv", 1, 8), ("l1_turn", 2, 0),
        ("l0_conv", 1, 9), ("l0_conv", 1, 10), ("l1_output", 2, 0), ("l0_conv", 1, 11), ("l2_weights", 4, 0, 0),
        ("l2_weights", 4, 0, 1), ("l3_output", 5, 0), ("l1_logits", 2, 1), ("l0_sum", 1, 8), ("l2_weights", 4, 1, 0),
        ("l2_weights", 4, 1, 1), ("l2_output", 4, 0), ("l2_weights", 4, 2, 0), ("l2_weights", 4, 2, 1),
        ("l1_turn", 2, 1), ("l2_output_turn", 4, 0), ("l0_conv", 1, 12), ("l2_weights", 4, 3, 0), ("l3_output", 5, 1),
        ("l1_output", 2, 1),
    ],
    "DVE": [
        ("l2_maximum", 4, 3), ("l3_scores", 5), ("l1_scores", 2), ("l2_maximum", 4, 4), ("l2_maximum", 4, 5),
        ("l3_values", 5), ("l0_messages", 1), ("l2_maximum", 4, 6), ("l2_maximum", 4, 7), ("l2_rows", 4),
        ("l1_logits", 2, 0), ("l3_weights", 5, 0), ("l3_weights", 5, 1), ("l1_output", 2, 0), ("l1_logits", 2, 1),
        ("l3_output", 5, 0), ("l2_output", 4, 0), ("l3_output", 5, 1), ("l1_output", 2, 1), ("l2_output", 4, 1),
        ("l1_logits", 2, 2), ("l0_mix", 1), ("l0_gate_r", 1), ("l2_output", 4, 2), ("l3_norm", 5),
        ("l1_output", 2, 2), ("l2_fetch", 3), ("l3_close", 5), ("l1_logits", 2, 3), ("l0_gate_z", 1), ("l0_u", 1),
        ("l2_output", 4, 3), ("l0_update", 1), ("l0_transposes", 0), ("l1_output", 2, 3), ("l1_norm", 2),
        ("l0_project", 0), ("l2_close", 4), ("l2_transposes", 2), ("l0_close", 1), ("l2_norm", 4), ("l2_project", 2),
        ("l0_apply", 1), ("l3_transposes", 4), ("l2_maximum", 3, 0), ("l2_maximum", 3, 1), ("l1_transposes", 1),
        ("l2_maximum", 3, 2),
    ],
    "Activation": [
        ("l1_turn", 3, 3), ("l0_transposes", 1), ("l0_project", 1), ("l0_s", 1), ("l0_distances", 1), ("l2_fetch", 4),
        ("l2_transposes", 3), ("l2_project", 3), ("l2_v", 3), ("l2_parts", 3), ("l3_transposes", 5),
        ("l1_transposes", 2), ("l2_round", 3), ("l1_values", 2), ("l1_rows", 2), ("l3_rows", 5), ("l2_rows", 4),
        ("l3_logits", 5), ("l1_exp", 2, 0), ("l1_turn", 2, 0), ("l2_weights", 4, 0, 0), ("l2_weights", 4, 0, 1),
        ("l2_weights", 4, 1, 0), ("l2_weights", 4, 1, 1), ("l1_exp", 2, 1), ("l2_weights", 4, 2, 0),
        ("l1_turn", 2, 1), ("l2_output_turn", 4, 0), ("l2_weights", 4, 2, 1), ("l2_output_turn", 4, 1),
        ("l1_exp", 2, 2), ("l0_nmp", 1), ("l1_turn", 2, 2), ("l0_xc", 1), ("l0_gate_r", 1), ("l2_weights", 4, 3, 0),
        ("l2_output_turn", 4, 2), ("l2_weights", 4, 3, 1), ("l1_exp", 2, 3), ("l0_gate_z", 1), ("l0_update", 1),
        ("l2_output_turn", 4, 3),
    ],
    "Pool": [
        ("l2_transposes", 3), ("l2_parts", 3), ("l2_round", 3), ("l3_values", 5), ("l3_norm", 5), ("l1_norm", 2),
        ("l0_close", 1), ("l2_norm", 4), ("l0_messages", 0), ("l0_distances", 0),
    ],
    "SP": [
        ("l1_transposes", 2), ("l0_transposes", 0), ("l2_parts", 3), ("l2_rows", 4), ("l2_fetch", 3), ("l3_close", 5),
    ],
}
DEPTH = 1 + max(piece[1] for pieces in ORDERS.values() for piece in pieces)


INS = ["x", "adj", "nodemask", "L0_gnn_w_se", "L0_gnn_b_se", "L0_gnn_conv1_w", "L0_gnn_bn1_g", "L0_gnn_bn1_b",
       "L0_gnn_bn1_m", "L0_gnn_bn1_v", "L0_gnn_conv2_w", "L0_gnn_bn2_g", "L0_gnn_bn2_b", "L0_gnn_bn2_m",
       "L0_gnn_bn2_v", "L0_gnn_w_msg", "L0_gnn_b_msg", "L0_gnn_w_ih", "L0_gnn_b_ih", "L0_gnn_w_hh", "L0_gnn_b_hh",
       "L1_gnn_W", "L1_gnn_a", "L2_gnn_Wq", "L2_gnn_bq", "L2_gnn_Wk", "L2_gnn_bk", "L2_gnn_Wv", "L2_gnn_bv",
       "L2_gnn_Wo", "L2_gnn_bo", "L3_gnn_W", "L3_gnn_b", "L3_gnn_a1", "L3_gnn_a2", "L3_gnn_att_b"]


def nth(q, per, k):
    return q * per + k


def later(q):
    return not isinstance(q, int) or q > 0


def build(nc, ins, out):
    with ExitStack() as ctx:
        def sb(name, shape, dt=F32):
            return ctx.enter_context(nc.sbuf_tensor(name, shape, dt))

        def sem(name):
            return ctx.enter_context(nc.semaphore(name))

        bank = [ctx.enter_context(nc.psum_tensor(f"bank{c}", [128, QUAD, 128], F32)) for c in "ABCDFGHI"]
        bA, bB, bC, bD, bF, bG, bH, bI = bank

        ident = sb("ident", [128, 128])
        ident16 = sb("ident16", [128, 128], BF16)
        w2raw = sb("w2raw", [128, D, TAPS])
        wihraw = sb("wihraw", [128, 3, 2, 128])
        whhraw = sb("whhraw", [128, 3, 128])
        raw = sb("raw", [128, 3, 128])
        wseraw = sb("wseraw", [3, 128])
        maskraw = sb("maskraw", [GRAPHS, N])
        w2T = sb("w2T", [128, 20, 128])
        tap2T = sb("tap2T", [128, PAIRS, 128])
        gateT = sb("gateT", [128, 9, 128])
        wseT = sb("wseT", [128, 35])
        nodeT = sb("nodeT", [128, GRAPHS])
        rows = sb("rows", [20, 128])
        col = sb("col", [128, 20])
        BN1G, BN1B, BN1M, BN1V, BN2G, BN2B, BN2M, BN2V, BIH, BHH, BQ, BK, BV, B3, A1, A2 = 0, 1, 2, 3, 4, 5, 6, 7, 8, 11, 14, 15, 16, 17, 18, 19
        VECTORS = 20
        bse = sb("bse", [35, 1])
        sc = sb("sc", [128, 16])
        SC1, SH1, SC2, SH2, HBR, HBZ, TMP = 0, 1, 2, 3, 4, 5, 6
        wa = sb("wa", [128, 2 * H1])
        w1 = sb("w1", [128, 128])
        abc = sb("abc", [128, H1, 2 * D1])
        aprod = sb("aprod", [128, 2 * H1, D1])
        wq = sb("wq", [128, 128])
        wk = sb("wk", [128, 128])
        wv = sb("wv", [128, 128])
        wo = sb("wo", [128, 128])
        bcast = sb("bcast", [128, 3, 128])
        cbc = sb("cbc", [128, 128])
        spread = sb("spread", [128, 2, 128])
        a12 = col[:, A1:A2 + 1]
        w3a = sb("w3a", [128, 2])
        attb = sb("attb", [128, 1])
        nc3 = sb("nc3", [128, 1])
        sel1 = sb("sel1", [3 * H1, H1, 128], BF16)
        ones3 = sb("ones3", [3, 128], BF16)
        half = sb("half", [128, QUAD])

        x0 = sb("x0", [128, QUAD, 128])
        adj0 = sb("adj0", [128, QUAD, 128])
        x0T = sb("x0T", [128, QUAD, 128])
        adjT = sb("adjT", [128, GRAPHS, 128])
        h1 = sb("h1", [128, 2, QUAD, HALF + PAD])
        hd = wihraw[:, :, :, :].rearrange("p c b i -> p (c b i)")[:, 0:2 * QUAD * (HALF + PAD)].rearrange("p (s g n) -> p s g n", s=2, g=QUAD)
        sa = sb("sa", [67, QUAD, 128])
        sbm = sb("sbm", [67, QUAD, 128])
        msgb = sb("msgb", [128, QUAD, 128])
        msg = sb("msg", [128, QUAD, 128])
        ea = sb("ea", [128, QUAD, 128])
        aT = sb("aT", [128, QUAD, 128])
        xnT = sb("xnT", [128, QUAD, 128])
        xcb = sb("xcb", [128, QUAD, 128])
        xcT = sb("xcT", [128, QUAD, 128])
        rT = sb("rT", [128, QUAD, 128])
        zT = sb("zT", [128, QUAD, 128])
        r1T = sb("r1T", [128, QUAD, 128])
        tT = sb("tT", [128, QUAD, 128])
        uT = sb("uT", [128, QUAD, 128])
        nT = sb("nT", [128, QUAD, 128])
        dT, sT, eT = uT, r1T, tT
        yT = sb("yT", [128, QUAD, 128])
        stats = [sb(f"stats{i}", [128, QUAD, 6]) for i in range(LAYERS)]
        mom = [sb(f"mom{i}", [128, 3, QUAD]) for i in range(LAYERS)]
        mv = [sb(f"mv{i}", [128, 3, QUAD]) for i in range(LAYERS)]
        ve = [sb(f"ve{i}", [128, QUAD]) for i in range(LAYERS)]
        rstd = [sb(f"rstd{i}", [128, QUAD]) for i in range(LAYERS)]
        x1 = sb("x1", [128, QUAD, 128])
        adj1 = sb("adj1", [128, QUAD, 128])
        x1T = sb("x1T", [128, QUAD, 128])
        mb1 = sb("mb1", [128, QUAD, 128], BF16)
        e1 = sb("e1", [128, QUAD, 2 * H1])
        ej3 = sb("ej3", [128, QUAD, H1, 3], BF16)
        ejr = sb("ejr", [128, QUAD, H1])
        ejT = sb("ejT", [3 * H1, QUAD, 128], BF16)
        h1x = sb("h1x", [128, QUAD, H1, D1 + 1])
        zi = sb("zi", [128, H1, 128])
        zl = sb("zl", [128, H1, 128])
        nm1 = sb("nm1", [128, H1])
        p1 = sb("p1", [128, H1, 128])
        p1T = sb("p1T", [128, H1, 128])
        rc1 = sb("rc1", [128, H1])
        o1 = sb("o1", [128, H1, D1])
        y1 = sb("y1", [128, QUAD, 128])
        x2 = sb("x2", [128, QUAD, 128])
        x2c = sb("x2c", [128, QUAD, 128])
        adj2 = sb("adj2", [128, QUAD, 128])
        x2T = sb("x2T", [128, QUAD, 128])
        mb2 = sb("mb2", [128, QUAD, 128], BF16)
        qf = sb("qf", [128, 2, QUAD, 128])
        pieces3 = sb("pieces3", [128, 2, 3, QUAD, 128], BF16)
        rest = sb("rest", [128, 2, QUAD, 128])
        qst = sb("qst", [STACK + 3, H2, QUAD, 128], BF16)
        kst = sb("kst", [STACK + 3, H2, QUAD, 128], BF16)
        v2n = sb("v2n", [128, QUAD, 128])
        v2x = sb("v2x", [128, QUAD, H2, D2 + 1])
        x2d = sb("x2d", [128, QUAD, 128])
        nm2 = sb("nm2", [128, H2, QUAD])
        nm2r = sb("nm2r", [128, H2, QUAD])
        nm23 = sb("nm23", [128, 3, H2, QUAD], BF16)
        nm2T = sb("nm2T", [3 * H2 * QUAD, 128], BF16)
        p2T_even = sb("p2T_even", [128, 2, 4, 128])
        rc2 = sb("rc2", [128, H2])
        o2 = sb("o2", [128, H2, D2])
        o2T = sb("o2T", [128, QUAD, 128])
        y2 = sb("y2", [128, QUAD, 128])
        x3 = sb("x3", [128, QUAD, 128])
        x3T = sb("x3T", [128, QUAD, 128])
        e3 = sb("e3", [128, QUAD, 2])
        s2n = sb("s2n", [128, QUAD])
        s13 = sb("s13", [128, QUAD, 3], BF16)
        s1r = sb("s1r", [128, QUAD])
        s1T = sb("s1T", [3, QUAD, 128], BF16)
        hb3 = sb("hb3", [128, QUAD, 128])
        h3x = sb("h3x", [128, QUAD, 129])
        mk = sb("mk", [128, QUAD])
        mk2 = sb("mk2", [128, QUAD])
        loan = w2raw[:, :, :].rearrange("p i k -> p (i k)")[:, 0:4 * QUAD * 128].rearrange("p (c g n) -> p c g n", c=4, g=QUAD)
        t3, att3 = loan[:, 0, :, :], loan[:, 1, :, :]
        p2T = [p2T_even, loan[:, 2:4, :, :]]
        den3 = sb("den3", [128, 2, 4])
        y3 = sb("y3", [128, QUAD, 128])
        res = sb("res", [128, QUAD, 128])

        names = """w_in c_in col_in pool_c prep_ps prep_a prep_d late_in late_ps late_d
            x0_in adj0_in x0T_ps adj0T_ps x0T_r adj0T_r h1_ps h1_r s_ps sa_r sb_r msg_ps msgb_r msg_r dist_ps ea_r hd_r sum_ps xs_r
            aT_r xn_ps xn_r c2_ps xcb_r xc_r ghn_ps r_ps r_r r1_r t_r z_ps z_r gin_ps u_r n_r d_r sT_r e_r y0_r
            y0T_ps adj1_in mb1_r x1_r x1T_ps x1T_r e1_ps e1_r ejs_r ej3_r ejT_ps ejT_r h1n_ps h1x_r z1_ps zi_r zl_r
            nm1_r p1_r p1T_ps p1T_r u1_ps rc1_r o1_r y1_r
            adj2_in mb2_r x2_r x2c_r x2d_r x2T_ps x2T_r q_ps qf_r k_ps kf_r v_ps v_r v2_r part0_r rest_r part1_r part2_r
            turn_w stack_in s2_ps nm2_r nms_r nm23_r nm2T_ps nm2T_r nmturn_w nm_in w2_ps p2_r u2_ps rc2_r o2_r
            o2T_ps o2T_r wo_ps y2_r
            x3_r x3T_ps x3T_r mk_r mks_r e3_ps e3_r s1s_r s13_r s1T_ps s1T_r h3_ps hb3_r h3x_r
            z3_ps t3_r d3_r att3_r u3_ps f3_r y3_r res_r out_w""".split()
        S = {n: sem(n) for n in names}
        st_r = [sem(f"stats{i}_r") for i in range(LAYERS)]
        mv_r = [sem(f"mv{i}_r") for i in range(LAYERS)]
        ve_r = [sem(f"ve{i}_r") for i in range(LAYERS)]
        rstd_r = [sem(f"rstd{i}_r") for i in range(LAYERS)]

        POOL_C = 18
        EARLY_C = 9
        COLUMNS_D = 13
        LATE_D = 5
        graphs = range(QUAD)
        mm = nc.tensor.matmul

        def quad_of(name, first):
            return ins[name][bass.ds(first, QUAD)].rearrange("g n d -> n g d")

        LAST = QUADS + DEPTH - 1
        FIRST, END = DEPTH, QUADS

        def run(engine, eng, pieces):
            def step(t):
                for name, behind, *more in ORDERS[engine]:
                    q = t - behind
                    if not isinstance(t, int) or 0 <= q < QUADS:
                        pieces[name](q, *more)

            for t in range(FIRST):
                step(t)
            with eng.Fori(FIRST, END) as t:
                step(t)
            for t in range(END, LAST):
                step(t)

        turn_qk = nc.dram_tensor("turn_qk", (2, 3, H2 * D2, QUAD * 128), BF16, kind="Internal").ap()
        turn_nm = nc.dram_tensor("turn_nm", (3, H2 * QUAD * 128), BF16, kind="Internal").ap()

        block = ctx.enter_context(nc.Block())

        @block.sync
        def _(sp):
            sp.dma_start(w2raw[:, :, :], ins["L0_gnn_conv2_w"]).then_inc(S["w_in"], 16)
            sp.dma_start(raw[:, 0, :], ins["L0_gnn_conv1_w"].rearrange("o i k -> o (i k)")).then_inc(S["w_in"], 16)
            sp.dma_start(raw[:, 1, :], ins["L0_gnn_w_msg"]).then_inc(S["w_in"], 16)
            sp.dma_start(raw[:, 2, :], ins["L3_gnn_W"]).then_inc(S["w_in"], 16)
            sp.dma_start(wihraw[:, :, :, :], ins["L0_gnn_w_ih"].rearrange("(c o) (b i) -> o c b i", c=3, b=2)).then_inc(S["w_in"], 16)
            sp.dma_start(whhraw[:, :, :], ins["L0_gnn_w_hh"].rearrange("(c o) i -> o c i", c=3)).then_inc(S["w_in"], 16)
            sp.dma_start(wseraw[:, :], ins["L0_gnn_w_se"]).then_inc(S["w_in"], 16)
            sp.dma_start(maskraw[:, :], ins["nodemask"]).then_inc(S["w_in"], 16)
            def ahead(*values):
                for value in values:
                    if not isinstance(value, int):
                        sp.compute_val(value)

            def l0_transposes(q):
                ahead(nth(q, 1, 0), q * QUAD)
                if later(q):
                    sp.wait_ge(S["x0T_ps"], nth(q, 1, 0))
                    sp.wait_ge(S["adj0T_ps"], nth(q, 1, 0))
                sp.dma_start(x0[:, :, :], quad_of("x", q * QUAD)).then_inc(S["x0_in"], 16)
                sp.dma_start(adj0[:, :, :], quad_of("adj", q * QUAD)).then_inc(S["adj0_in"], 16)

            def l1_transposes(q):
                ahead(nth(q, 1, 0), q * QUAD)
                if later(q):
                    sp.wait_ge(S["mb1_r"], nth(q, 1, 0))
                sp.dma_start(adj1[:, :, :], quad_of("adj", q * QUAD)).then_inc(S["adj1_in"], 16)

            def l2_fetch(q):
                ahead(nth(q, 2 * QUAD, 0), nth(q, 32, 32), nth(q, 1, 0), q * QUAD)
                if later(q):
                    sp.wait_ge(S["w2_ps"], nth(q, 2 * QUAD, 0))
                sp.wait_ge(S["turn_w"], nth(q, 32, 32))
                for i in range(SLOTS):
                    for tile, side, part in ((qst, 0, Q_PARTS[i]), (kst, 1, K_PARTS[i])):
                        sp.dma_start(tile[D2 * i:D2 * i + D2, :, :, :].rearrange("d h g n -> d h (g n)"),
                                     turn_qk[side, part].rearrange("(h d) x -> d h x", h=H2)).then_inc(S["stack_in"], 16)
                if later(q):
                    sp.wait_ge(S["mb2_r"], nth(q, 1, 0))
                sp.dma_start(adj2[:, :, :], quad_of("adj", q * QUAD)).then_inc(S["adj2_in"], 16)

            def l2_parts(q):
                ahead(nth(q, 32 * SLOTS, 0), nth(q, 2, 1), nth(q, 2, 2))
                if later(q):
                    sp.wait_ge(S["stack_in"], nth(q, 32 * SLOTS, 0))
                for side in range(2):
                    sp.wait_ge(S["part2_r"], nth(q, 2, side + 1))
                    sp.dma_start(turn_qk[side].rearrange("c p x -> p c x"),
                                 pieces3[:, side, :, :, :].rearrange("p c g n -> p c (g n)")).then_inc(S["turn_w"], 16)

            def l2_rows(q):
                ahead(nth(q, 16, 0), nth(q, 1, 1), nth(q, 16, 16), nth(q, 2 * QUAD, 0))
                if later(q):
                    sp.wait_ge(S["nm_in"], nth(q, 16, 0))
                sp.wait_ge(S["nm2T_r"], nth(q, 1, 1))
                sp.dma_start(turn_nm.rearrange("c (x n) -> (c x) n", n=128), nm2T[:, :]).then_inc(S["nmturn_w"], 16)
                sp.wait_ge(S["nmturn_w"], nth(q, 16, 16))
                if later(q):
                    sp.wait_ge(S["w2_ps"], nth(q, 2 * QUAD, 0))
                sp.dma_start(qst[STACK:STACK + 3, :, :, :].rearrange("c h g n -> c (h g n)"), turn_nm).then_inc(S["nm_in"], 16)

            def l3_close(q):
                ahead(nth(q, 1, 1), q * QUAD)
                sp.wait_ge(S["res_r"], nth(q, 1, 1))
                sp.dma_start(out[bass.ds(q * QUAD, QUAD)].rearrange("g n d -> n g d"), res[:, :, :]).then_inc(S["out_w"], 16)

            run("SP", sp, dict(l0_transposes=l0_transposes, l1_transposes=l1_transposes, l2_fetch=l2_fetch, l2_parts=l2_parts,
                         l2_rows=l2_rows, l3_close=l3_close))
            sp.wait_ge(S["out_w"], 16 * QUADS)

        @block.gpsimd
        def _(gp):
            g_ = nc.gpsimd
            n_c = [0]

            def const(ins_):
                n_c[0] += 1
                ins_.then_inc(S["pool_c"], 1)

            const(g_.memset(bse[:, :], 0.0))
            const(g_.memset(ident[:, :], 0.0))
            const(g_.memset(wseT[:, :], 0.0))
            const(g_.memset(h1[:, :, :, :], 0.0))
            const(g_.memset(sa[:, :, :], 0.0))
            const(g_.memset(sbm[:, :, :], 0.0))
            gp.wait_ge(S["pool_c"], n_c[0])
            const(g_.affine_select(out=ident[:, :], in_=ident[:, :], compare_op=ALU.not_equal, fill=1.0, base=0,
                                   pattern=[[-1, 128]], channel_multiplier=1))
            for tile, value in ((sa[64:67, :, :], 1.0), (sbm[32:35, :, :], -1.0)):
                gp.wait_ge(S["pool_c"], n_c[0])
                const(g_.memset(tile, value))
            assert n_c[0] == EARLY_C
            for dst, name in ((w1, "L1_gnn_W"), (wq, "L2_gnn_Wq"), (wk, "L2_gnn_Wk"), (wv, "L2_gnn_Wv"), (wo, "L2_gnn_Wo")):
                gp.dma_start(dst[:, :], ins[name]).then_inc(S["late_in"], 16)
            gp.dma_start(abc[:, :, :], ins["L1_gnn_a"].partition_broadcast(128)).then_inc(S["late_in"], 16)
            for i, name in enumerate(("L0_gnn_b_msg", "L2_gnn_bo", "L3_gnn_b")):
                gp.dma_start(bcast[:, i, :], ins[name].partition_broadcast(128)).then_inc(S["late_in"], 16)
            gp.wait_ge(S["pool_c"], n_c[0])
            const(g_.memset(sel1[:, :, :], 1.0))
            const(g_.memset(ones3[:, :], 1.0))
            const(g_.memset(half[:, :], -0.5))
            const(g_.memset(h1x[:, :, :, D1:D1 + 1], 1.0))
            const(g_.memset(v2x[:, :, :, D2:D2 + 1], 1.0))
            gp.wait_ge(S["pool_c"], n_c[0])
            const(g_.affine_select(out=sel1[:, :, :], in_=sel1[:, :, :], compare_op=ALU.is_ge, fill=0.0, base=0,
                                   pattern=[[-3, H1], [0, 128]], channel_multiplier=1))
            gp.wait_ge(S["pool_c"], n_c[0])
            const(g_.affine_select(out=sel1[:, :, :], in_=sel1[:, :, :], compare_op=ALU.is_ge, fill=0.0, base=2,
                                   pattern=[[3, H1], [0, 128]], channel_multiplier=-1))
            const(g_.tensor_copy(ident16[:, :], ident[:, :]))
            const(g_.memset(kst[:, :, :, :], 1.0))
            gp.wait_ge(S["pool_c"], n_c[0])
            assert n_c[0] == POOL_C
            gp.wait_ge(S["late_d"], LATE_D)

            def root(i, q):
                gp.wait_ge(ve_r[i], nth(q, 1, 1))
                g_.tensor_tensor(rstd[i][:, :], ve[i][:, :], half[:, :], ALU.pow).then_inc(rstd_r[i], 1)

            def l2_transposes(q):
                gp.wait_ge(S["x2_r"], nth(q, QUAD, QUAD))
                if later(q):
                    gp.wait_ge(S["x2d_r"], nth(q, 1, 0))
                g_.tensor_tensor(x2c[:, :, :], x2[:, :, :], cbc[:, :].unsqueeze(1).to_broadcast([128, QUAD, 128]),
                                 ALU.add).then_inc(S["x2c_r"], 1)

            def l2_parts(q):
                for side, ready in ((0, "qf_r"), (1, "kf_r")):
                    gp.wait_ge(S["part0_r"], nth(q, 2, side + 1))
                    g_.tensor_tensor(rest[:, side, :, :], qf[:, side, :, :], pieces3[:, side, 0, :, :], ALU.subtract).then_inc(S["rest_r"], 1)

            def l2_round(q):
                for side in range(2):
                    gp.wait_ge(S["part1_r"], nth(q, 2, side + 1))
                    g_.tensor_tensor(pieces3[:, side, 2, :, :], rest[:, side, :, :], pieces3[:, side, 1, :, :], ALU.subtract).then_inc(S["part2_r"], 1)

            def l0_messages(q):
                gp.wait_ge(S["h1_r"], nth(q, 1, 1))
                if later(q):
                    gp.wait_ge(S["c2_ps"], nth(q, 1, 0))
                g_.tensor_tensor(hd[:, 0, :, :], h1[:, 0, :, :], h1[:, 1, :, :], ALU.subtract).then_inc(S["hd_r"], 1)
                g_.tensor_tensor(hd[:, 1, :, 0:HALF + PAD - 1], h1[:, 0, :, 1:HALF + PAD], h1[:, 1, :, 0:HALF + PAD - 1],
                                 ALU.subtract).then_inc(S["hd_r"], 1)

            def l0_distances(q):
                gp.wait_ge(S["adj0T_r"], nth(q, 1, 1))
                gp.wait_ge(S["ea_r"], nth(q, 1, 1))
                g_.tensor_tensor(aT[:, :, :], ea[:, :, :], adjT[:, bass.ds(q * QUAD, QUAD), :], ALU.mult).then_inc(S["aT_r"], 1)

            def l3_values(q):
                gp.wait_ge(S["hb3_r"], nth(q, 1, 1))
                gp.wait_ge(S["mk_r"], nth(q, 1, 1))
                g_.tensor_tensor(h3x[:, :, 0:128], hb3[:, :, :], mk[:, :].unsqueeze(2).to_broadcast([128, QUAD, 128]),
                                 ALU.mult).then_inc(S["h3x_r"], 1)
                g_.tensor_copy(h3x[:, :, 128:129], mk[:, :].unsqueeze(2)).then_inc(S["h3x_r"], 1)

            run("Pool", gp, dict(l0_messages=l0_messages, l1_norm=lambda q: root(1, q), l2_norm=lambda q: root(2, q),
                         l0_close=lambda q: root(0, q), l2_transposes=l2_transposes, l2_parts=l2_parts, l2_round=l2_round,
                         l0_distances=l0_distances, l3_values=l3_values, l3_norm=lambda q: root(3, q)))

        @block.tensor
        def _(pe):
            def transpose(o, i, size=128):
                return nc.tensor.transpose(o, i, ident[0:size, 0:size])

            pe.wait_ge(S["pool_c"], EARLY_C)
            pe.wait_ge(S["w_in"], 16 * 8)
            for b in range(4):
                for k in range(4):
                    last = transpose(bank[b][:, k, :], w2raw[:, :, 4 * b + k])
                last.then_inc(S["prep_ps"], 1)
            transpose(bF[:, 0, :], w2raw[:, :, 16])
            for k in range(3):
                last = transpose(bF[:, k + 1, :], raw[:, k, :])
            last.then_inc(S["prep_ps"], 1)
            gates = [wihraw[:, c, b, :] for c in range(3) for b in range(2)] + [whhraw[:, c, :] for c in range(3)]
            for b in range(2):
                for k in range(4):
                    last = transpose(bank[5 + b][:, k, :], gates[4 * b + k])
                last.then_inc(S["prep_ps"], 1)
            transpose(bI[:, 0, :], gates[8])
            nc.tensor.transpose(bI[:, 1, 0:GRAPHS], maskraw[:, :], ident[0:GRAPHS, 0:GRAPHS])
            pe.wait_ge(S["col_in"], 16 * 19)
            nc.tensor.transpose(bI[:, 3, 0:VECTORS], rows[:, :], ident[0:VECTORS, 0:VECTORS])
            nc.tensor.transpose(bI[:, 2, 0:3], wseraw[:, :], ident[0:3, 0:3]).then_inc(S["prep_ps"], 1)
            pe.wait_ge(S["late_in"], 16 * 9)
            pe.wait_ge(S["prep_d"], 2)
            pe.wait_ge(S["late_d"], 2)
            mm(bD[:, 0, 0:2], raw[:, 2, :], a12, start=True, stop=True)
            mm(bD[:, 1, 0:2], spread[:, 1, :], a12, start=True, stop=True)
            mm(bD[:, 2, :], spread[:, 0, :], wo[:, :], start=True, stop=True).then_inc(S["late_ps"], 1)
            pe.wait_ge(S["prep_d"], 7)
            pe.wait_ge(S["prep_a"], 4)

            def transposes(dst, src):
                for g in graphs:
                    last = transpose(dst[:, g, :], src[:, g, :])
                return last

            def weights_first(dst, lhsT, rhs, start=True, stop=True):
                return mm(dst, lhsT, rhs, start=start, stop=stop)

            def l0_transposes(q):
                pe.wait_ge(S["x0_in"], nth(q, 16, 16))
                if later(q):
                    pe.wait_ge(S["u_r"], nth(q, 1, 0))
                transposes(bA, x0).then_inc(S["x0T_ps"], 1)
                pe.wait_ge(S["adj0_in"], nth(q, 16, 16))
                if later(q):
                    pe.wait_ge(S["t_r"], nth(q, 1, 0))
                transposes(bB, adj0).then_inc(S["adj0T_ps"], 1)

            def l0_project(q):
                pe.wait_ge(S["x0T_r"], nth(q, 1, 1))
                mm(bA[:, :, :], w2T[:, 17, :], x0T[:, :, :], start=True, stop=True).then_inc(S["h1_ps"], 1)
                pe.wait_ge(S["adj0T_r"], nth(q, 1, 1))
                mm(bB[0:35, :, :], wseT[:, :], x0T[:, :, :], start=True, stop=True).then_inc(S["s_ps"], 1)

            def l0_messages(q):
                pe.wait_ge(S["h1_r"], nth(q, 1, 1))
                for g in graphs:
                    last = mm(bA[:, g, :], x0T[:, g, :], w2T[:, 18, :], start=True, stop=True)
                last.then_inc(S["msg_ps"], 1)

            def l0_distances(q):
                pe.wait_ge(S["sa_r"], nth(q, 2, 2))
                pe.wait_ge(S["sb_r"], nth(q, 2, 2))
                for g in graphs:
                    last = mm(bB[:, g, :], sa[:, g, :], sbm[:, g, :], start=True, stop=True)
                last.then_inc(S["dist_ps"], 1)

            def l0_nmp(q):
                pe.wait_ge(S["msg_r"], nth(q, 1, 1))
                pe.wait_ge(S["aT_r"], nth(q, 1, 1))
                for g in graphs:
                    last = mm(bA[:, g, :], msg[:, g, :], aT[:, g, :], start=True, stop=True)
                last.then_inc(S["xn_ps"], 1)

            even, odd = (bC[:, :, :].rearrange("p g n -> p (g n)")[:, QUAD * HALF * i:QUAD * HALF * (i + 1)].rearrange("p (g n) -> p g n", g=QUAD)
                         for i in range(2))
            both = bB[:, :, :].rearrange("p g n -> p (g n)")[:, 0:QUAD * HALF].rearrange("p (g n) -> p g n", g=QUAD)

            def l0_sum(q, j):
                if j == 0:
                    pe.wait_ge(S["ea_r"], nth(q, 1, 1))
                weights = tap2T[:, j, :] if j < PAIRS else w2T[:, TAPS - 1, :]
                last = mm(both, weights, h1[:, 1, :, j:j + HALF], start=j == 0, stop=j == PAIRS)
                if j == PAIRS:
                    last.then_inc(S["sum_ps"], 1)

            def l0_conv(q, k):
                if k == 0:
                    pe.wait_ge(S["hd_r"], nth(q, 2, 2))
                    if later(q):
                        pe.wait_ge(S["x1_r"], nth(q, QUAD, 0))
                if k <= PAIRS:
                    last = mm(even, w2T[:, 2 * k, :], hd[:, 0, :, k:k + HALF], start=k == 0, stop=k == PAIRS)
                else:
                    j = k - PAIRS - 1
                    last = mm(odd, w2T[:, 2 * j + 1, :], hd[:, 1, :, j:j + HALF], start=j == 0, stop=j == PAIRS - 1)
                if k == TAPS - 1:
                    last.then_inc(S["c2_ps"], 1)

            def l0_gate_hn(q):
                pe.wait_ge(S["xs_r"], nth(q, 1, 1))
                mm(bB[:, :, :], gateT[:, 8, :], x0T[:, :, :], start=True, stop=True).then_inc(S["ghn_ps"], 1)

            def l0_gate(q, dst, c):
                mm(dst, gateT[:, 6 + c, :], x0T[:, :, :], start=True, stop=False)
                mm(dst, gateT[:, 2 * c + 1, :], xnT[:, :, :], start=False, stop=False)
                return mm(dst, gateT[:, 2 * c, :], xcT[:, :, :], start=False, stop=True)

            def l0_gate_r(q):
                pe.wait_ge(S["xn_r"], nth(q, 1, 1))
                pe.wait_ge(S["xc_r"], nth(q, 1, 1))
                l0_gate(q, bA[:, :, :], 0).then_inc(S["r_ps"], 1)

            def l0_gate_z(q):
                l0_gate(q, bC[:, :, :], 1).then_inc(S["z_ps"], 1)

            def l0_gate_n(q):
                pe.wait_ge(S["r_r"], nth(q, 1, 1))
                mm(bA[:, :, :], gateT[:, 5, :], xnT[:, :, :], start=True, stop=False)
                mm(bA[:, :, :], gateT[:, 4, :], xcT[:, :, :], start=False, stop=True).then_inc(S["gin_ps"], 1)

            def l0_close(q):
                pe.wait_ge(S["y0_r"], nth(q, 1, 1))
                transposes(bC, yT).then_inc(S["y0T_ps"], 1)

            def l1_transposes(q):
                pe.wait_ge(S["x1_r"], nth(q, QUAD, QUAD))
                if later(q):
                    pe.wait_ge(S["o1_r"], nth(q, QUAD, 0))
                transposes(bD, x1).then_inc(S["x1T_ps"], 1)

            def l1_scores(q):
                pe.wait_ge(S["x1T_r"], nth(q, 1, 1))
                for g in graphs:
                    last = mm(bD[:, 0, 8 * g:8 * g + 8], x1T[:, g, :], wa[:, :], start=True, stop=True)
                last.then_inc(S["e1_ps"], 1)

            def l1_values(q):
                pe.wait_ge(S["e1_r"], nth(q, 1, 1))
                for g in graphs:
                    last = mm(bD[:, g, :], x1T[:, g, :], w1[:, :], start=True, stop=True)
                last.then_inc(S["h1n_ps"], 1)

            ejT_ps = bD[:, :, :].rearrange("p g n -> p (g n)").bitcast(BF16)

            def l1_rows(q):
                pe.wait_ge(S["h1x_r"], nth(q, 1, 1))
                pe.wait_ge(S["ej3_r"], nth(q, 1, 1))
                for g in graphs:
                    last = nc.tensor.transpose(ejT_ps[0:3 * H1, 128 * g:128 * g + 128],
                                               ej3[:, g, :, :].rearrange("p h c -> p (h c)"), ident16[:, :])
                last.then_inc(S["ejT_ps"], 1)

            def l1_logits(q, g):
                pe.wait_ge(S["mb1_r"], nth(q, 1, 1))
                if g == 0:
                    pe.wait_ge(S["ejT_r"], nth(q, 1, 1))
                else:
                    pe.wait_ge(S["o1_r"], nth(q, QUAD, g))
                mm(bD[:, :, :], ident16[:, :], mb1[:, g:g + 1, :].to_broadcast([128, H1, 128]), start=True, stop=False)
                for h in range(H1):
                    last = mm(bD[:, h, :], sel1[:, h, :], ejT[:, g, :], start=False, stop=h == H1 - 1)
                last.then_inc(S["z1_ps"], 1)

            def l1_turn(q, g):
                pe.wait_ge(S["p1_r"], nth(q, QUAD, g + 1))
                for h in range(H1):
                    last = transpose(bD[:, h, :], p1[:, h, :])
                last.then_inc(S["p1T_ps"], 1)

            def l1_output(q, g):
                pe.wait_ge(S["p1T_r"], nth(q, QUAD, g + 1))
                for h in range(H1):
                    last = mm(bD[:, h, 0:D1 + 1], p1T[:, h, :], h1x[:, g, h, :], start=True, stop=True)
                last.then_inc(S["u1_ps"], 1)

            def l2_transposes(q):
                pe.wait_ge(S["x2_r"], nth(q, QUAD, QUAD))
                if not isinstance(q, int) or q >= 2:
                    pe.wait_ge(S["y2_r"], nth(q - 1, 1, 0))
                transposes(bH, x2).then_inc(S["x2T_ps"], 1)

            def l2_project(q):
                pe.wait_ge(S["x2T_r"], nth(q, 1, 1))
                if not isinstance(q, int) or q >= 2:
                    pe.wait_ge(S["p2_r"], nth(q - 1, 2 * QUAD, 0))
                mm(bF[:, :, :], wq[:, :], x2T[:, :, :], start=True, stop=True).then_inc(S["q_ps"], 1)
                mm(bG[:, :, :], wk[:, :], x2T[:, :, :], start=True, stop=True).then_inc(S["k_ps"], 1)
                for g in graphs:
                    last = mm(bH[:, g, :], x2T[:, g, :], wv[:, :], start=True, stop=True)
                last.then_inc(S["v_ps"], 1)

            pair = (bF, bG)

            def l2_maximum(q, job):
                g, i = divmod(job, 2)
                if job == 0:
                    pe.wait_ge(S["stack_in"], nth(q, 32 * SLOTS, 32 * SLOTS))
                    pe.wait_ge(S["mb2_r"], nth(q, 1, 1))
                if job < 2:
                    if not isinstance(q, int) or q + 1 < QUADS:
                        pe.wait_ge(S["qf_r" if job == 0 else "kf_r"], nth(q, 1, 2))
                    elif later(q):
                        pe.wait_ge(S["p2_r"], nth(q, 2 * QUAD, 0))
                else:
                    pe.wait_ge(S["nm2_r"], nth(q, 2 * QUAD, job - 1))
                dst = pair[i]
                mm(dst[:, :, :], ident16[:, :], mb2[:, g:g + 1, :].to_broadcast([128, 4, 128]), start=True, stop=False)
                for h in range(4):
                    last = mm(dst[:, h, :], qst[0:STACK, 4 * i + h, g, :], kst[0:STACK, 4 * i + h, g, :], start=False, stop=h == 3)
                last.then_inc(S["s2_ps"], 1)

            def l2_rows(q):
                pe.wait_ge(S["nm23_r"], nth(q, 1, 1))
                if not isinstance(q, int) or q + 1 < QUADS:
                    pe.wait_ge(S["v_r"], nth(q, 1, 2))
                elif later(q):
                    pe.wait_ge(S["y2_r"], nth(q, 1, 0))
                nc.tensor.transpose(bH[:, :, :].rearrange("p g n -> p (g n)").bitcast(BF16)[0:3 * H2 * QUAD, 0:128],
                                    nm23[:, :, :, :].rearrange("p c h g -> p (c h g)"), ident16[:, :]).then_inc(S["nm2T_ps"], 1)

            def l2_weights(q, g, i):
                if g == 0 and i == 0:
                    pe.wait_ge(S["nm_in"], nth(q, 16, 16))
                    pe.wait_ge(S["nm2_r"], nth(q, 2 * QUAD, 2 * QUAD))
                if g:
                    pe.wait_ge(S["p2_r"], nth(q, 2 * QUAD, 2 * g + i - 1))
                dst = pair[i]
                mm(dst[:, :, :], mb2[:, g, :], ident16[:, :].unsqueeze(1).to_broadcast([128, 4, 128]), start=True, stop=False)
                for h in range(4):
                    last = mm(dst[:, h, :], kst[:, 4 * i + h, g, :], qst[:, 4 * i + h, g, :], start=False, stop=h == 3)
                last.then_inc(S["w2_ps"], 1)

            uv = bH[:, :, :].rearrange("p g n -> p (g n)")[:, 0:H2 * (D2 + 1)].rearrange("p (h e) -> p h e", h=H2)

            def l2_output(q, g):
                pe.wait_ge(S["v2_r"], nth(q, 1, 1))
                if g == 0:
                    pe.wait_ge(S["nm2T_r"], nth(q, 1, 1))
                else:
                    pe.wait_ge(S["o2T_r"], nth(q, QUAD, g))
                pe.wait_ge(S["p2_r"], nth(q, 2 * QUAD, 2 * g + 2))
                for h in range(H2):
                    last = mm(uv[:, h, :], p2T[g % 2][:, h // 4, h % 4, :], v2x[:, g, h, :], start=True, stop=True)
                last.then_inc(S["u2_ps"], 1)

            def l2_output_turn(q, g):
                pe.wait_ge(S["o2_r"], nth(q, QUAD, g + 1))
                transpose(bH[:, g, :], o2[:, :, :].rearrange("p h e -> p (h e)")).then_inc(S["o2T_ps"], 1)

            def l2_close(q):
                pe.wait_ge(S["o2T_r"], nth(q, QUAD, QUAD))
                for g in graphs:
                    last = mm(bH[:, g, :], o2T[:, g, :], wo[:, :], start=True, stop=True)
                last.then_inc(S["wo_ps"], 1)

            def l3_transposes(q):
                pe.wait_ge(S["x3_r"], nth(q, QUAD, QUAD))
                if later(q):
                    pe.wait_ge(S["y3_r"], nth(q, QUAD, 0))
                transposes(bI, x3).then_inc(S["x3T_ps"], 1)

            def l3_scores(q):
                pe.wait_ge(S["x3T_r"], nth(q, 1, 1))
                for g in graphs:
                    last = mm(bI[:, 0, 2 * g:2 * g + 2], x3T[:, g, :], w3a[:, :], start=True, stop=True)
                last.then_inc(S["e3_ps"], 1)

            def l3_values(q):
                pe.wait_ge(S["e3_r"], nth(q, 1, 1))
                for g in graphs:
                    last = mm(bI[:, g, :], x3T[:, g, :], w2T[:, 19, :], start=True, stop=True)
                last.then_inc(S["h3_ps"], 1)

            s1T_ps = bI[:, :, :].rearrange("p g n -> p (g n)").bitcast(BF16)

            def l3_rows(q):
                pe.wait_ge(S["hb3_r"], nth(q, 1, 1))
                pe.wait_ge(S["s13_r"], nth(q, 1, 1))
                for g in graphs:
                    last = nc.tensor.transpose(s1T_ps[0:3, 128 * g:128 * g + 128], s13[:, g, :], ident16[:, :])
                last.then_inc(S["s1T_ps"], 1)

            def l3_logits(q):
                pe.wait_ge(S["s1T_r"], nth(q, 1, 1))
                mm(bI[:, :, :], ones3[:, :], s1T[:, :, :], start=True, stop=True).then_inc(S["z3_ps"], 1)

            u3 = bI[:, :, :].rearrange("p g n -> p (g n)")[:, 0:2 * 129].rearrange("p (g e) -> p g e", g=2)

            def l3_output(q, pair):
                pe.wait_ge(S["att3_r"], nth(q, 2, pair + 1))
                if pair == 0:
                    pe.wait_ge(S["h3x_r"], nth(q, 2, 2))
                else:
                    pe.wait_ge(S["y3_r"], nth(q, QUAD, 2))
                for g in range(2):
                    last = mm(u3[:, g, :], att3[:, 2 * pair + g, :], h3x[:, 2 * pair + g, :], start=True, stop=True)
                last.then_inc(S["u3_ps"], 1)

            run("PE", pe, dict(l0_transposes=l0_transposes, l0_project=l0_project, l0_messages=l0_messages,
                         l0_distances=l0_distances, l0_nmp=l0_nmp, l0_conv=l0_conv, l0_sum=l0_sum, l0_gate_hn=l0_gate_hn, l0_gate_r=l0_gate_r,
                         l0_gate_z=l0_gate_z, l0_gate_n=l0_gate_n, l0_close=l0_close, l1_transposes=l1_transposes,
                         l1_scores=l1_scores, l1_values=l1_values, l1_rows=l1_rows, l1_logits=l1_logits, l1_turn=l1_turn,
                         l1_output=l1_output, l2_transposes=l2_transposes, l2_project=l2_project, l2_maximum=l2_maximum,
                         l2_rows=l2_rows, l2_weights=l2_weights, l2_output=l2_output, l2_output_turn=l2_output_turn,
                         l2_close=l2_close, l3_transposes=l3_transposes, l3_scores=l3_scores, l3_values=l3_values,
                         l3_rows=l3_rows, l3_logits=l3_logits, l3_output=l3_output))

        @block.scalar
        def _(act):
            a_ = nc.scalar.activation
            for at, name, parts in ((BN1G, "L0_gnn_bn1_g", 1), (BN1B, "L0_gnn_bn1_b", 1), (BN1M, "L0_gnn_bn1_m", 1),
                                    (BN1V, "L0_gnn_bn1_v", 1), (BN2G, "L0_gnn_bn2_g", 1), (BN2B, "L0_gnn_bn2_b", 1),
                                    (BN2M, "L0_gnn_bn2_m", 1), (BN2V, "L0_gnn_bn2_v", 1), (BIH, "L0_gnn_b_ih", 3),
                                    (BHH, "L0_gnn_b_hh", 3), (BQ, "L2_gnn_bq", 1), (BK, "L2_gnn_bk", 1), (BV, "L2_gnn_bv", 1),
                                    (B3, "L3_gnn_b", 1), (A1, "L3_gnn_a1", 1), (A2, "L3_gnn_a2", 1)):
                act.dma_start(rows[at:at + parts, :], ins[name].rearrange("(c p) -> c p", c=parts)).then_inc(S["col_in"], 16)
            act.wait_ge(S["pool_c"], 1)
            act.dma_start(attb[:, :], ins["L3_gnn_att_b"].partition_broadcast(128)).then_inc(S["col_in"], 16)
            for at in (0, 32):
                act.dma_start(bse[at:at + 3, :], ins["L0_gnn_b_se"].rearrange("(p c) -> p c", c=1)).then_inc(S["col_in"], 16)
            for b, dst in ((0, w2T[:, 0:4, :]), (2, w2T[:, 8:12, :]), (4, w2T[:, 16:20, :]), (6, gateT[:, 4:8, :])):
                act.wait_ge(S["prep_ps"], b + 1)
                a_(dst, bank[b][:, :, :], ACT.Copy).then_inc(S["prep_a"], 1)
            act.wait_ge(S["late_d"], 1)
            for at in (SC1, SC2):
                a_(sc[:, at:at + 1], sc[:, at + 1:at + 2], ACT.Sqrt).then_inc(S["prep_a"], 1)
            act.wait_ge(S["prep_d"], COLUMNS_D)

            def l0_x(q):
                act.wait_ge(S["x0T_ps"], nth(q, 1, 1))
                if later(q):
                    act.wait_ge(S["d_r"], nth(q, 1, 0))
                    act.wait_ge(S["sT_r"], nth(q, 1, 0))
                a_(x0T[:, :, :], bA[:, :, :], ACT.Copy).then_inc(S["x0T_r"], 1)

            def l0_h1(q):
                act.wait_ge(S["h1_ps"], nth(q, 1, 1))
                a_(h1[:, :, :, PAD // 2:PAD // 2 + HALF].rearrange("p s g i -> p g i s"),
                   bA[:, :, :].rearrange("p g (i s) -> p g i s", s=2), ACT.Relu, bias=sc[:, SH1:SH1 + 1], scale=sc[:, SC1:SC1 + 1]).then_inc(S["h1_r"], 1)

            def l0_s(q):
                act.wait_ge(S["s_ps"], nth(q, 1, 1))
                if later(q):
                    act.wait_ge(S["sb_r"], nth(q, 2, 0))
                a_(sa[0:3, :, :], bB[0:3, :, :], ACT.Identity, bias=bse[0:3, :]).then_inc(S["sa_r"], 1)
                a_(sa[32:35, :, :], bB[32:35, :, :], ACT.Square, bias=bse[32:35, :]).then_inc(S["sa_r"], 1)

            def l0_exp(q):
                act.wait_ge(S["dist_ps"], nth(q, 1, 1))
                if later(q):
                    act.wait_ge(S["aT_r"], nth(q, 1, 0))
                a_(ea[:, :, :], bB[:, :, :], ACT.Exp).then_inc(S["ea_r"], 1)

            def l0_xn(q):
                act.wait_ge(S["xn_ps"], nth(q, 1, 1))
                a_(xnT[:, :, :], bA[:, :, :], ACT.Copy).then_inc(S["xn_r"], 1)

            def l0_xc(q):
                act.wait_ge(S["xcb_r"], nth(q, 1, 1))
                a_(xcT[:, :, :], xcb[:, :, :], ACT.Relu, bias=sc[:, SH2:SH2 + 1]).then_inc(S["xc_r"], 1)

            def l0_r(q):
                act.wait_ge(S["r_ps"], nth(q, 1, 1))
                if later(q):
                    act.wait_ge(S["r1_r"], nth(q, 1, 0))
                a_(rT[:, :, :], bA[:, :, :], ACT.Tanh, bias=sc[:, HBR:HBR + 1], scale=0.5).then_inc(S["r_r"], 1)

            def l0_z(q):
                act.wait_ge(S["z_ps"], nth(q, 1, 1))
                if later(q):
                    act.wait_ge(S["e_r"], nth(q, 1, 0))
                a_(zT[:, :, :], bC[:, :, :], ACT.Tanh, bias=sc[:, HBZ:HBZ + 1], scale=0.5).then_inc(S["z_r"], 1)

            def l0_n(q):
                act.wait_ge(S["u_r"], nth(q, 1, 1))
                a_(nT[:, :, :], uT[:, :, :], ACT.Tanh, bias=col[:, BIH + 2:BIH + 3]).then_inc(S["n_r"], 1)

            def l1_x(q):
                act.wait_ge(S["x1T_ps"], nth(q, 1, 1))
                a_(x1T[:, :, :], bD[:, :, :], ACT.Copy).then_inc(S["x1T_r"], 1)

            def l1_h(q):
                act.wait_ge(S["h1n_ps"], nth(q, 1, 1))
                a_(h1x[:, :, :, 0:D1], bD[:, :, :].rearrange("p g (h e) -> p g h e", h=H1), ACT.Copy).then_inc(S["h1x_r"], 1)

            def l1_rows(q):
                act.wait_ge(S["ejT_ps"], nth(q, 1, 1))
                a_(ejT[:, :, :], bD[:, :, :].rearrange("p g n -> p (g n)").bitcast(BF16)[0:3 * H1, 0:512].rearrange("p (g n) -> p g n", g=QUAD),
                   ACT.Copy).then_inc(S["ejT_r"], 1)

            def l1_exp(q, g):
                act.wait_ge(S["nm1_r"], nth(q, QUAD, g + 1))
                if g or later(q):
                    act.wait_ge(S["p1T_ps"], nth(q, QUAD, g))
                for h in range(H1):
                    last = a_(p1[:, h, :], zl[:, h, :], ACT.Exp, bias=nm1[:, h:h + 1])
                last.then_inc(S["p1_r"], 1)

            def l1_turned(q, g):
                act.wait_ge(S["p1T_ps"], nth(q, QUAD, g + 1))
                if g or later(q):
                    act.wait_ge(S["u1_ps"], nth(q, QUAD, g))
                a_(p1T[:, :, :], bD[:, :, :], ACT.Copy).then_inc(S["p1T_r"], 1)

            def l2_x(q):
                act.wait_ge(S["x2T_ps"], nth(q, 1, 1))
                a_(x2T[:, :, :], bH[:, :, :], ACT.Copy).then_inc(S["x2T_r"], 1)

            def l2_k(q):
                act.wait_ge(S["k_ps"], nth(q, 1, 1))
                if later(q):
                    act.wait_ge(S["part2_r"], nth(q, 2, 0))
                    act.wait_ge(S["turn_w"], nth(q, 32, 0))
                a_(qf[:, 1, :, :], bG[:, :, :], ACT.Identity, bias=col[:, BK:BK + 1]).then_inc(S["kf_r"], 1)

            def l2_v(q):
                act.wait_ge(S["v_ps"], nth(q, 1, 1))
                if later(q):
                    act.wait_ge(S["v2_r"], nth(q, 1, 0))
                a_(v2n[:, :, :], bH[:, :, :], ACT.Copy).then_inc(S["v_r"], 1)

            def l2_fetch(q):
                act.wait_ge(S["x2c_r"], nth(q, 1, 1))
                if later(q):
                    act.wait_ge(S["y2_r"], nth(q, 1, 0))
                a_(x2d[:, :, :], x2c[:, :, :], ACT.Copy).then_inc(S["x2d_r"], 1)
                act.wait_ge(S["v_r"], nth(q, 1, 1))
                if later(q):
                    act.wait_ge(S["u2_ps"], nth(q, QUAD, 0))
                a_(v2x[:, :, :, 0:D2], v2n[:, :, :].rearrange("p g (h e) -> p g h e", h=H2), ACT.Copy).then_inc(S["v2_r"], 1)

            def l2_parts(q):
                for side, ready in ((0, "qf_r"), (1, "kf_r")):
                    act.wait_ge(S[ready], nth(q, 1, 1))
                    a_(pieces3[:, side, 0, :, :], qf[:, side, :, :], ACT.Copy).then_inc(S["part0_r"], 1)

            def l2_round(q):
                for side in range(2):
                    act.wait_ge(S["rest_r"], nth(q, 2, side + 1))
                    a_(pieces3[:, side, 1, :, :], rest[:, side, :, :], ACT.Copy).then_inc(S["part1_r"], 1)

            def l2_rows(q):
                act.wait_ge(S["nm2T_ps"], nth(q, 1, 1))
                if later(q):
                    act.wait_ge(S["nmturn_w"], nth(q, 16, 0))
                a_(nm2T[:, :], bH[:, :, :].rearrange("p g n -> p (g n)").bitcast(BF16)[0:3 * H2 * QUAD, 0:128], ACT.Copy).then_inc(S["nm2T_r"], 1)

            def l2_weights(q, g, i):
                act.wait_ge(S["w2_ps"], nth(q, 2 * QUAD, 2 * g + i + 1))
                if g > 1 or later(q):
                    act.wait_ge(S["u2_ps"], nth(q, QUAD, g - 1))
                a_(p2T[g % 2][:, i, :, :], (bF, bG)[i][:, :, :], ACT.Exp).then_inc(S["p2_r"], 1)

            def l2_output_turned(q, g):
                act.wait_ge(S["o2T_ps"], nth(q, QUAD, g + 1))
                a_(o2T[:, g, :], bH[:, g, :], ACT.Copy).then_inc(S["o2T_r"], 1)

            def l3_x(q):
                act.wait_ge(S["x3T_ps"], nth(q, 1, 1))
                a_(x3T[:, :, :], bI[:, :, :], ACT.Copy).then_inc(S["x3T_r"], 1)

            def l3_rows(q):
                act.wait_ge(S["s1T_ps"], nth(q, 1, 1))
                a_(s1T[:, :, :], bI[:, :, :].rearrange("p g n -> p (g n)").bitcast(BF16)[0:3, 0:512].rearrange("p (g n) -> p g n", g=QUAD),
                   ACT.Copy).then_inc(S["s1T_r"], 1)

            def l3_exp(q):
                act.wait_ge(S["z3_ps"], nth(q, 1, 1))
                act.wait_ge(S["e3_r"], nth(q, 1, 1))
                if later(q):
                    act.wait_ge(S["att3_r"], nth(q, 2, 0))
                for g in graphs:
                    last = a_(t3[:, g, :], bI[:, g, :], ACT.Exp, bias=s2n[:, g:g + 1], scale=-1.0)
                last.then_inc(S["t3_r"], 1)

            run("Activation", act, dict(l0_transposes=l0_x, l0_project=l0_h1, l0_s=l0_s, l0_distances=l0_exp, l0_nmp=l0_xn, l0_xc=l0_xc, l0_gate_r=l0_r,
                          l0_gate_z=l0_z, l0_update=l0_n, l1_transposes=l1_x, l1_values=l1_h, l1_rows=l1_rows,
                          l1_exp=l1_exp, l1_turn=l1_turned, l2_transposes=l2_x, l2_project=l2_k, l2_v=l2_v, l2_fetch=l2_fetch,
                          l2_parts=l2_parts, l2_round=l2_round, l2_rows=l2_rows, l2_weights=l2_weights, l2_output_turn=l2_output_turned,
                          l3_transposes=l3_x, l3_rows=l3_rows, l3_logits=l3_exp))

        @block.vector
        def _(dve):
            v = nc.vector
            for b, dst in ((1, w2T[:, 4:8, :]), (3, w2T[:, 12:16, :]), (5, gateT[:, 0:4, :])):
                dve.wait_ge(S["prep_ps"], b + 1)
                v.tensor_copy(dst, bank[b][:, :, :]).then_inc(S["prep_d"], 1)
            dve.wait_ge(S["prep_ps"], 8)
            v.tensor_copy(gateT[:, 8, :], bI[:, 0, :]).then_inc(S["prep_d"], 1)
            v.tensor_copy(nodeT[:, :], bI[:, 1, 0:GRAPHS]).then_inc(S["prep_d"], 1)
            dve.wait_ge(S["pool_c"], EARLY_C)
            for at in (0, 32):
                last = v.tensor_copy(wseT[:, at:at + 3], bI[:, 2, 0:3])
            last.then_inc(S["prep_d"], 1)
            v.tensor_copy(col[:, :], bI[:, 3, 0:VECTORS]).then_inc(S["prep_d"], 1)
            dve.wait_ge(S["prep_d"], 7)
            for at, src in ((SH1, BN1V), (SH2, BN2V)):
                last = v.tensor_scalar(sc[:, at:at + 1], col[:, src:src + 1], EPS, None, ALU.add)
            last.then_inc(S["late_d"], 1)
            v.tensor_copy(spread[:, 0, :], col[:, BV:BV + 1].to_broadcast([128, 128]))
            v.tensor_copy(spread[:, 1, :], col[:, B3:B3 + 1].to_broadcast([128, 128])).then_inc(S["late_d"], 1)
            dve.wait_ge(S["prep_a"], 6)
            n = [7]

            def chain(ins_):
                n[0] += 1
                ins_.then_inc(S["prep_d"], 1)
                dve.wait_ge(S["prep_d"], n[0])

            norms = sc[:, 0:4].rearrange("p (n c) -> p n c", n=2)
            given = col[:, BN1G:BN2V + 1].rearrange("p (n c) -> p n c", n=2)
            scale, shift, tmp = norms[:, :, 0], norms[:, :, 1], sc[:, TMP:TMP + 2]
            chain(v.reciprocal(tmp, scale))
            chain(v.tensor_tensor(scale, tmp, given[:, :, 0], ALU.mult))
            chain(v.tensor_tensor(tmp, scale, given[:, :, 2], ALU.mult))
            chain(v.tensor_tensor(shift, given[:, :, 1], tmp, ALU.subtract))
            chain(v.tensor_tensor(tmp, col[:, BIH:BIH + 2], col[:, BHH:BHH + 2], ALU.add))
            chain(v.tensor_scalar(sc[:, HBR:HBR + 2], tmp, 0.5, None, ALU.mult))
            assert n[0] == COLUMNS_D
            v.tensor_tensor(tap2T[:, :, :], w2T[:, 0:2 * PAIRS:2, :], w2T[:, 1:2 * PAIRS:2, :], ALU.add)
            dve.wait_ge(S["late_in"], 16 * 9)
            w1h = w1[:, :].rearrange("p (h e) -> p h e", h=H1)
            for i in range(2):
                chain(v.tensor_tensor(aprod[:, H1 * i:H1 * i + H1, :], w1h, abc[:, :, D1 * i:D1 * i + D1], ALU.mult))
            chain(v.tensor_reduce(wa[:, :], aprod[:, :, :], AX.X, ALU.add))
            dve.wait_ge(S["late_ps"], 1)
            v.tensor_copy(w3a[:, :], bD[:, 0, 0:2]).then_inc(S["late_d"], 1)
            chain(v.tensor_copy(sc[:, 8:10], bD[:, 1, 0:2]))
            chain(v.tensor_tensor(sc[:, 10:11], sc[:, 8:9], sc[:, 9:10], ALU.add))
            chain(v.tensor_tensor(sc[:, 11:12], sc[:, 10:11], attb[:, :], ALU.add))
            v.tensor_scalar(nc3[:, :], sc[:, 11:12], -1.0, None, ALU.mult).then_inc(S["late_d"], 1)
            v.tensor_tensor(cbc[:, :], bD[:, 2, :], bcast[:, 1, :], ALU.add).then_inc(S["late_d"], 1)
            dve.wait_ge(S["late_d"], LATE_D)

            def norm_stats(i, q, src):
                if later(q):
                    dve.wait_ge(rstd_r[i], nth(q, 1, 0))
                for g in graphs:
                    last = v.bn_stats(stats[i][:, g, :], src[:, g, :])
                last.then_inc(st_r[i], 1)
                dve.wait_ge(st_r[i], nth(q, 1, 1))
                mean_e, m2_e, mean_o, m2_o = (stats[i][:, :, c] for c in (1, 2, 4, 5))
                v.tensor_tensor(mom[i][:, 0, :], mean_e, mean_o, ALU.add)
                v.tensor_tensor(mom[i][:, 1, :], mean_e, mean_o, ALU.subtract)
                v.tensor_tensor(mom[i][:, 2, :], m2_e, m2_o, ALU.add).then_inc(mv_r[i], 1)
                dve.wait_ge(mv_r[i], nth(q, 2, 1))
                v.tensor_scalar(mv[i][:, 0, :], mom[i][:, 0, :], 0.5, None, ALU.mult)
                v.tensor_tensor(mv[i][:, 1, :], mom[i][:, 1, :], mom[i][:, 1, :], ALU.mult)
                v.tensor_scalar(mv[i][:, 2, :], mom[i][:, 2, :], 1.0 / D, EPS, ALU.mult, ALU.add).then_inc(mv_r[i], 1)
                dve.wait_ge(mv_r[i], nth(q, 2, 2))
                v.scalar_tensor_tensor(ve[i][:, :], mv[i][:, 1, :], 0.25, mv[i][:, 2, :], ALU.mult, ALU.add).then_inc(ve_r[i], 1)

            def norm_apply(i, q, dst, src, done):
                dve.wait_ge(rstd_r[i], nth(q, 1, 1))
                for g in graphs:
                    last = v.tensor_scalar(dst[:, g, :], src[:, g, :], mv[i][:, 0, g:g + 1], rstd[i][:, g:g + 1], ALU.subtract, ALU.mult)
                    if done != S["res_r"]:
                        last.then_inc(done, 1)
                if done == S["res_r"]:
                    last.then_inc(done, 1)

            def split3(dst, src, rest, first, last_sem, q):
                v.tensor_copy(dst[0], src).then_inc(first, 1)
                dve.wait_ge(first, nth(q, 3, 1))
                v.tensor_tensor(rest, src, dst[0], ALU.subtract).then_inc(first, 1)
                dve.wait_ge(first, nth(q, 3, 2))
                v.tensor_copy(dst[1], rest).then_inc(first, 1)
                dve.wait_ge(first, nth(q, 3, 3))
                v.tensor_tensor(dst[2], rest, dst[1], ALU.subtract).then_inc(last_sem, 1)

            def l0_adj(q):
                dve.wait_ge(S["adj0T_ps"], nth(q, 1, 1))
                v.tensor_copy(adjT[:, bass.ds(q * QUAD, QUAD), :], bB[:, :, :]).then_inc(S["adj0T_r"], 1)

            def l0_s(q):
                dve.wait_ge(S["sa_r"], nth(q, 2, 2))
                v.tensor_scalar(sbm[0:3, :, :], sa[0:3, :, :], 2.0, None, ALU.mult).then_inc(S["sb_r"], 1)
                v.tensor_scalar(sbm[64:67, :, :], sa[32:35, :, :], -1.0, None, ALU.mult).then_inc(S["sb_r"], 1)

            def l0_msg(q):
                dve.wait_ge(S["msg_ps"], nth(q, 1, 1))
                v.tensor_tensor(msgb[:, :, :], bA[:, :, :], bcast[:, 0:1, :].to_broadcast([128, QUAD, 128]), ALU.add).then_inc(S["msgb_r"], 1)
                dve.wait_ge(S["msgb_r"], nth(q, 1, 1))
                v.tensor_scalar(msg[:, :, :], msgb[:, :, :], 0.0, None, ALU.max).then_inc(S["msg_r"], 1)

            xcb2 = xcb[:, :, :].rearrange("p g (i s) -> p g i s", s=2)

            def l0_mix(q):
                dve.wait_ge(S["sum_ps"], nth(q, 1, 1))
                both = bB[:, :, :].rearrange("p g n -> p (g n)")[:, 0:QUAD * HALF].rearrange("p (g n) -> p g n", g=QUAD)
                v.scalar_tensor_tensor(xcb2, both.unsqueeze(3).to_broadcast([128, QUAD, HALF, 2]), sc[:, SC2:SC2 + 1],
                                       x0T[:, :, :].rearrange("p g (i s) -> p g i s", s=2), ALU.mult, ALU.add).then_inc(S["xs_r"], 1)

            def l0_xc(q):
                dve.wait_ge(S["xs_r"], nth(q, 1, 1))
                dve.wait_ge(S["c2_ps"], nth(q, 1, 1))
                v.scalar_tensor_tensor(xcb2, bC[:, :, :].rearrange("p g n -> p (g n)").rearrange("p (s g i) -> p g i s", s=2, g=QUAD),
                                       sc[:, SC2:SC2 + 1], xcb2, ALU.mult, ALU.add).then_inc(S["xcb_r"], 1)

            def l0_r1(q):
                dve.wait_ge(S["r_r"], nth(q, 1, 1))
                v.tensor_scalar(r1T[:, :, :], rT[:, :, :], 1.0, None, ALU.add).then_inc(S["r1_r"], 1)
                dve.wait_ge(S["r1_r"], nth(q, 1, 1))
                dve.wait_ge(S["ghn_ps"], nth(q, 1, 1))
                v.scalar_tensor_tensor(tT[:, :, :], bB[:, :, :], col[:, BHH + 2:BHH + 3], r1T[:, :, :], ALU.add, ALU.mult).then_inc(S["t_r"], 1)

            def l0_u(q):
                dve.wait_ge(S["t_r"], nth(q, 1, 1))
                dve.wait_ge(S["gin_ps"], nth(q, 1, 1))
                v.scalar_tensor_tensor(uT[:, :, :], tT[:, :, :], 0.5, bA[:, :, :], ALU.mult, ALU.add).then_inc(S["u_r"], 1)

            def l0_y(q):
                dve.wait_ge(S["n_r"], nth(q, 1, 1))
                v.tensor_tensor(dT[:, :, :], x0T[:, :, :], nT[:, :, :], ALU.subtract).then_inc(S["d_r"], 1)
                v.tensor_tensor(sT[:, :, :], x0T[:, :, :], nT[:, :, :], ALU.add).then_inc(S["sT_r"], 1)
                dve.wait_ge(S["d_r"], nth(q, 1, 1))
                dve.wait_ge(S["z_r"], nth(q, 1, 1))
                v.scalar_tensor_tensor(eT[:, :, :], zT[:, :, :], 1.0, dT[:, :, :], ALU.add, ALU.mult).then_inc(S["e_r"], 1)
                dve.wait_ge(S["e_r"], nth(q, 1, 1))
                v.scalar_tensor_tensor(yT[:, :, :], eT[:, :, :], 0.5, sT[:, :, :], ALU.mult, ALU.add).then_inc(S["y0_r"], 1)

            def bias_of(dst, src, loaded, used, done, q):
                dve.wait_ge(S[loaded], nth(q, 16, 16))
                if later(q):
                    dve.wait_ge(S[used[0]], nth(q, used[1], 0))
                v.tensor_scalar(dst[:, :, :], src[:, :, :], 0.0, NEG, ALU.is_le, ALU.mult).then_inc(S[done], 1)

            def l1_scores(q):
                dve.wait_ge(S["e1_ps"], nth(q, 1, 1))
                v.tensor_copy(e1[:, :, :], bD[:, 0, 0:8 * QUAD].rearrange("p (g c) -> p g c", g=QUAD)).then_inc(S["e1_r"], 1)
                dve.wait_ge(S["e1_r"], nth(q, 1, 1))
                split3([ej3[:, :, :, i] for i in range(3)], e1[:, :, H1:2 * H1], ejr[:, :, :], S["ejs_r"], S["ej3_r"], q)

            def l1_logits(q, g):
                dve.wait_ge(S["z1_ps"], nth(q, QUAD, g + 1))
                v.tensor_tensor(zi[:, :, :], bD[:, :, :], e1[:, g, 0:H1].unsqueeze(2).to_broadcast([128, H1, 128]), ALU.add).then_inc(S["zi_r"], 1)
                dve.wait_ge(S["zi_r"], nth(q, QUAD, g + 1))
                if g or later(q):
                    dve.wait_ge(S["p1_r"], nth(q, QUAD, g))
                v.scalar_tensor_tensor(zl[:, :, :], zi[:, :, :], SLOPE, zi[:, :, :], ALU.mult, ALU.max).then_inc(S["zl_r"], 1)
                dve.wait_ge(S["zl_r"], nth(q, QUAD, g + 1))
                v.tensor_reduce(nm1[:, :], zl[:, :, :], AX.X, ALU.max, negate=True).then_inc(S["nm1_r"], 1)

            def l1_output(q, g):
                dve.wait_ge(S["u1_ps"], nth(q, QUAD, g + 1))
                v.reciprocal(rc1[:, :], bD[:, :, D1]).then_inc(S["rc1_r"], 1)
                dve.wait_ge(S["rc1_r"], nth(q, QUAD, g + 1))
                v.tensor_tensor(o1[:, :, :], bD[:, :, 0:D1], rc1[:, :].unsqueeze(2).to_broadcast([128, H1, D1]), ALU.mult).then_inc(S["o1_r"], 1)
                dve.wait_ge(S["o1_r"], nth(q, QUAD, g + 1))
                v.tensor_tensor(y1[:, g, :], o1[:, :, :].rearrange("p h e -> p (h e)"), x1[:, g, :], ALU.add).then_inc(S["y1_r"], 1)

            def l2_q(q):
                dve.wait_ge(S["q_ps"], nth(q, 1, 1))
                if later(q):
                    dve.wait_ge(S["part2_r"], nth(q, 2, 0))
                v.tensor_scalar(qf[:, 0, :, :], bF[:, :, :], col[:, BQ:BQ + 1], float(D2) ** -0.5, ALU.add, ALU.mult).then_inc(S["qf_r"], 1)

            def l2_maximum(q, job):
                g, i = divmod(job, 2)
                dve.wait_ge(S["s2_ps"], nth(q, 2 * QUAD, job + 1))
                v.tensor_reduce(nm2[:, 4 * i:4 * i + 4, g], (bF, bG)[i][:, :, :], AX.X, ALU.max, negate=True).then_inc(S["nm2_r"], 1)

            def l2_rows(q):
                dve.wait_ge(S["nm2_r"], nth(q, 2 * QUAD, 2 * QUAD))
                split3([nm23[:, i, :, :] for i in range(3)], nm2[:, :, :], nm2r[:, :, :], S["nms_r"], S["nm23_r"], q)

            uv = bH[:, :, :].rearrange("p g n -> p (g n)")[:, 0:H2 * (D2 + 1)].rearrange("p (h e) -> p h e", h=H2)

            def l2_output(q, g):
                dve.wait_ge(S["u2_ps"], nth(q, QUAD, g + 1))
                v.reciprocal(rc2[:, :], uv[:, :, D2]).then_inc(S["rc2_r"], 1)
                dve.wait_ge(S["rc2_r"], nth(q, QUAD, g + 1))
                v.tensor_tensor(o2[:, :, :], uv[:, :, 0:D2], rc2[:, :].unsqueeze(2).to_broadcast([128, H2, D2]), ALU.mult).then_inc(S["o2_r"], 1)

            def l2_close(q):
                dve.wait_ge(S["wo_ps"], nth(q, 1, 1))
                dve.wait_ge(S["x2d_r"], nth(q, 1, 1))
                v.tensor_tensor(y2[:, :, :], bH[:, :, :], x2d[:, :, :], ALU.add).then_inc(S["y2_r"], 1)

            def l3_masks(q):
                if later(q):
                    dve.wait_ge(S["h3x_r"], nth(q, 2, 0))
                v.tensor_copy(mk[:, :], nodeT[:, bass.ds(q * QUAD, QUAD)]).then_inc(S["mk_r"], 1)
                dve.wait_ge(S["mk_r"], nth(q, 1, 1))
                v.tensor_tensor(mk2[:, :], mk[:, :], mk[:, :], ALU.mult).then_inc(S["mks_r"], 1)

            def l3_scores(q):
                dve.wait_ge(S["e3_ps"], nth(q, 1, 1))
                if later(q):
                    dve.wait_ge(S["t3_r"], nth(q, 1, 0))
                e = bI[:, 0, 0:2 * QUAD].rearrange("p (g c) -> p g c", g=QUAD)
                v.tensor_scalar(s2n[:, :], e[:, :, 1], -1.0, nc3[:, :], ALU.mult, ALU.add)
                v.tensor_copy(e3[:, :, :], e).then_inc(S["e3_r"], 1)
                dve.wait_ge(S["e3_r"], nth(q, 1, 1))
                split3([s13[:, :, i] for i in range(3)], e3[:, :, 0], s1r[:, :], S["s1s_r"], S["s13_r"], q)

            def l3_values(q):
                dve.wait_ge(S["h3_ps"], nth(q, 1, 1))
                if later(q):
                    dve.wait_ge(S["h3x_r"], nth(q, 2, 0))
                v.tensor_tensor(hb3[:, :, :], bI[:, :, :], bcast[:, 2:3, :].to_broadcast([128, QUAD, 128]), ALU.add).then_inc(S["hb3_r"], 1)

            def l3_att(q, pair):
                at = slice(2 * pair, 2 * pair + 2)
                dve.wait_ge(S["t3_r"], nth(q, 1, 1))
                v.tensor_scalar(t3[:, at, :], t3[:, at, :], 1.0, BIG, ALU.add, ALU.min).then_inc(S["d3_r"], 1)
                dve.wait_ge(S["d3_r"], nth(q, 4, 2 * pair + 1))
                v.reciprocal(t3[:, at, :], t3[:, at, :]).then_inc(S["d3_r"], 1)
                dve.wait_ge(S["d3_r"], nth(q, 4, 2 * pair + 2))
                v.tensor_tensor(att3[:, at, :], t3[:, at, :], adjT[:, bass.ds(q * QUAD + 2 * pair, 2), :], ALU.mult).then_inc(S["att3_r"], 1)

            u3 = bI[:, :, :].rearrange("p g n -> p (g n)")[:, 0:2 * 129].rearrange("p (g e) -> p g e", g=2)

            def l3_output(q, pair):
                at = slice(2 * pair, 2 * pair + 2)
                k = 4 * pair
                dve.wait_ge(S["u3_ps"], nth(q, 2, pair + 1))
                v.tensor_tensor(den3[:, :, 0], u3[:, :, 128], mk[:, at], ALU.mult).then_inc(S["f3_r"], 1)
                dve.wait_ge(S["f3_r"], nth(q, 8, k + 1))
                v.tensor_scalar(den3[:, :, 1], den3[:, :, 0], TINY, None, ALU.add).then_inc(S["f3_r"], 1)
                dve.wait_ge(S["f3_r"], nth(q, 8, k + 2))
                v.reciprocal(den3[:, :, 2], den3[:, :, 1]).then_inc(S["f3_r"], 1)
                dve.wait_ge(S["f3_r"], nth(q, 8, k + 3))
                v.tensor_tensor(den3[:, :, 3], den3[:, :, 2], mk2[:, at], ALU.mult).then_inc(S["f3_r"], 1)
                dve.wait_ge(S["f3_r"], nth(q, 8, k + 4))
                for g in range(2):
                    v.scalar_tensor_tensor(y3[:, 2 * pair + g, :], u3[:, g, 0:128], den3[:, g, 3:4], x3[:, 2 * pair + g, :],
                                           ALU.mult, ALU.add).then_inc(S["y3_r"], 1)

            def l3_norm(q):
                dve.wait_ge(S["y3_r"], nth(q, QUAD, QUAD))
                norm_stats(3, q, y3)

            def l3_close(q):
                if later(q):
                    dve.wait_ge(S["out_w"], nth(q, 16, 0))
                norm_apply(3, q, res, y3, S["res_r"])

            def l1_norm(q):
                dve.wait_ge(S["y1_r"], nth(q, QUAD, QUAD))
                norm_stats(1, q, y1)

            def l0_close(q):
                dve.wait_ge(S["y0T_ps"], nth(q, 1, 1))
                norm_stats(0, q, bC)

            def l2_norm(q):
                dve.wait_ge(S["y2_r"], nth(q, 1, 1))
                norm_stats(2, q, y2)

            run("DVE", dve, dict(
                l0_transposes=l0_adj, l1_norm=l1_norm, l2_output=l2_output, l0_project=l0_s, l2_close=l2_close, l2_norm=l2_norm,
                l2_fetch=lambda q: bias_of(mb2, adj2, "adj2_in", ("w2_ps", 2 * QUAD), "mb2_r", q),
                l0_messages=l0_msg, l0_close=l0_close,
                l2_transposes=lambda q: norm_apply(1, q, x2, y1, S["x2_r"]),
                l2_project=l2_q, l3_transposes=lambda q: (norm_apply(2, q, x3, y2, S["x3_r"]), l3_masks(q)),
                l0_mix=l0_mix, l0_apply=lambda q: norm_apply(0, q, x1, bC, S["x1_r"]),
                l1_transposes=lambda q: bias_of(mb1, adj1, "adj1_in", ("z1_ps", QUAD), "mb1_r", q),
                l3_scores=l3_scores, l2_maximum=l2_maximum, l1_scores=l1_scores, l3_values=l3_values,
                l1_logits=l1_logits, l1_output=l1_output, l2_rows=l2_rows, l3_weights=l3_att, l3_output=l3_output,
                l3_norm=l3_norm, l3_close=l3_close, l0_gate_r=l0_xc, l0_gate_z=l0_r1, l0_u=l0_u, l0_update=l0_y))


def kernel(**inputs):
    import numpy as np
    import concourse.bacc as bacc
    from concourse.bass_utils import run_bass_kernel_spmd

    nc = bacc.Bacc("TRN2", target_bir_lowering=False, num_devices=1)
    arrays, ins = {}, {}
    for name in INS:
        a = np.ascontiguousarray(inputs[name])
        if a.ndim == 0:
            a = a.reshape(1)
        arrays["in_" + name] = a
        ins[name] = nc.dram_tensor("in_" + name, a.shape, mybir.dt.from_np(a.dtype), kind="ExternalInput").ap()
    out = nc.dram_tensor("out_0", (GRAPHS, N, D), F32, kind="ExternalOutput").ap()
    build(nc, ins, out)
    r = run_bass_kernel_spmd(nc, [arrays], core_ids=[0])
    return r.results[0]["out_0"]
```
